# Optimizing a Trainium2 kernel written in Bass

```python
import numpy as np
import jax
import jax.numpy as jnp

def _softmax(x, axis=-1):
    return jax.nn.softmax(x, axis=axis)

def _gelu(x):
    return jax.nn.gelu(x, approximate=True)

def _silu(x):
    return jax.nn.silu(x)

def _sigmoid(x):
    return jax.nn.sigmoid(x)

def _layernorm(x, axis=-1, eps=1e-05):
    m = jnp.mean(x, axis=axis, keepdims=True)
    v = jnp.var(x, axis=axis, keepdims=True)
    return (x - m) / jnp.sqrt(v + eps)

def _scatter_add(tgt, idx, src, axis=0):
    return tgt.at[idx].add(src)

def _segment_sum(src, seg, n):
    return jax.ops.segment_sum(src, seg, n)
kernel_name = 'mk_decoder_preln_d1_seqx_r2_ff607e'

def setup_inputs(seed: int=0):
    np.random.seed(seed)
    _w = jnp.asarray

    def _rec_inputs():
        import jax
        import jax.numpy as jnp
        _rk = jax.random.key(seed)
        x = -0.0002928 + 1 * jax.random.normal(jax.random.fold_in(_rk, 1), (16, 256, 512), jnp.float32)
        _lenS = 256 - jax.random.randint(jax.random.fold_in(_rk, 7), (16,), 0, max(1, 256 // 4) + 1, jnp.int32)
        _lenS2 = 256 - jax.random.randint(jax.random.fold_in(_rk, 8), (16,), 0, max(1, 256 // 4) + 1, jnp.int32)
        _ctx_1024P = jax.random.normal(jax.random.fold_in(_rk, 11), (16, 16, 512), jnp.float32)
        _ctx_1024c = jax.random.dirichlet(jax.random.fold_in(_rk, 511), 0.3 * jnp.ones((16,), jnp.float32), (16, 256))
        _ctx_1024t = jnp.einsum('bsk,bkd->bsd', _ctx_1024c, _ctx_1024P)
        _ctx_1024t = _ctx_1024t * jax.lax.rsqrt(jnp.mean(jnp.square(_ctx_1024t)) + 1e-12) * 0.953939
        ctx_1024 = -1.39393e-06 + 0.999914 * (_ctx_1024t + 0.3 * jax.random.normal(jax.random.fold_in(_rk, 611), (16, 256, 512), jnp.float32))
        return (x, ctx_1024)
    x, ctx_1024 = _rec_inputs()

    def _L0_attn_setup():
        import jax, jax.numpy as jnp
        import numpy as np
        D_MODEL = 512
        D_STATE = 16
        D_CONV = 4
        EXPAND = 2
        D_INNER = EXPAND * D_MODEL
        DT_MIN, DT_MAX = (0.001, 0.1)
        BATCH, SEQ = (4, 1024)

        def _silu(v):
            return v * jax.nn.sigmoid(v)
        key = jax.random.key(seed)
        ks = jax.random.split(key, 5)
        x = jax.random.normal(ks[0], (BATCH, SEQ, D_MODEL), jnp.float32)
        W_in = jax.random.normal(ks[1], (2 * D_INNER, D_MODEL), jnp.float32) / np.sqrt(D_MODEL)
        conv_w = jax.random.normal(ks[2], (D_INNER, D_CONV), jnp.float32) / np.sqrt(D_CONV)
        conv_b = jnp.zeros((D_INNER,), jnp.float32)
        W_xproj = jax.random.normal(ks[3], (2 * D_STATE + 1, D_INNER), jnp.float32) / np.sqrt(D_INNER)
        A_log = jnp.log(jnp.arange(1, D_STATE + 1, dtype=jnp.float32))
        D_param = jnp.ones((D_INNER,), jnp.float32)
        W_out = jax.random.normal(ks[4], (D_MODEL, D_INNER), jnp.float32) / np.sqrt(D_INNER)
        return dict(x=x, W_in=W_in, conv_w=conv_w, conv_b=conv_b, W_xproj=W_xproj, A_log=A_log, D_param=D_param, W_out=W_out)
    _L0_attn_all = _L0_attn_setup()
    _L0_attn_in = {k: v for k, v in _L0_attn_all.items() if k in ('W_in', 'conv_w', 'conv_b', 'W_xproj', 'A_log', 'D_param', 'W_out')}
    del _L0_attn_all

    def _L0_xattn_setup():
        import jax, jax.numpy as jnp
        import numpy as np
        B, S, H, NH = (2, 1024, 512, 16)
        DK = H // NH
        key = jax.random.key(seed)
        ks = jax.random.split(key, 11)
        sc = 1.0 / np.sqrt(H)
        return {'q': jax.random.normal(ks[0], (B, S, H), jnp.float32), 'v': jax.random.normal(ks[1], (B, S, H), jnp.float32), 'k': jax.random.normal(ks[2], (B, S, H), jnp.float32), 'Wq': jax.random.normal(ks[3], (H, H), jnp.float32) * sc, 'bq': jax.random.normal(ks[4], (H,), jnp.float32) * 0.01, 'Wk': jax.random.normal(ks[5], (H, H), jnp.float32) * sc, 'bk': jax.random.normal(ks[6], (H,), jnp.float32) * 0.01, 'Wv': jax.random.normal(ks[7], (H, H), jnp.float32) * sc, 'bv': jax.random.normal(ks[8], (H,), jnp.float32) * 0.01, 'Wo': jax.random.normal(ks[9], (H, H), jnp.float32) * sc, 'bo': jax.random.normal(ks[10], (H,), jnp.float32) * 0.01}
    _L0_xattn_all = _L0_xattn_setup()
    _L0_xattn_in = {k: v for k, v in _L0_xattn_all.items() if k in ('Wq', 'bq', 'Wk', 'bk', 'Wv', 'bv', 'Wo', 'bo')}
    del _L0_xattn_all

    def _L0_ffn_setup():
        import jax, jax.numpy as jnp
        import numpy as np
        import math
        E = 8
        K = 2
        CF = 1.2
        D = 512
        H = 2048
        key = jax.random.key(seed)
        k0, k1, k2, k3 = jax.random.split(key, 4)
        B, T = (8, 1024)
        x_btd = jax.random.normal(k0, (B, T, D), jnp.float32)
        Wr = jax.random.normal(k1, (D, E), jnp.float32) / np.sqrt(D)
        br = jnp.zeros((E,), jnp.float32)
        W1 = jax.random.normal(k2, (E, D, H), jnp.float32) / np.sqrt(D)
        b1 = jnp.zeros((E, H), jnp.float32)
        W2 = jax.random.normal(k3, (E, H, D), jnp.float32) / np.sqrt(H)
        b2 = jnp.zeros((E, D), jnp.float32)
        return dict(x_btd=x_btd, Wr=Wr, br=br, W1=W1, b1=b1, W2=W2, b2=b2)
    _L0_ffn_all = _L0_ffn_setup()
    _L0_ffn_in = {k: v for k, v in _L0_ffn_all.items() if k in ('Wr', 'br', 'W1', 'b1', 'W2', 'b2')}
    del _L0_ffn_all
    return {'x': x, 'ctx_1024': ctx_1024, 'L0_attn_W_in': _L0_attn_in['W_in'], 'L0_attn_conv_w': _L0_attn_in['conv_w'], 'L0_attn_conv_b': _L0_attn_in['conv_b'], 'L0_attn_W_xproj': _L0_attn_in['W_xproj'], 'L0_attn_A_log': _L0_attn_in['A_log'], 'L0_attn_D_param': _L0_attn_in['D_param'], 'L0_attn_W_out': _L0_attn_in['W_out'], 'L0_xattn_Wq': _L0_xattn_in['Wq'], 'L0_xattn_bq': _L0_xattn_in['bq'], 'L0_xattn_Wk': _L0_xattn_in['Wk'], 'L0_xattn_bk': _L0_xattn_in['bk'], 'L0_xattn_Wv': _L0_xattn_in['Wv'], 'L0_xattn_bv': _L0_xattn_in['bv'], 'L0_xattn_Wo': _L0_xattn_in['Wo'], 'L0_xattn_bo': _L0_xattn_in['bo'], 'L0_ffn_Wr': _L0_ffn_in['Wr'], 'L0_ffn_br': _L0_ffn_in['br'], 'L0_ffn_W1': _L0_ffn_in['W1'], 'L0_ffn_b1': _L0_ffn_in['b1'], 'L0_ffn_W2': _L0_ffn_in['W2'], 'L0_ffn_b2': _L0_ffn_in['b2']}

def reference(x, ctx_1024, L0_attn_W_in, L0_attn_conv_w, L0_attn_conv_b, L0_attn_W_xproj, L0_attn_A_log, L0_attn_D_param, L0_attn_W_out, L0_xattn_Wq, L0_xattn_bq, L0_xattn_Wk, L0_xattn_bk, L0_xattn_Wv, L0_xattn_bv, L0_xattn_Wo, L0_xattn_bo, L0_ffn_Wr, L0_ffn_br, L0_ffn_W1, L0_ffn_b1, L0_ffn_W2, L0_ffn_b2):
    import jax
    import jax.numpy as jnp

    def _L0_attn_ref(x, W_in, conv_w, conv_b, W_xproj, A_log, D_param, W_out):
        import jax, jax.numpy as jnp
        import numpy as np
        D_MODEL = 512
        D_STATE = 16
        D_CONV = 4
        EXPAND = 2
        D_INNER = EXPAND * D_MODEL
        DT_MIN, DT_MAX = (0.001, 0.1)
        BATCH, SEQ = (4, 1024)

        def _silu(v):
            return v * jax.nn.sigmoid(v)
        b, l, d = x.shape
        xz = x @ W_in.T
        x_proj, z = jnp.split(xz, 2, axis=-1)
        xp = jnp.pad(x_proj, ((0, 0), (D_CONV - 1, 0), (0, 0)))
        x_conv = conv_b + sum((xp[:, k:k + l, :] * conv_w[:, k] for k in range(D_CONV)))
        x_conv = _silu(x_conv)
        x_dbl = x_conv @ W_xproj.T
        Bmat = x_dbl[..., :D_STATE]
        Cmat = x_dbl[..., D_STATE:2 * D_STATE]
        dt = jnp.clip(jax.nn.softplus(x_dbl[..., -1]), DT_MIN, DT_MAX)
        A = -jnp.exp(A_log)

        def step(h, inp):
            x_t, dt_t, B_t, C_t = inp
            dt_A = jnp.clip(dt_t[:, None] * A, -20.0, 0.0)
            A_bar = jnp.exp(dt_A)[:, None, :]
            B_bar = jnp.clip(dt_t[:, None] * B_t, -10.0, 10.0)[:, None, :]
            h = jnp.clip(A_bar * h + B_bar * x_t[:, :, None], -100.0, 100.0)
            y_t = jnp.einsum('bds,bs->bd', h, C_t)
            return (h, y_t)
        h0 = jnp.zeros((b, D_INNER, D_STATE), x.dtype)
        xs = (jnp.swapaxes(x_conv, 0, 1), jnp.swapaxes(dt, 0, 1), jnp.swapaxes(Bmat, 0, 1), jnp.swapaxes(Cmat, 0, 1))
        _, ys = jax.lax.scan(step, h0, xs)
        y = jnp.swapaxes(ys, 0, 1)
        y = y * _silu(z) + x_conv * D_param
        return y @ W_out.T

    def _L0_xattn_ref(q, v, k, Wq, bq, Wk, bk, Wv, bv, Wo, bo):
        import jax, jax.numpy as jnp
        import numpy as np
        B, S, H, NH = (2, 1024, 512, 16)
        DK = H // NH
        b, s, h = q.shape
        qh = (q @ Wq.T + bq).reshape(b, s, NH, DK).transpose(0, 2, 1, 3)
        kh = (k @ Wk.T + bk).reshape(b, s, NH, DK).transpose(0, 2, 1, 3)
        vh = (v @ Wv.T + bv).reshape(b, s, NH, DK).transpose(0, 2, 1, 3)
        scores = jnp.einsum('bhqd,bhkd->bhqk', qh, kh) / jnp.sqrt(jnp.asarray(DK, qh.dtype))
        probs = jax.nn.softmax(scores, axis=-1)
        ctx = jnp.einsum('bhqk,bhkd->bhqd', probs, vh)
        concat = ctx.transpose(0, 2, 1, 3).reshape(b, s, h)
        return concat @ Wo.T + bo

    def _L0_ffn_ref(x_btd, Wr, br, W1, b1, W2, b2):
        import jax, jax.numpy as jnp
        import numpy as np
        import math
        E = 8
        K = 2
        CF = 1.2
        D = 512
        H = 2048
        B, T, Dm = x_btd.shape
        N = B * T
        x = x_btd.reshape(N, Dm)
        cap = int(math.ceil(CF * N / E))
        probs = jax.nn.softmax(x @ Wr + br, axis=-1)
        gates, ids = jax.lax.top_k(probs, K)
        flat_ids = ids.reshape(-1)
        flat_g = gates.reshape(-1)
        M = N * K
        order = jnp.lexsort((-flat_g, flat_ids))
        s_ids = flat_ids[order]
        s_tok = (order // K).astype(jnp.int32)
        s_g = flat_g[order]
        counts = jnp.bincount(flat_ids, length=E)
        starts = jnp.concatenate([jnp.zeros((1,), counts.dtype), jnp.cumsum(counts)[:-1]])
        rank = jnp.arange(M) - starts[s_ids]
        valid = rank < cap
        pos = jnp.where(valid, s_ids * cap + rank, E * cap)
        disp_tok = jnp.zeros((E * cap + 1,), jnp.int32).at[pos].set(s_tok)[:E * cap]
        disp_g = jnp.zeros((E * cap + 1,), x.dtype).at[pos].set(s_g)[:E * cap]
        xg = x[disp_tok].reshape(E, cap, Dm)
        h = jax.nn.silu(jnp.einsum('ecd,edh->ech', xg, W1) + b1[:, None, :])
        out = jnp.einsum('ech,ehd->ecd', h, W2) + b2[:, None, :]
        gated = out * disp_g.reshape(E, cap, 1)
        y = jnp.zeros((N, Dm), x.dtype).at[disp_tok].add(gated.reshape(E * cap, Dm))
        return y.reshape(B, T, Dm)
    x = x + _L0_attn_ref(_layernorm(x, axis=-1), L0_attn_W_in, L0_attn_conv_w, L0_attn_conv_b, L0_attn_W_xproj, L0_attn_A_log, L0_attn_D_param, L0_attn_W_out)
    x = x + _L0_xattn_ref(_layernorm(x, axis=-1), ctx_1024, ctx_1024, L0_xattn_Wq, L0_xattn_bq, L0_xattn_Wk, L0_xattn_bk, L0_xattn_Wv, L0_xattn_bv, L0_xattn_Wo, L0_xattn_bo)
    x = x + _L0_ffn_ref(_layernorm(x, axis=-1), L0_ffn_Wr, L0_ffn_br, L0_ffn_W1, L0_ffn_b1, L0_ffn_W2, L0_ffn_b2)
    return x

_drawn_inputs = setup_inputs


def setup_inputs(seed=0):
    import zlib

    import numpy as np

    out = dict(_drawn_inputs(seed))
    spreads = {'L0_attn_conv_b': (0.0, 0.1),
     'L0_attn_D_param': (1.0, 0.2),
     'L0_ffn_br': (0.0, 0.1),
     'L0_ffn_b1': (0.0, 0.442),
     'L0_ffn_b2': (0.0, 0.271)}
    factors = {'L0_xattn_bq': 22.613, 'L0_xattn_bk': 64.0, 'L0_xattn_bv': 5.97, 'L0_xattn_bo': 5.719}
    for name, (base, spread) in spreads.items():
        noise = np.random.default_rng([zlib.crc32(name.encode()), seed]).standard_normal(out[name].shape)
        drawn = base * np.exp(spread * noise) if base else spread * noise
        out[name] = jnp.asarray(drawn.astype(out[name].dtype))
    for name, factor in factors.items():
        out[name] = (out[name] * factor).astype(out[name].dtype)
    return out
```

```python
from contextlib import ExitStack

import concourse.bass as bass
from concourse import mybir

F32 = mybir.dt.float32
F32R = mybir.dt.float32r
I32 = mybir.dt.int32
ALU = mybir.AluOpType
ACT = mybir.ActivationFunctionType
AX = mybir.AxisListType
RMAX = bass.bass_isa.ReduceOp.max

P = 128
D = 512
KD = D // P
EPS = 1e-5


def wait(eng, sem, value):
    if isinstance(value, int) and value <= 0:
        return
    eng.wait_ge(sem, value)


class Chain:

    def __init__(self, eng, sem, per, b):
        self.eng, self.sem, self.per, self.b, self.n = eng, sem, per, b, 0

    def did(self, instruction):
        instruction.then_inc(self.sem, 1)
        self.n += 1

    def wait(self):
        self.eng.wait_ge(self.sem, self.b * self.per + self.n)


def f32(ap):
    return ap.bitcast(F32)


def mamba_phase(nc, x, W_inT, conv_w, conv_b, W_xprojT, A_log, D_param, W_outT, x1, rows_dram):
    B, S, _ = x.shape
    E = conv_w.shape[0]
    KE = E // P
    N = 16
    TT = S // P
    BL = 32
    NB = S // BL
    HB = P // BL
    NI = NB + NB - HB
    CL = 8
    with ExitStack() as ctx:
        def sb(name, shape, dt=F32):
            return ctx.enter_context(nc.sbuf_tensor("a_" + name, shape, dt))

        def sem(name):
            return ctx.enter_context(nc.semaphore("a_" + name))

        win_h, win_l = sb("win_h", [P, KD, 2 * E], F32R), sb("win_l", [P, KD, 2 * E], F32R)
        wout_h, wout_l = sb("wout_h", [P, KE, D], F32R), sb("wout_l", [P, KE, D], F32R)
        wx_h, wx_l = sb("wx_h", [P, KE, P], F32R), sb("wx_l", [P, KE, P], F32R)
        wx_raw = sb("wx_raw", [P, KE, 33])
        cw, cb, dp = sb("cw", [P, KE, 4]), sb("cb", [P, KE]), sb("dp", [P, KE])
        a_neg, a_log = sb("a_neg", [N, 1]), sb("a_log", [N, 1])
        ident, mask, half = sb("ident", [P, P]), sb("mask", [P, S + P]), sb("half", [P, TT])
        ones_row = sb("ones_row", [N, S])
        xl = sb("xl", [P, TT, D])
        xres = sb("xres", [P, TT, D])
        xn = sb("xn", [P, TT, D])
        st, mv, ve, rs = sb("st", [P, TT, 6]), sb("mv", [P, TT, 2]), sb("ve", [P, TT]), sb("rs", [P, TT])
        xnT_h, xnT_l = sb("xnT_h", [P, KD, S], F32R), sb("xnT_l", [P, KD, S], F32R)
        v = sb("v", [P, 2, S])
        xc = [sb(f"xc{i}", [P, KE, S]) for i in range(2)]
        xcr_h, xcr_l = sb("xcr_h", [P, 2, S], F32R), sb("xcr_l", [P, 2, S], F32R)
        zs = sb("zs", [P, KE, S])
        XT_h, XT_l = sb("XT_h", [P, TT, E], F32R), sb("XT_l", [P, TT, E], F32R)
        MTf, MT_h, MT_l = sb("MTf", [P, S + P]), sb("MT_h", [P, S + P], F32R), sb("MT_l", [P, S + P], F32R)
        t1, y2 = sb("t1", [P, 2, S]), sb("y2", [P, 2, S])
        y2_h, y2_l = sb("y2_h", [P, 2, S], F32R), sb("y2_l", [P, 2, S], F32R)
        dt_r, l_r, Bb, Cr, ab, gb = (sb(n, [N, S]) for n in ("dt_r", "l_r", "Bb", "Cr", "ab", "gb"))
        abar = sb("abar", [N, S])
        lam = sb("lam", [N, S + 1])
        EB, EC = sb("EB", [N, NI, P]), sb("EC", [N, S])
        rng, scl = sb("rng", [N, NB]), sb("scl", [N, 2])
        fl, flr, fls = sb("fl", [P, 3]), sb("flr", [P, 3]), sb("fls", [P, 2])
        flg = [sb(f"flg{i}", [P, 1], I32) for i in range(2)]
        hst, hcb, abc, xch = sb("hst", [P, N]), sb("hcb", [P, CL, N]), sb("abc", [P, 3, N, CL]), sb("xch", [P, CL])
        bxs = sb("bxs", [P, N])

        psT = [ctx.enter_context(nc.psum_tensor(f"a_psT{i}", [P, 512], F32)) for i in range(2)]
        psP = [ctx.enter_context(nc.psum_tensor(f"a_psP{i}", [P, 512], F32)) for i in range(3)]
        psX = ctx.enter_context(nc.psum_tensor("a_psX", [P, 512], F32))
        psO = [ctx.enter_context(nc.psum_tensor(f"a_psO{i}", [P, 512], F32)) for i in range(2)]

        w_ld = sem("w_ld")
        stg = [sem(f"stg{i}") for i in range(2)]
        stg_h, stg_l = sem("stg_h"), sem("stg_l")
        setup_pool, setup_dve, setup_act = sem("setup_pool"), sem("setup_dve"), sem("setup_act")
        x_ld = sem("x_ld")
        xres_ld, x1_st = sem("xres_ld"), sem("x1_st")
        ln, rstd = sem("ln"), sem("rstd")
        xn_tp, xnT_hi, xnT_lo = sem("xn_tp"), sem("xnT_hi"), sem("xnT_lo")
        x_mm, z_mm, y_mm, o_mm, xd_mm = sem("x_mm"), sem("z_mm"), sem("y_mm"), sem("o_mm"), sem("xd_mm")
        v_rdy, conv, xc_rdy, xc_hi, xc_lo = sem("v_rdy"), sem("conv"), sem("xc_rdy"), sem("xc_hi"), sem("xc_lo")
        z_rdy = sem("z_rdy")
        xt_tp, xt_hi, xt_lo = sem("xt_tp"), sem("xt_hi"), sem("xt_lo")
        m_mm, mt_f, mt_hi, mt_lo = sem("m_mm"), sem("mt_f"), sem("mt_hi"), sem("mt_lo")
        t1_rdy, t1_ok, y2_rdy, y2_hi, y2_lo, res = (sem(n) for n in ("t1_rdy", "t1_ok", "y2_rdy", "y2_hi", "y2_lo", "res"))
        rows_a, rows_b, rows_c, rows_d = sem("rows_a"), sem("rows_b"), sem("rows_c"), sem("rows_d")
        exps_a, exps_b = sem("exps_a"), sem("exps_b")
        bnd = sem("bnd")
        flag, flag_c, fb_dma = sem("flag"), sem("flag_c"), sem("fb_dma")

        passed_v = sem("passed_v")
        fb_range = range(fb_dma.num, fb_dma.num + 1)

        x_v = x.rearrange("b (t p) d -> b p t d", p=P)
        x1_v = x1.rearrange("b (t p) d -> b p t d", p=P)
        win_v = W_inT.rearrange("(k p) n -> k p n", p=P)
        wout_v = W_outT.rearrange("(c k p) n -> c p k n", p=P, k=4)
        stage = [xc[i][:].rearrange("p a b -> p (a b)") for i in range(2)]
        chunks = [(win_h[:, k, :], win_l[:, k, :], win_v[k]) for k in range(KD)]
        chunks += [(wout_h[:, 4 * c:4 * c + 4, :].rearrange("p k n -> p (k n)"),
                    wout_l[:, 4 * c:4 * c + 4, :].rearrange("p k n -> p (k n)"), wout_v[c]) for c in range(KE // 4)]
        NCH = len(chunks)

        def run(body, eng, tail):
            body(0, 0, 0, False, True)
            with eng.Fori(0, B // 2 - 1) as i:
                body(i * 2 + 1, i, 1, True, True)
                body(i * 2 + 2, i + 1, 0, True, True)
            body(B - 1, B // 2 - 1, 1, True, True)
            body(B, B // 2, 0, True, False)
            tail()

        block = ctx.enter_context(nc.Block())

        @block.sync
        def _(sp):
            sp.dma_start(xl[:], x_v[0]).then_inc(x_ld, 16)
            for c, (_, _, src) in enumerate(chunks):
                if c >= 2:
                    sp.wait_ge(stg_h, c - 1)
                    sp.wait_ge(stg_l, c - 1)
                dst = stage[c % 2] if c < KD else stage[c % 2].rearrange("p (k n) -> p k n", k=4)
                sp.dma_start(dst, src).then_inc(stg[c % 2], 16)
                if c == 0:
                    with nc.allow_non_contiguous_dma(reason="small parameters"):
                        sp.dma_start(wx_raw[:], W_xprojT.rearrange("(k p) n -> p k n", p=P)).then_inc(w_ld, 16)
                        sp.dma_start(cw[:], conv_w.rearrange("(k p) n -> p k n", p=P)).then_inc(w_ld, 16)
                        sp.dma_start(cb[:], conv_b.rearrange("(k p) -> p k", p=P)).then_inc(w_ld, 16)
                        sp.dma_start(dp[:], D_param.rearrange("(k p) -> p k", p=P)).then_inc(w_ld, 16)
                        sp.dma_start(a_log[:], A_log.rearrange("(k p) -> k p", p=1)).then_inc(w_ld, 16)

            def body(b, k, par, prev, cur):
                if cur and not (isinstance(b, int) and b == B - 1):
                    sp.wait_ge(ln, 7 * b + 7)
                    sp.dma_start(xl[:], x_v[b + 1]).then_inc(x_ld, 16)
                if prev:
                    wait(sp, x1_st, 16 * (b - 1))
                    sp.dma_start(xres[:], x_v[b - 1]).then_inc(xres_ld, 16)
                    sp.wait_ge(res, 2 * b)
                    sp.dma_start(x1_v[b - 1], xres[:]).then_inc(x1_st, 16)

            run(body, sp, lambda: sp.wait_ge(x1_st, 16 * B))

        @block.gpsimd
        def _(pool):
            g = nc.gpsimd
            g.memset(ident[:], 0.0).then_inc(setup_pool, 1)
            g.memset(mask[:], 1.0).then_inc(setup_pool, 1)
            g.memset(half[:], -0.5).then_inc(setup_pool, 1)
            g.memset(f32(wx_h[:]), 0.0).then_inc(setup_pool, 1)
            g.memset(f32(wx_l[:]), 0.0).then_inc(setup_pool, 1)
            pool.wait_ge(setup_pool, 5)
            g.affine_select(out=ident[:], in_=ident[:], compare_op=ALU.not_equal, fill=1.0, base=0,
                            pattern=[[-1, P]], channel_multiplier=1).then_inc(setup_pool, 1)
            g.affine_select(out=mask[:, 0:S], in_=mask[:, 0:S], compare_op=ALU.is_ge, fill=0.0, base=0,
                            pattern=[[1, S]], channel_multiplier=-1).then_inc(setup_pool, 1)
            g.affine_select(out=mask[:, S:S + P], in_=mask[:, S:S + P], compare_op=ALU.is_ge, fill=0.0, base=0,
                            pattern=[[1, P]], channel_multiplier=-1).then_inc(setup_pool, 1)

            def rsqrt(b):
                pool.wait_ge(ln, 7 * b + 5)
                g.tensor_tensor(rs[:], ve[:], half[:], ALU.pow).then_inc(rstd, 1)

            def recurrence(b, par, d):
                o = 1 - par
                g.memset(hst[:], 0.0)
                with pool.Fori(0, S // CL) as c:
                    pool.drain()
                    with nc.allow_non_contiguous_dma(reason="rows to all partitions"):
                        for r in range(3):
                            src = rows_dram[r].rearrange("(o n) t -> o n t", o=1)[:, :, bass.ds(c * CL, CL)].broadcast_to([P, N, CL])
                            pool.dma_start(abc[:, r], src).then_inc(fb_dma, 16)
                    pool.wait_ge(fb_dma, 48)
                    pool.dma_reset(fb_range)
                    pool.sem_clear(fb_dma)
                    g.tensor_copy(xch[:], xc[o][:, d, bass.ds(c * CL, CL)])
                    for t in range(CL):
                        pool.drain()
                        g.tensor_tensor(hst[:], hst[:], abc[:, 0, :, t], ALU.mult)
                        g.tensor_tensor(bxs[:], abc[:, 1, :, t], xch[:, t:t + 1].broadcast_to([P, N]), ALU.mult)
                        pool.drain()
                        g.tensor_tensor(hst[:], hst[:], bxs[:], ALU.add)
                        pool.drain()
                        g.tensor_scalar(hst[:], hst[:], 100.0, -100.0, ALU.min, ALU.max)
                        pool.drain()
                        g.tensor_tensor(hcb[:, t], hst[:], abc[:, 2, :, t], ALU.mult)
                    w = N
                    while w > 1:
                        w //= 2
                        pool.drain()
                        g.tensor_tensor(hcb[:, :, 0:w], hcb[:, :, 0:w], hcb[:, :, w:2 * w], ALU.add)
                    pool.drain()
                    g.tensor_tensor(t1[:, d % 2, bass.ds(c * CL, CL)], hcb[:, :, 0],
                                    zs[:, d, bass.ds(c * CL, CL)], ALU.mult)
                pool.drain()

            rsqrt(0)

            def body(b, k, par, prev, cur):
                if prev:
                    beyond = pool.value_load(flg[1 - par][0:1, 0:1])
                    for d in range(KE):
                        pool.wait_ge(t1_rdy, 8 * (b - 1) + d + 1)
                        pool.sem_inc(flag_c, 1)
                        with pool.If(beyond > 999):
                            recurrence(b, par, d)
                        pool.sem_inc(t1_ok, 1)
                if cur:
                    pool.wait_ge(flag, b + 1)
                    pool.sem_inc(flag_c, 1)
                    g.partition_all_reduce(flr[:], fl[:], P, RMAX)
                    pool.drain()
                    g.tensor_tensor(fls[:, 0:1], flr[:, 0:1], flr[:, 1:2], ALU.mult)
                    pool.drain()
                    g.tensor_scalar(fls[:, 1:2], fls[:, 0:1], flr[:, 2:3], 1000.0, ALU.max, ALU.mult)
                    pool.drain()
                    g.tensor_scalar(flg[par][:], fls[:, 1:2], 1.0e6, None, ALU.min)
                    pool.drain()
                    again = pool.value_load(flg[par][0:1, 0:1])
                    with pool.If(again > 999):
                        for r, row in enumerate((abar, Bb, Cr)):
                            pool.dma_start(rows_dram[r], row[:]).then_inc(fb_dma, 16)
                        pool.wait_ge(fb_dma, 48)
                        pool.dma_reset(fb_range)
                        pool.sem_clear(fb_dma)
                    pool.sem_inc(rows_d, 1)
                    if not (isinstance(b, int) and b == B - 1):
                        rsqrt(b + 1)

            run(body, pool, lambda: None)

        @block.tensor
        def _(pe):
            def split_mm(out, hi_w, lo_w, hi_x, lo_x, first, last):
                pe.matmul(out, lo_w, hi_x, start=first, stop=False)
                pe.matmul(out, hi_w, lo_x, start=False, stop=False)
                return pe.matmul(out, hi_w, hi_x, start=False, stop=last)

            pe.wait_ge(setup_pool, 8)
            pe.wait_ge(setup_dve, 1)

            def body(b, k, par, prev, cur):
                def ring(n):
                    m = n - 3
                    if m < 0:
                        wait(pe, z_rdy, 8 * (b - 1) + m + 8 + 1)
                    elif m < 8:
                        if cur:
                            pe.wait_ge(conv, 24 * b + 3 * m + 3)
                        else:
                            pe.wait_ge(z_rdy, 8 * b)
                    elif m < 16:
                        if prev:
                            pe.wait_ge(t1_rdy, 8 * (b - 1) + m - 8 + 1)
                        else:
                            pe.wait_ge(conv, 24 * b + 24)
                    else:
                        pe.wait_ge(z_rdy, 8 * b + m - 16 + 1)
                    return psP[n % 3]

                def in_proj(n, m, done):
                    ps = ring(n)
                    for kk in range(KD):
                        if isinstance(b, int) and b == 0 and m == 0:
                            pe.wait_ge(stg_h, kk + 1)
                            pe.wait_ge(stg_l, kk + 1)
                        c = slice(m * P, m * P + P)
                        mm = split_mm(ps[:, 0:S], win_h[:, kk, c], win_l[:, kk, c], xnT_h[:, kk, :], xnT_l[:, kk, :],
                                      kk == 0, kk == KD - 1)
                    mm.then_inc(done, 1)

                def x_dbl(i):
                    pe.wait_ge(xc_lo, 8 * b + i + 1)
                    if i == 0:
                        wait(pe, mt_f, b)
                        if isinstance(b, int) and b == 0:
                            pe.wait_ge(setup_dve, 3)
                    split_mm(psX[:, 0:S], wx_h[:, i, :], wx_l[:, i, :], xcr_h[:, i % 2, :], xcr_l[:, i % 2, :],
                             i == 0, i == KE - 1).then_inc(xd_mm, 1)

                if cur:
                    pe.wait_ge(ln, 7 * b + 7)
                    for h in range(2):
                        wait(pe, xt_lo, 4 * (b - 1) + 3 + h)
                        for kk in range(2):
                            for t in range(TT):
                                mm = pe.transpose(psT[h][:, kk * S + t * P:kk * S + (t + 1) * P],
                                                  xn[:, t, (2 * h + kk) * P:(2 * h + kk + 1) * P], ident[:])
                        mm.then_inc(xn_tp, 1)
                    pe.wait_ge(xnT_lo, 2 * b + 2)
                    for i in range(KE):
                        in_proj(i, i, x_mm)
                        if i >= 2:
                            x_dbl(i - 2)
                    x_dbl(KE - 2)
                    x_dbl(KE - 1)
                if prev:
                    pe.wait_ge(mt_lo, b)
                    pe.wait_ge(xt_lo, 4 * b)

                    def out_proj(d):
                        pe.wait_ge(y2_lo, 8 * (b - 1) + d + 1)
                        if d == 0:
                            wait(pe, res, 2 * (b - 1))
                        for t in range(TT):
                            c = slice(t * P, t * P + P)
                            mm = split_mm(psO[t][:], y2_h[:, d % 2, c], y2_l[:, d % 2, c], wout_h[:, d, :], wout_l[:, d, :],
                                          d == 0, d == KE - 1)
                        mm.then_inc(o_mm, 1)

                    for d in range(KE):
                        ps = ring(8 + d)
                        c = slice(d * P, d * P + P)
                        split_mm(ps[:, 0:S], XT_h[:, 0, c], XT_l[:, 0, c], MT_h[:, 0:S], MT_l[:, 0:S], True, False)
                        split_mm(ps[:, P:S], XT_h[:, 1, c], XT_l[:, 1, c], MT_h[:, S:], MT_l[:, S:], False, True).then_inc(y_mm, 1)
                        if d >= 2:
                            out_proj(d - 2)
                    out_proj(KE - 2)
                    out_proj(KE - 1)
                if cur:
                    for j in range(4):
                        pe.wait_ge(xc_rdy, 8 * b + 2 * j + 2)
                        if j < 2:
                            pe.wait_ge(xnT_lo, 2 * b + j + 1)
                        else:
                            pe.wait_ge(xt_lo, 4 * b + j - 1)
                        for t in range(TT):
                            for i in range(2):
                                mm = pe.transpose(psT[j % 2][:, (2 * t + i) * P:(2 * t + i + 1) * P],
                                                  xc[par][:, 2 * j + i, t * P:(t + 1) * P], ident[:])
                        mm.then_inc(xt_tp, 1)
                    for i in range(KE):
                        in_proj(16 + i, KE + i, z_mm)
                    pe.wait_ge(rows_c, 2 * b + 2)
                    for n in range(NI):
                        i = n if n < NB else n - NB + HB
                        c = i * BL if n < NB else S + (n - NB) * BL
                        mm = pe.matmul(psX[:, c:c + BL], EB[:, n, :], EC[:, i * BL:(i + 1) * BL], start=True, stop=True)
                    mm.then_inc(m_mm, 1)

            run(body, pe, lambda: None)

        @block.scalar
        def _(act):
            def copy(out, in_, done):
                act.activation(out, in_, ACT.Copy).then_inc(done, 1)

            for c, (hi, _, _) in enumerate(chunks):
                act.wait_ge(stg[c % 2], 16 * (c // 2 + 1))
                copy(hi, stage[c % 2], stg_h)
            act.wait_ge(w_ld, 80)
            act.activation(a_neg[:], a_log[:], ACT.Exp).then_inc(setup_act, 1)
            act.wait_ge(stg_l, NCH)

            def body(b, k, par, prev, cur):
                if cur:
                    wait(act, z_mm, 8 * b)
                    for h in range(2):
                        act.wait_ge(xn_tp, 2 * b + h + 1)
                        copy(xnT_h[:, 2 * h:2 * h + 2, :], psT[h][:].rearrange("p (k s) -> p k s", k=2), xnT_hi)

                    def silu(i):
                        act.wait_ge(conv, 24 * b + 3 * i + 3)
                        if i == 0:
                            wait(act, y2_rdy, 8 * (b - 1))
                        act.activation(xc[par][:, i, :], v[:, i % 2, :], ACT.Silu).then_inc(xc_rdy, 1)
                        act.wait_ge(xc_rdy, 8 * b + i + 1)
                        wait(act, xd_mm, 8 * b + i - 1)
                        copy(xcr_h[:, i % 2, :], xc[par][:, i, :], xc_hi)

                    for i in range(KE):
                        act.wait_ge(x_mm, 8 * b + i + 1)
                        wait(act, xc_rdy, 8 * b + i - 1)
                        act.activation(v[:, i % 2, :], psP[i % 3][:, 0:S], ACT.Identity,
                                       scale=cw[:, i, 3:4], bias=cb[:, i:i + 1]).then_inc(v_rdy, 1)
                        if i >= 1:
                            silu(i - 1)
                    silu(KE - 1)

                def y_hi(d):
                    act.wait_ge(y2_rdy, 8 * (b - 1) + d + 1)
                    wait(act, o_mm, 8 * (b - 1) + max(d - 1, 0))
                    copy(y2_h[:, d % 2, :], y2[:, d % 2, :], y2_hi)

                for d in range(KE):
                    if prev:
                        y_hi(d)
                    if cur and d == 1:
                        act.wait_ge(rows_a, 3 * b + 3)
                        ch = Chain(act, exps_a, 2, b)
                        ch.did(act.activation(dt_r[:], dt_r[:], ACT.Exp))
                        ch.wait()
                        ch.did(act.activation(dt_r[:], dt_r[:], ACT.Ln, bias=1.0))
                    if cur and d == 4:
                        act.wait_ge(rows_b, 11 * b + 11)
                        act.activation(abar[:], l_r[:], ACT.Exp).then_inc(exps_b, 1)
                        act.activation(EB[:], EB[:], ACT.Exp, scale=-1.0).then_inc(exps_b, 1)
                        act.activation(EC[:], EC[:], ACT.Exp).then_inc(exps_b, 1)
                if cur:
                    for j in range(4):
                        act.wait_ge(xt_tp, 4 * b + j + 1)
                        copy(XT_h[:, :, 2 * j * P:(2 * j + 2) * P], psT[j % 2][:].rearrange("p (t s) -> p t s", t=TT), xt_hi)
                    for i in range(KE):
                        act.wait_ge(z_mm, 8 * b + i + 1)
                        wait(act, t1_ok, 8 * (b - 1) + i + 1)
                        act.activation(zs[:, i, :], psP[(16 + i) % 3][:, 0:S], ACT.Silu).then_inc(z_rdy, 1)
                    act.wait_ge(mt_f, b + 1)
                    wait(act, y_mm, 8 * b)
                    copy(MT_h[:], MTf[:], mt_hi)

            run(body, act, lambda: None)

        @block.vector
        def _(dve):
            def minus(out, a, b_, done):
                dve.tensor_tensor(out, a, b_, ALU.subtract).then_inc(done, 1)

            def layernorm(b):
                ch = Chain(dve, ln, 7, b)
                dve.wait_ge(x_ld, 16 * b + 16)
                for t in range(TT):
                    ch.did(dve.bn_stats(st[:, t, :], xl[:, t, :]))
                ch.wait()
                dve.sem_inc(passed_v, 1)
                for t in range(TT):
                    ch.did(dve.bn_aggr(mv[:, t, :], st[:, t, :]))
                ch.wait()
                ch.did(dve.tensor_scalar(ve[:], mv[:, :, 1], EPS, None, ALU.add))
                wait(dve, xn_tp, 2 * b)
                dve.wait_ge(rstd, b + 1)
                for t in range(TT):
                    ch.did(dve.tensor_scalar(xn[:, t, :], xl[:, t, :], mv[:, t, 0:1], rs[:, t:t + 1],
                                             ALU.subtract, ALU.mult))

            dve.memset(ones_row[:], 1.0).then_inc(setup_dve, 1)
            dve.memset(lam[:, 0:1], 0.0).then_inc(setup_act, 1)
            dve.memset(fl[:], 0.0).then_inc(setup_act, 1)
            dve.memset(scl[:, 0:1], 0.01).then_inc(setup_act, 1)
            dve.memset(scl[:, 1:2], 1.0 / 60).then_inc(setup_act, 1)
            dve.wait_ge(setup_pool, 3)
            layernorm(0)
            for c, (hi, lo, _) in enumerate(chunks):
                dve.wait_ge(stg_h, c + 1)
                minus(lo, stage[c % 2], f32(hi), stg_l)
                if c == 0:
                    dve.wait_ge(w_ld, 80)
                    dve.wait_ge(setup_pool, 5)
                    cols = [(wx_raw[:, :, 0:N], slice(0, N)), (wx_raw[:, :, N:2 * N], slice(32, 32 + N)),
                            (wx_raw[:, :, 2 * N:2 * N + 1].broadcast_to([P, KE, N]), slice(64, 64 + N))]
                    for src, at in cols:
                        ins = dve.tensor_copy(wx_h[:, :, at], src)
                    ins.then_inc(setup_dve, 1)
                    dve.wait_ge(setup_dve, 2)
                    for src, at in cols:
                        ins = dve.tensor_tensor(wx_l[:, :, at], src, f32(wx_h[:, :, at]), ALU.subtract)
                    ins.then_inc(setup_dve, 1)
            dve.wait_ge(setup_act, 5)
            dve.tensor_scalar(a_neg[:], a_neg[:], -1.0, None, ALU.mult).then_inc(setup_dve, 1)

            def body(b, k, par, prev, cur):
                first = isinstance(b, int) and b == 0
                if cur:
                    for h in range(2):
                        dve.wait_ge(xnT_hi, 2 * b + h + 1)
                        minus(xnT_l[:, 2 * h:2 * h + 2, :], psT[h][:].rearrange("p (k s) -> p k s", k=2),
                              f32(xnT_h[:, 2 * h:2 * h + 2, :]), xnT_lo)

                    def x_lo(i):
                        dve.wait_ge(xc_hi, 8 * b + i + 1)
                        minus(xcr_l[:, i % 2, :], xc[par][:, i, :], f32(xcr_h[:, i % 2, :]), xc_lo)

                    for i in range(KE):
                        dve.wait_ge(v_rdy, 8 * b + i + 1)
                        for j in range(1, 4):
                            dve.scalar_tensor_tensor(out=v[:, i % 2, j:S], in0=psP[i % 3][:, 0:S - j],
                                                     scalar=cw[:, i, 3 - j:4 - j], in1=v[:, i % 2, j:S],
                                                     op0=ALU.mult, op1=ALU.add).then_inc(conv, 1)
                            if j < 3:
                                dve.wait_ge(conv, 24 * b + 3 * i + j)
                        if i >= 1:
                            x_lo(i - 1)
                    x_lo(KE - 1)

                def rows_1():
                    dve.wait_ge(xd_mm, 8 * b + 8)
                    wait(dve, rows_d, b)
                    wait(dve, m_mm, b)
                    dve.tensor_scalar(dt_r[:], psX[64:64 + N, 0:S], 5.0, None, ALU.min).then_inc(rows_a, 1)
                    dve.tensor_copy(Bb[:], psX[0:N, 0:S]).then_inc(rows_a, 1)
                    dve.tensor_copy(Cr[:], psX[32:32 + N, 0:S]).then_inc(rows_a, 1)

                def rows_2():
                    if first:
                        dve.wait_ge(setup_dve, 4)
                    dve.wait_ge(exps_a, 2 * b + 2)
                    dve.wait_ge(rows_a, 3 * b + 3)
                    ch = Chain(dve, rows_b, 11, b)
                    ch.did(dve.tensor_scalar(dt_r[:], dt_r[:], 0.001, 0.1, ALU.max, ALU.min))
                    ch.wait()
                    ch.did(dve.tensor_scalar(l_r[:], dt_r[:], a_neg[:, 0:1], -20.0, ALU.mult, ALU.max))
                    ch.did(dve.tensor_tensor(Bb[:], Bb[:], dt_r[:], ALU.mult))
                    ch.wait()
                    ch.did(dve.tensor_tensor_scan(lam[:, 1:S + 1], ones_row[:], l_r[:], 0.0, ALU.mult, ALU.add))
                    ch.did(dve.tensor_scalar(Bb[:], Bb[:], -10.0, 10.0, ALU.max, ALU.min))
                    ch.wait()
                    ref = lam[:, 0:S].rearrange("n (i t) -> n i t", t=BL)
                    ends = lam[:, 1:S + 1].rearrange("n (i t) -> n i t", t=BL)
                    ch.did(dve.tensor_tensor(EB[:, 0:NB, :], lam[:, 1:P + 1].rearrange("n (o t) -> n o t", o=1).broadcast_to([N, NB, P]),
                                             ref[:, :, 0:1].broadcast_to([N, NB, P]), ALU.subtract))
                    ch.did(dve.tensor_tensor(EB[:, NB:, :], lam[:, P + 1:].rearrange("n (o t) -> n o t", o=1).broadcast_to([N, NI - NB, P]),
                                             ref[:, HB:, 0:1].broadcast_to([N, NI - NB, P]), ALU.subtract))
                    ch.did(dve.tensor_tensor(EC[:].rearrange("n (i t) -> n i t", t=BL), ends,
                                             ref[:, :, 0:1].broadcast_to([N, NB, BL]), ALU.subtract))
                    ch.did(dve.tensor_tensor(rng[:], ref[:, :, 0], ends[:, :, BL - 1], ALU.subtract))
                    ch.did(dve.scalar_tensor_tensor(out=ab[:], in0=Bb[:], scalar=-1.0, in1=Bb[:], op0=ALU.mult, op1=ALU.max))
                    ch.wait()
                    ch.did(dve.tensor_scalar(EB[:], EB[:], -60.0, None, ALU.max))

                def rows_3():
                    dve.wait_ge(exps_b, 3 * b + 3)
                    bb = Bb[:].rearrange("n (o t) -> n o t", t=P)
                    dve.tensor_tensor(EB[:, 0:NB, :], EB[:, 0:NB, :], bb[:, 0:1, :].broadcast_to([N, NB, P]), ALU.mult)
                    dve.tensor_tensor(EB[:, NB:, :], EB[:, NB:, :], bb[:, 1:2, :].broadcast_to([N, NI - NB, P]),
                                      ALU.mult).then_inc(rows_c, 1)
                    dve.tensor_tensor(EC[:], EC[:], Cr[:], ALU.mult).then_inc(rows_c, 1)

                def bounds():
                    wait(dve, rows_d, b)
                    ch = Chain(dve, bnd, 4, b)
                    ch.did(dve.tensor_tensor_scan(gb[:], abar[:], ab[:], 0.0, ALU.mult, ALU.add))
                    ch.did(dve.tensor_reduce(fl[:, 0:1], xc[par][:].rearrange("p a b -> p (a b)"), AX.X, ALU.max,
                                             apply_absolute_value=True))
                    ch.did(dve.tensor_reduce(fl[0:N, 2:3], rng[:], AX.X, ALU.max))
                    ch.wait()
                    ch.did(dve.tensor_reduce(fl[0:N, 1:2], gb[:], AX.X, ALU.max))
                    ch.wait()
                    dve.tensor_tensor(fl[0:N, 1:3], fl[0:N, 1:3], scl[:], ALU.mult).then_inc(flag, 1)

                def y_tile(d):
                    o = 1 - par
                    dve.wait_ge(y_mm, 8 * (b - 1) + d + 1)
                    if d == 0:
                        dve.wait_ge(z_rdy, 8 * b)
                    wait(dve, y2_rdy, 8 * (b - 1) + max(d - 1, 0))
                    dve.tensor_tensor(t1[:, d % 2, :], psP[(8 + d) % 3][:, 0:S], zs[:, d, :], ALU.mult).then_inc(t1_rdy, 1)
                    if d >= 1:
                        y_sum(d - 1)

                def y_sum(d):
                    o = 1 - par
                    dve.wait_ge(t1_ok, 8 * (b - 1) + d + 1)
                    wait(dve, y2_hi, 8 * (b - 1) + max(d - 1, 0))
                    wait(dve, y2_lo, 8 * (b - 1) + max(d - 1, 0))
                    dve.scalar_tensor_tensor(out=y2[:, d % 2, :], in0=xc[o][:, d, :], scalar=dp[:, d:d + 1],
                                             in1=t1[:, d % 2, :], op0=ALU.mult, op1=ALU.add).then_inc(y2_rdy, 1)
                    if d >= 1:
                        y_lo(d - 1)

                def y_lo(d):
                    dve.wait_ge(y2_hi, 8 * (b - 1) + d + 1)
                    minus(y2_l[:, d % 2, :], y2[:, d % 2, :], f32(y2_h[:, d % 2, :]), y2_lo)

                for d in range(KE):
                    if prev:
                        y_tile(d)
                    if cur and d == 0:
                        rows_1()
                    if cur and d == 3:
                        rows_2()
                    if cur and d == 6:
                        rows_3()
                        bounds()
                if prev:
                    y_sum(KE - 1)
                    y_lo(KE - 1)
                    dve.wait_ge(xres_ld, 16 * b)
                    dve.wait_ge(o_mm, 8 * b)
                    for t in range(TT):
                        dve.tensor_tensor(xres[:, t, :], psO[t][:], xres[:, t, :], ALU.add).then_inc(res, 1)
                if cur:
                    for j in range(4):
                        dve.wait_ge(xt_hi, 4 * b + j + 1)
                        c = slice(2 * j * P, (2 * j + 2) * P)
                        minus(XT_l[:, :, c], psT[j % 2][:].rearrange("p (t s) -> p t s", t=TT), f32(XT_h[:, :, c]), xt_lo)
                    if not (isinstance(b, int) and b == B - 1):
                        layernorm(b + 1)
                    dve.wait_ge(m_mm, b + 1)
                    dve.wait_ge(mt_lo, b) if not first else None
                    dve.tensor_tensor(MTf[:], psX[:, 0:S + P], mask[:], ALU.mult).then_inc(mt_f, 1)
                    dve.wait_ge(mt_hi, b + 1)
                    minus(MT_l[:], MTf[:], f32(MT_h[:]), mt_lo)

            run(body, dve, lambda: None)
    return


def attention_phase(nc, x1, ctxT, WqT, bq, WkT, bk, WvT, bv, WoT, bo, Wr, br, y, xn3_d, lg, qs_d, ks_d):
    B, S, _ = x1.shape
    H, DK = 16, 32
    TT = S // P
    G = P // DK
    U = 2 * KD
    NE = Wr.shape[1]
    SCALE = float(DK) ** -0.5
    with ExitStack() as ctx:
        def sb(name, shape, dt=F32):
            return ctx.enter_context(nc.sbuf_tensor("b_" + name, shape, dt))

        def sem(name):
            return ctx.enter_context(nc.semaphore("b_" + name))

        w_h = [sb(f"w_h{i}", [P, KD, D], F32R) for i in range(4)]
        w_l = [sb(f"w_l{i}", [P, KD, D], F32R) for i in range(4)]
        wr, brb = sb("wr", [P, KD, NE]), sb("brb", [P, NE])
        bqc, bkc, bvc, bob = sb("bqc", [P, KD]), sb("bkc", [P, KD]), sb("bvc", [P, KD]), sb("bob", [P, D])
        ident, half = sb("ident", [P, P]), sb("half", [P, TT])
        xa, xres, xn = sb("xa", [P, TT, D]), sb("xres", [P, TT, D]), sb("xn", [P, TT, D])
        xn3 = sb("xn3", [P, TT, D])
        st, mv, ve, rs = sb("st", [P, TT, 6]), sb("mv", [P, TT, 2]), sb("ve", [P, TT]), sb("rs", [P, TT])
        st3, mv3, ve3, rs3 = sb("st3", [P, TT, 6]), sb("mv3", [P, TT, 2]), sb("ve3", [P, TT]), sb("rs3", [P, TT])
        xnT_h, xnT_l = sb("xnT_h", [P, KD, S], F32R), sb("xnT_l", [P, KD, S], F32R)
        cx, cx_h, cx_l = sb("cx", [P, KD, S]), sb("cx_h", [P, KD, S], F32R), sb("cx_l", [P, KD, S], F32R)
        t_h, t_l = sb("t_h", [P, 2, S], F32R), sb("t_l", [P, 2, S], F32R)
        qst = [sb(f"qst{i}", [3 * DK, H, S], F32R) for i in range(2)]
        kst = [sb(f"kst{i}", [3 * DK, H, S], F32R) for i in range(2)]
        V = [sb(f"V{i}", [P, TT, D]) for i in range(2)]
        pr = sb("pr", [P, 2, G, S])
        PT = sb("PT", [P, G, TT, S])
        mx, nm, rsum, rinv = sb("mx", [P, 2, G]), sb("nm", [P, 2, G]), sb("rsum", [P, 2, G]), sb("rinv", [P, 2, G])
        co_h, co_l = sb("co_h", [P, KD, S], F32R), sb("co_l", [P, KD, S], F32R)
        xn3T = xn[:].rearrange("p t d -> p (t d)").rearrange("p (k s) -> p k s", k=KD)

        psS = [ctx.enter_context(nc.psum_tensor(f"b_psS{i}", [P, G, S], F32)) for i in range(2)]
        psT = ctx.enter_context(nc.psum_tensor("b_psT", [P, 2 * G, P], F32))
        psV = ctx.enter_context(nc.psum_tensor("b_psV", [P, 512], F32))
        psQ = ctx.enter_context(nc.psum_tensor("b_psQ", [P, 512], F32))

        w_ld, p_ld, w_hi, w_lo = [sem(f"w_ld{i}") for i in range(2)], sem("p_ld"), sem("w_hi"), sem("w_lo")
        setup = sem("setup")
        xa_ld, xres_ld, cx_ld, x2_st, xn3_st = sem("xa_ld"), sem("xres_ld"), sem("cx_ld"), sem("x2_st"), sem("xn3_st")
        ln, rstd, ln3, rstd3 = sem("ln"), sem("rstd"), sem("ln3"), sem("rstd3")
        xn_tp, xnT_hi, xnT_lo = sem("xn_tp"), sem("xnT_hi"), sem("xnT_lo")
        cx_hi, cx_lo = sem("cx_hi"), sem("cx_lo")
        qk_mm, qk_hi, qk_lo = sem("qk_mm"), sem("qk_hi"), sem("qk_lo")
        tq_st, tk_st = [sem(f"tq_st{i}") for i in range(2)], [sem(f"tk_st{i}") for i in range(2)]
        q_ld, k_ld = sem("q_ld"), sem("k_ld")
        v_mm, v_cp = sem("v_mm"), sem("v_cp")
        s_mm, mx_s, nm_s, exp_s, ri_s, norm_s = (sem(n) for n in ("s_mm", "mx_s", "nm_s", "exp_s", "ri_s", "norm_s"))
        p_tp, pt_cp, pv_mm, co_hi, co_lo = (sem(n) for n in ("p_tp", "pt_cp", "pv_mm", "co_hi", "co_lo"))
        o_mm, x2_s, xb_s = sem("o_mm"), sem("x2_s"), sem("xb_s")
        r_tp, r_cp, r_mm, lg_s = sem("r_tp"), sem("r_cp"), sem("r_mm"), sem("lg_s")

        passed_v, passed_s, passed_p = sem("passed_v"), sem("passed_s"), sem("passed_p")

        x1_v = x1.rearrange("b (t p) d -> b p t d", p=P)
        y_v = y[0:B * S, :].rearrange("(b t p) d -> b p t d", p=P, t=TT)
        xn3_v = xn3_d[0:B * S, :].rearrange("(b t p) d -> b p t d", p=P, t=TT)
        ctx_v = ctxT.rearrange("b (k p) s -> b p k s", p=P)
        stage = [V[i] for i in range(2)]
        weights = (WqT, WkT, WvT, WoT)

        def run(body, eng):
            body(0, 0, True, False, False)
            body(1, 1, True, True, False)
            with eng.Fori(0, B // 2 - 2) as i:
                body(i * 2 + 2, 0, True, True, True)
                body(i * 2 + 3, 1, True, True, True)
            body(B - 2, 0, True, True, True)
            body(B - 1, 1, True, True, True)
            body(B, 0, False, True, True)
            body(B + 1, 1, False, False, True)

        def last(b):
            return isinstance(b, int) and b >= B - 1

        block = ctx.enter_context(nc.Block())

        @block.sync
        def _(sp):
            sp.dma_start(xa[:], x1_v[0]).then_inc(xa_ld, 16)
            sp.dma_start(cx[:], ctx_v[0]).then_inc(cx_ld, 16)
            with nc.allow_non_contiguous_dma(reason="small parameters"):
                for col, src in ((bqc, bq), (bkc, bk), (bvc, bv)):
                    sp.dma_start(col[:], src.rearrange("(k p) -> p k", p=P)).then_inc(p_ld, 16)
                sp.dma_start(wr[:], Wr.rearrange("(k p) n -> p k n", p=P)).then_inc(p_ld, 16)
                sp.dma_start(bob[:], bo.rearrange("(o n) -> o n", o=1).broadcast_to([P, D])).then_inc(p_ld, 16)
                sp.dma_start(brb[:], br.rearrange("(o n) -> o n", o=1).broadcast_to([P, NE])).then_inc(p_ld, 16)
            for c in range(8):
                if c >= 2:
                    sp.wait_ge(w_hi, c - 1)
                    sp.wait_ge(w_lo, c - 1)
                src = weights[c // 2].rearrange("(k p) n -> p k n", p=P)[:, 2 * (c % 2):2 * (c % 2) + 2, :]
                sp.dma_start(stage[c % 2][:], src).then_inc(w_ld[c % 2], 16)

            def body(b, par, cur, prev, prev2):
                if cur and not last(b):
                    sp.wait_ge(ln, 7 * b + 7)
                    sp.dma_start(xa[:], x1_v[b + 1]).then_inc(xa_ld, 16)
                if prev:
                    wait(sp, x2_st, 16 * (b - 1))
                    sp.dma_start(xres[:], x1_v[b - 1]).then_inc(xres_ld, 16)
                if cur and not last(b):
                    sp.wait_ge(cx_lo, b + 1)
                    sp.dma_start(cx[:], ctx_v[b + 1]).then_inc(cx_ld, 16)
                if cur:
                    for scratch, st_, ld, stack, first in ((qs_d, tq_st, q_ld, qst, 0), (ks_d, tk_st, k_ld, kst, KD)):
                        wait(sp, ld, 48 * b)
                        sp.sem_inc(passed_s, 1)
                        for i in range(KD):
                            sp.wait_ge(qk_lo, U * b + first + i + 1)
                            for part, t in enumerate((t_h, t_l)):
                                sp.dma_start(f32(scratch[part, i * P:(i + 1) * P, :]), f32(t[:, (first + i) % 2, :])).then_inc(st_[i % 2], 16)
                        for p_ in range(2):
                            sp.wait_ge(st_[p_], 64 * b + 64)
                            sp.sem_inc(passed_s, 1)
                        wait(sp, s_mm, U * (b - 1))
                        parts = (0, 1, 0) if scratch is qs_d else (0, 0, 1)
                        for r, part in enumerate(parts):
                            sp.dma_start(f32(stack[par][r * DK:(r + 1) * DK, :, :]),
                                         f32(scratch[part].rearrange("(h d) s -> d h s", d=DK))).then_inc(ld, 16)
                if prev:
                    sp.wait_ge(x2_s, 2 * b)
                    sp.dma_start(y_v[b - 1], xres[:]).then_inc(x2_st, 16)
                    sp.wait_ge(ln3, 7 * b)
                    sp.dma_start(xn3_v[b - 1], xn3[:]).then_inc(xn3_st, 16)

            run(body, sp)
            sp.wait_ge(x2_st, 16 * B)
            sp.wait_ge(xn3_st, 16 * B)

        @block.gpsimd
        def _(pool):
            g = nc.gpsimd
            g.memset(ident[:], 0.0).then_inc(setup, 1)
            g.memset(half[:], -0.5).then_inc(setup, 1)
            pool.wait_ge(setup, 2)
            g.affine_select(out=ident[:], in_=ident[:], compare_op=ALU.not_equal, fill=1.0, base=0,
                            pattern=[[-1, P]], channel_multiplier=1).then_inc(setup, 1)

            def rsqrt(b, ln_, ve_, rs_, done):
                pool.wait_ge(ln_, 7 * b + 5)
                g.tensor_tensor(rs_[:], ve_[:], half[:], ALU.pow).then_inc(done, 1)

            rsqrt(0, ln, ve, rs, rstd)

            def body(b, par, cur, prev, prev2):
                if cur:
                    wait(pool, v_mm, 2 * b)
                    pool.wait_ge(cx_ld, 16 * b + 16)
                    g.sem_inc(passed_p, 1)
                    g.tensor_copy(cx_h[:], cx[:]).then_inc(cx_hi, 1)
                    pool.wait_ge(cx_hi, b + 1)
                    g.tensor_tensor(cx_l[:], cx[:], f32(cx_h[:]), ALU.subtract).then_inc(cx_lo, 1)
                if prev:
                    pool.wait_ge(xres_ld, 16 * b)
                    if isinstance(b, int) and b == 1:
                        pool.wait_ge(p_ld, 96)
                    for t in range(TT):
                        g.tensor_tensor(xres[:, t, :], xres[:, t, :], bob[:], ALU.add).then_inc(xb_s, 1)
                if cur and not last(b):
                    rsqrt(b + 1, ln, ve, rs, rstd)
                if prev:
                    rsqrt(b - 1, ln3, ve3, rs3, rstd3)

            run(body, pool)

        @block.tensor
        def _(pe):
            def split_mm(out, hi_w, lo_w, hi_x, lo_x, first, last_):
                pe.matmul(out, lo_w, hi_x, start=first, stop=False)
                pe.matmul(out, hi_w, lo_x, start=False, stop=False)
                return pe.matmul(out, hi_w, hi_x, start=False, stop=last_)

            def turn_xn(b):
                pe.wait_ge(ln, 7 * b + 7)
                wait(pe, pt_cp, U * (b - 1))
                for kk in range(KD):
                    for t in range(TT):
                        mm = pe.transpose(psT[:, 2 * kk + t, :], xn[:, t, kk * P:(kk + 1) * P], ident[:])
                mm.then_inc(xn_tp, 1)

            pe.wait_ge(setup, 3)
            turn_xn(0)
            pe.wait_ge(w_lo, 8)

            def body(b, par, cur, prev, prev2):
                o = 1 - par

                def qk_tile(i):
                    m = i % KD
                    if i:
                        pe.wait_ge(qk_lo, U * b + i)
                    else:
                        wait(pe, x2_s, 2 * (b - 1))
                        wait(pe, v_cp, 2 * b)
                        wait(pe, lg_s, b - 1)
                        pe.wait_ge(xnT_lo, b + 1)
                    if i == KD:
                        pe.wait_ge(cx_lo, b + 1)
                    n = i // KD
                    xh, xl = (xnT_h, xnT_l) if n == 0 else (cx_h, cx_l)
                    for kk in range(KD):
                        c = slice(m * P, m * P + P)
                        mm = split_mm(psQ[:, 0:S], w_h[n][:, kk, c], w_l[n][:, kk, c], xh[:, kk, :], xl[:, kk, :],
                                      kk == 0, kk == KD - 1)
                    mm.then_inc(qk_mm, 1)

                def v_tile(t):
                    if t:
                        pe.wait_ge(v_cp, 2 * b + 1)
                    else:
                        pe.wait_ge(qk_lo, U * b + U)
                    c = slice(t * P, t * P + P)
                    for kk in range(KD):
                        mm = split_mm(psQ[:], cx_h[:, kk, c], cx_l[:, kk, c], w_h[2][:, kk, :], w_l[2][:, kk, :],
                                      kk == 0, kk == KD - 1)
                    mm.then_inc(v_mm, 1)

                def scores(u):
                    j, qt = u // TT, u % TT
                    wait(pe, exp_s, U * G * 0 + 4 * (U * (b - 1) + u - 1))
                    if u == 0:
                        pe.wait_ge(q_ld, 48 * b)
                        pe.wait_ge(k_ld, 48 * b)
                    for h in range(G):
                        mm = pe.matmul(psS[u % 2][:, h, :], qst[o][:, G * j + h, qt * P:(qt + 1) * P],
                                       kst[o][:, G * j + h, :], start=True, stop=True)
                    mm.then_inc(s_mm, 1)

                def turn_p(u):
                    pe.wait_ge(norm_s, U * (b - 1) + u + 1)
                    if u:
                        pe.wait_ge(pt_cp, U * (b - 1) + u)
                    elif prev2:
                        pe.wait_ge(r_cp, b - 1)
                    else:
                        pe.wait_ge(xnT_lo, b + 1 if cur else b)
                    for h in range(G):
                        for kt in range(TT):
                            mm = pe.transpose(psT[:, 2 * h + kt, :], pr[:, u % 2, h, kt * P:(kt + 1) * P], ident[:])
                    mm.then_inc(p_tp, 1)

                def pv(j):
                    pe.wait_ge(pt_cp, U * (b - 1) + 2 * j + 2)
                    wait(pe, co_lo, 4 * (b - 1) + j)
                    if j == 0:
                        pe.wait_ge(v_cp, 2 * b)
                    for kt in range(TT):
                        for h in range(G):
                            c = slice((G * j + h) * DK, (G * j + h + 1) * DK)
                            mm = pe.matmul(psV[h * DK:(h + 1) * DK, 0:S], V[o][:, kt, c], PT[:, h, kt, :],
                                           start=kt == 0, stop=kt == TT - 1)
                    mm.then_inc(pv_mm, 1)

                if prev:
                    scores(0)
                if prev2:
                    pe.wait_ge(ln3, 7 * (b - 1))
                    if cur:
                        pe.wait_ge(xnT_lo, b + 1)
                    else:
                        wait(pe, pt_cp, U * (b - 1))
                    for kk in range(KD):
                        for t in range(TT):
                            mm = pe.transpose(psT[:, 2 * kk + t, :], xn3[:, t, kk * P:(kk + 1) * P], ident[:])
                    mm.then_inc(r_tp, 1)
                for u in range(U):
                    if prev and u + 1 < U:
                        scores(u + 1)
                    if u == 0 and prev2:
                        pe.wait_ge(r_cp, b - 1)
                        wait(pe, x2_s, 2 * (b - 1))
                        for t in range(TT):
                            for kk in range(KD):
                                mm = pe.matmul(psQ[:, t * NE:(t + 1) * NE], xn3T[:, kk, t * P:(t + 1) * P], wr[:, kk, :],
                                               start=kk == 0, stop=kk == KD - 1)
                        mm.then_inc(r_mm, 1)
                    if cur:
                        qk_tile(u)
                    if prev and u:
                        turn_p(u - 1)
                    if prev and u >= 3 and u % 2:
                        pv((u - 3) // 2)
                if cur:
                    v_tile(0)
                if prev:
                    turn_p(U - 1)
                if cur:
                    v_tile(1)
                if prev:
                    pv(KD - 1)
                if cur and not last(b):
                    turn_xn(b + 1)
                if prev:
                    for t in range(TT):
                        pe.wait_ge(co_lo, 4 * b)
                        if t:
                            pe.wait_ge(x2_s, 2 * (b - 1) + 1)
                        elif cur:
                            pe.wait_ge(v_cp, 2 * b + 2)
                        else:
                            pe.wait_ge(lg_s, b - 1)
                        c = slice(t * P, t * P + P)
                        for kk in range(KD):
                            mm = split_mm(psQ[:], co_h[:, kk, c], co_l[:, kk, c], w_h[3][:, kk, :], w_l[3][:, kk, :],
                                          kk == 0, kk == KD - 1)
                        mm.then_inc(o_mm, 1)

            run(body, pe)

        @block.scalar
        def _(act):
            def copy(out, in_, done):
                act.activation(out, in_, ACT.Copy).then_inc(done, 1)

            for c in range(8):
                act.wait_ge(w_ld[c % 2], 16 * (c // 2 + 1))
                copy(w_h[c // 2][:, 2 * (c % 2):2 * (c % 2) + 2, :], stage[c % 2][:], w_hi)

            def split_xn(b):
                act.wait_ge(xn_tp, b + 1)
                wait(act, qk_mm, U * (b - 1) + 4)
                copy(xnT_h[:], psT[:].rearrange("p (k t) s -> p k (t s)", t=TT), xnT_hi)

            split_xn(0)
            act.wait_ge(p_ld, 96)
            act.wait_ge(w_lo, 8)

            def body(b, par, cur, prev, prev2):
                o = 1 - par

                def qk_hi_(i):
                    act.wait_ge(qk_mm, U * b + i + 1)
                    n, m = i // KD, i % KD
                    if m >= 2:
                        act.wait_ge((tq_st, tk_st)[n][m % 2], 64 * b + 32)
                    elif n == 1:
                        act.wait_ge(tq_st[m % 2], 64 * b + 64)
                    else:
                        wait(act, tk_st[m % 2], 64 * b)
                    act.activation(t_h[:, i % 2, :], psQ[:, 0:S], ACT.Identity,
                                   bias=(bqc, bkc)[n][:, m:m + 1]).then_inc(qk_hi, 1)

                def exps(u):
                    act.wait_ge(nm_s, U * (b - 1) + u + 1)
                    wait(act, p_tp, U * (b - 1) + u - 1)
                    wait(act, norm_s, U * (b - 1) + u - 1)
                    for h in range(G):
                        act.activation(pr[:, u % 2, h, :], psS[u % 2][:, h, :], ACT.Exp, bias=nm[:, u % 2, h:h + 1],
                                       scale=SCALE, accum_out=rsum[:, u % 2, h:h + 1]).then_inc(exp_s, 1)

                def pt_copy(u):
                    act.wait_ge(p_tp, U * (b - 1) + u + 1)
                    if u % 2 == 0:
                        wait(act, pv_mm, 4 * (b - 1) + u // 2)
                    c = slice((u % 2) * P, (u % 2) * P + P)
                    copy(PT[:, :, :, c], psT[:].rearrange("p (h k) s -> p h k s", k=TT), pt_cp)

                def ctx_hi(j):
                    act.wait_ge(pv_mm, 4 * (b - 1) + j + 1)
                    wait(act, o_mm, 2 * (b - 1))
                    act.activation(co_h[:, j, :], psV[:, 0:S], ACT.Identity, bias=bvc[:, j:j + 1]).then_inc(co_hi, 1)

                def v_copy(t):
                    act.wait_ge(v_mm, 2 * b + t + 1)
                    wait(act, pv_mm, 4 * (b - 1))
                    copy(V[par][:, t, :], psQ[:], v_cp)

                if prev2:
                    act.wait_ge(r_tp, b - 1)
                    copy(xn3T, psT[:].rearrange("p (k t) s -> p k (t s)", t=TT), r_cp)
                for u in range(U):
                    if prev:
                        exps(u)
                    if cur:
                        qk_hi_(u)
                    if prev and u:
                        pt_copy(u - 1)
                    if prev and u >= 3 and u % 2:
                        ctx_hi((u - 3) // 2)
                if cur:
                    v_copy(0)
                if prev:
                    pt_copy(U - 1)
                if cur:
                    v_copy(1)
                if prev:
                    ctx_hi(KD - 1)
                if cur and not last(b):
                    split_xn(b + 1)

            run(body, act)

        @block.vector
        def _(dve):
            def minus(out, a, b_, done):
                dve.tensor_tensor(out, a, b_, ALU.subtract).then_inc(done, 1)

            def layernorm(b, src, ready, st, mv, ve, rs, rstd, out, read, sem_):
                ch = Chain(dve, sem_, 7, b)
                ready()
                for t in range(TT):
                    ch.did(dve.bn_stats(st[:, t, :], src[:, t, :]))
                ch.wait()
                dve.sem_inc(passed_v, 1)
                for t in range(TT):
                    ch.did(dve.bn_aggr(mv[:, t, :], st[:, t, :]))
                ch.wait()
                ch.did(dve.tensor_scalar(ve[:], mv[:, :, 1], EPS, None, ALU.add))
                return ch

            def normalize(ch, b, src, mv, rs, rstd, out, read):
                dve.wait_ge(rstd, b + 1)
                read()
                for t in range(TT):
                    ch.did(dve.tensor_scalar(out[:, t, :], src[:, t, :], mv[:, t, 0:1], rs[:, t:t + 1],
                                             ALU.subtract, ALU.mult))

            def ln2(b):
                ch = layernorm(b, xa, lambda: dve.wait_ge(xa_ld, 16 * b + 16), st, mv, ve, rs, rstd, xn, None, ln)
                normalize(ch, b, xa, mv, rs, rstd, xn, lambda: wait(dve, xn_tp, b))

            def split_xn(b):
                dve.wait_ge(xnT_hi, b + 1)
                minus(xnT_l[:], psT[:].rearrange("p (k t) s -> p k (t s)", t=TT), f32(xnT_h[:]), xnT_lo)

            ln2(0)
            for c in range(8):
                dve.wait_ge(w_hi, c + 1)
                minus(w_l[c // 2][:, 2 * (c % 2):2 * (c % 2) + 2, :], stage[c % 2][:],
                      f32(w_h[c // 2][:, 2 * (c % 2):2 * (c % 2) + 2, :]), w_lo)
            split_xn(0)
            dve.wait_ge(p_ld, 96)

            def body(b, par, cur, prev, prev2):
                o = 1 - par

                def qk_lo_(i):
                    n, m = i // KD, i % KD
                    dve.wait_ge(qk_hi, U * b + i + 1)
                    dve.scalar_tensor_tensor(out=t_l[:, i % 2, :], in0=psQ[:, 0:S], scalar=(bqc, bkc)[n][:, m:m + 1],
                                             in1=f32(t_h[:, i % 2, :]), op0=ALU.add, op1=ALU.subtract).then_inc(qk_lo, 1)

                def row_max(u):
                    n = U * (b - 1) + u
                    dve.wait_ge(s_mm, n + 1)
                    wait(dve, exp_s, 4 * (n - 1))
                    wait(dve, nm_s, n - 1)
                    dve.tensor_reduce(mx[:, u % 2, :], psS[u % 2][:], AX.X, ALU.max).then_inc(mx_s, 1)
                    dve.wait_ge(mx_s, n + 1)
                    dve.tensor_scalar(nm[:, u % 2, :], mx[:, u % 2, :], -SCALE, None, ALU.mult).then_inc(nm_s, 1)

                def norm(u):
                    n = U * (b - 1) + u
                    dve.wait_ge(exp_s, 4 * (n + 1))
                    wait(dve, norm_s, n - 1)
                    dve.reciprocal(rinv[:, u % 2, :], rsum[:, u % 2, :]).then_inc(ri_s, 1)
                    dve.wait_ge(ri_s, n + 1)
                    for h in range(G):
                        ins = dve.tensor_scalar(pr[:, u % 2, h, :], pr[:, u % 2, h, :], rinv[:, u % 2, h:h + 1], None, ALU.mult)
                    ins.then_inc(norm_s, 1)

                def ctx_lo(j):
                    dve.wait_ge(co_hi, 4 * (b - 1) + j + 1)
                    dve.scalar_tensor_tensor(out=co_l[:, j, :], in0=psV[:, 0:S], scalar=bvc[:, j:j + 1],
                                             in1=f32(co_h[:, j, :]), op0=ALU.add, op1=ALU.subtract).then_inc(co_lo, 1)

                if prev:
                    row_max(0)
                for u in range(U):
                    if prev and u + 1 < U:
                        row_max(u + 1)
                    if u == 0 and prev2:
                        dve.wait_ge(r_mm, b - 1)
                        for t in range(TT):
                            ins = dve.tensor_tensor(lg[:, bass.ds((b * TT + (t - 2 * TT)) * NE, NE)], psQ[:, t * NE:(t + 1) * NE],
                                                    brb[:], ALU.add)
                        ins.then_inc(lg_s, 1)
                    if cur:
                        qk_lo_(u)
                    if prev:
                        norm(u)
                    if prev and u >= 3 and u % 2:
                        ctx_lo((u - 3) // 2)
                    if cur and u == 4 and not last(b):
                        wait(dve, r_mm, b - 1)
                        ln2(b + 1)
                if prev:
                    ctx_lo(KD - 1)
                if cur and not last(b):
                    split_xn(b + 1)
                if prev:
                    for t in range(TT):
                        dve.wait_ge(o_mm, 2 * (b - 1) + t + 1)
                        dve.wait_ge(xb_s, 2 * b)
                        dve.tensor_tensor(xres[:, t, :], psQ[:], xres[:, t, :], ALU.add).then_inc(x2_s, 1)

                    def free():
                        wait(dve, r_tp, b - 1)
                        wait(dve, xn3_st, 16 * (b - 1))

                    ch = layernorm(b - 1, xres, lambda: dve.wait_ge(x2_s, 2 * b), st3, mv3, ve3, rs3, rstd3, xn3, None, ln3)
                    normalize(ch, b - 1, xres, mv3, rs3, rstd3, xn3, free)

            run(body, dve)


CAPACITY = 1.2


def routing_phase(nc, lg, list_d, y, xn3_d, n_tok, NE):
    T = n_tok // P
    cap = -(-int(CAPACITY * 10) * n_tok // (10 * NE))
    R = next(r for r in range(P, 0, -1) if cap % r == 0)
    NG = NE * cap // R
    W = T * NE
    BITS = 30
    BIG = 1.0e5
    with ExitStack() as ctx:
        def sb(name, shape, dt=F32):
            return ctx.enter_context(nc.sbuf_tensor("c_" + name, shape, dt))

        def sem(name):
            return ctx.enter_context(nc.semaphore("c_" + name))

        te = [P, T, NE]
        ex, pb, eq, tmp, sel1, sel2, p2 = (sb(n, te) for n in ("ex", "pb", "eq", "tmp", "sel1", "sel2", "p2"))
        m, s, r, g1, g2, i1 = (sb(n, [P, T]) for n in ("m", "s", "r", "g1", "g2", "i1"))
        gate = sb("gate", [P, NE, T])
        ge, gt, tie, sel, pos, cum, slot = (sb(n, [P, NE, T]) for n in ("ge", "gt", "tie", "sel", "pos", "cum", "slot"))
        ione, iof = sb("ione", [P, NE], I32), sb("iof", [P, NE])
        tok, pay = sb("tok", [P, T], I32), sb("pay", [P, T, 2, 2])
        idx = sb("idx", [P, T, 2], I32)
        sl = sb("sl", [P, 2, T])
        thr, cand, bit, keep = (sb(n, [P, NE], I32) for n in ("thr", "cand", "bit", "keep"))
        cnt, need, base = sb("cnt", [P, NE]), sb("need", [P, NE]), sb("base", [P, NE])
        ones, below = sb("ones", [P, P]), sb("below", [P, P])
        one_w = sb("one_w", [P, W])
        fill, fill_id = sb("fill", [P, NG, 2]), sb("fill_id", [P, NG], I32)
        zero = sb("zero", [P, D])
        psC = ctx.enter_context(nc.psum_tensor("c_psC", [P, NE], F32))
        psA = ctx.enter_context(nc.psum_tensor("c_psA", [P, NE, T], F32))
        psB = ctx.enter_context(nc.psum_tensor("c_psB", [P, NE, T], F32))

        made, made_v, zero_st, fill_st = sem("made"), sem("made_v"), sem("zero_st"), sem("fill_st")
        ch_s, exp_s, cnt_s, sum_s, bit_s = sem("ch"), sem("exp"), sem("cnt"), sem("sum"), sem("bit")
        pre_s, mm_s, pay_s, sc_s = sem("pre"), sem("mm"), sem("pay"), sem("sc")
        passed = sem("passed")

        block = ctx.enter_context(nc.Block())

        @block.gpsimd
        def _(pool):
            g = nc.gpsimd
            g.iota(ione[:], [[1, NE]], base=0, channel_multiplier=0).then_inc(made, 1)
            g.iota(tok[:], [[P, T]], base=0, channel_multiplier=1).then_inc(made, 1)
            g.iota(fill_id[:], [[0, NG]], base=n_tok, channel_multiplier=1).then_inc(made, 1)
            g.memset(ones[:], 1.0).then_inc(made, 1)
            g.memset(below[:], 1.0).then_inc(made, 1)
            g.memset(zero[:], 0.0).then_inc(made, 1)
            g.memset(fill[:], 0.0).then_inc(made, 1)
            pool.wait_ge(made, 7)
            g.affine_select(out=below[:], in_=below[:], compare_op=ALU.is_gt, fill=0.0, base=0,
                            pattern=[[1, P]], channel_multiplier=-1).then_inc(made, 1)
            pool.wait_ge(pay_s, 1)
            pool.wait_ge(fill_st, 16)
            for t in range(T):
                for kk in range(2):
                    g.indirect_dma_start(out=list_d, out_offset=bass.IndirectOffsetOnAxis(ap=idx[:, t, kk:kk + 1], axis=0),
                                         in_=pay[:, t, kk, :], in_offset=None, bounds_check=NE * cap - 1,
                                         oob_is_err=False).then_inc(sc_s, 16)
            pool.wait_ge(sc_s, 16 * 2 * T)

        @block.sync
        def _(sp):
            sp.wait_ge(made, 8)
            sp.dma_start(y[n_tok:n_tok + P, :], zero[:]).then_inc(zero_st, 16)
            sp.dma_start(xn3_d[n_tok:n_tok + P, :], zero[:]).then_inc(zero_st, 16)
            sp.wait_ge(made_v, 1)
            with nc.allow_non_contiguous_dma(reason="the lists' rows"):
                sp.dma_start(list_d.rearrange("(g r) c -> r g c", r=R), fill[0:R]).then_inc(fill_st, 16)
            sp.wait_ge(zero_st, 32)

        @block.scalar
        def _(act):
            act.wait_ge(ch_s, 2)
            act.activation(ex[:], ex[:], ACT.Exp).then_inc(exp_s, 1)

        @block.tensor
        def _(pe):
            pe.wait_ge(made, 8)
            with pe.Fori(0, BITS) as i:
                pe.wait_ge(cnt_s, i + 1)
                pe.matmul(psC[:], ones[:], cnt[:], start=True, stop=True).then_inc(sum_s, 1)
            pe.wait_ge(cnt_s, BITS + 1)
            pe.matmul(psC[:], ones[:], cnt[:], start=True, stop=True).then_inc(sum_s, 1)
            for j, src in enumerate((tie, sel)):
                pe.wait_ge(pre_s, j + 1)
                pe.matmul(psA[:].rearrange("p e t -> p (e t)"), below[:], src[:].rearrange("p e t -> p (e t)"), start=True, stop=True)
                pe.matmul(psB[:].rearrange("p e t -> p (e t)"), ones[:], src[:].rearrange("p e t -> p (e t)"),
                          start=True, stop=True).then_inc(mm_s, 1)

        @block.vector
        def _(dve):
            n = [0]

            def did(ins):
                ins.then_inc(ch_s, 1)
                n[0] += 1
                dve.wait_ge(ch_s, n[0])

            def over_e(ap):
                return ap.rearrange("p (t o) -> p t o", o=1).broadcast_to(te)

            def over_t(ap):
                return ap.rearrange("p (e o) -> p e o", o=1).broadcast_to([P, NE, T])

            lgv = lg[:].rearrange("p (t e) -> p t e", e=NE)
            dve.memset(one_w[:], 1.0)
            dve.memset(thr[:], 0)
            dve.memset(bit[:], 1 << (BITS - 1))
            dve.wait_ge(made, 8)
            dve.tensor_copy(fill[:, :, 0].bitcast(I32), fill_id[:]).then_inc(made_v, 1)
            did(dve.tensor_reduce(m[:], lgv, AX.X, ALU.max))
            did(dve.tensor_tensor(ex[:], lgv, over_e(m[:]), ALU.subtract))
            did(dve.tensor_copy(iof[:], ione[:]))
            dve.wait_ge(exp_s, 1)
            did(dve.tensor_reduce(s[:], ex[:], AX.X, ALU.add))
            did(dve.reciprocal(r[:], s[:]))
            did(dve.tensor_tensor(pb[:], ex[:], over_e(r[:]), ALU.mult))

            def top(p, g, sl_):
                did(dve.tensor_reduce(g[:], p[:], AX.X, ALU.max))
                did(dve.tensor_tensor(eq[:], p[:], over_e(g[:]), ALU.is_equal))
                io = iof[:].rearrange("p (o e) -> p o e", o=1).broadcast_to(te)
                did(dve.scalar_tensor_tensor(out=tmp[:], in0=eq[:], scalar=-float(NE), in1=io, op0=ALU.mult, op1=ALU.add))
                did(dve.tensor_reduce(i1[:], tmp[:], AX.X, ALU.min))
                did(dve.tensor_tensor(sl_[:], tmp[:], over_e(i1[:]), ALU.is_equal))

            top(pb, g1, sel1)
            did(dve.scalar_tensor_tensor(out=p2[:], in0=sel1[:], scalar=-2.0, in1=pb[:], op0=ALU.mult, op1=ALU.add))
            top(p2, g2, sel2)
            did(dve.tensor_tensor(tmp[:], sel1[:], sel2[:], ALU.add))
            did(dve.tensor_tensor(gate[:].rearrange("p e t -> p t e"), pb[:], tmp[:], ALU.mult))
            with dve.Fori(0, BITS) as i:
                dve.tensor_tensor(cand[:], thr[:], bit[:], ALU.bitwise_or).then_inc(bit_s, 1)
                dve.wait_ge(bit_s, i * 5 + 1)
                dve.tensor_tensor(ge[:], gate[:], over_t(cand[:].bitcast(F32)), ALU.is_ge).then_inc(bit_s, 1)
                dve.tensor_scalar(bit[:], bit[:], 1, None, ALU.logical_shift_right).then_inc(bit_s, 1)
                dve.wait_ge(bit_s, i * 5 + 3)
                dve.tensor_reduce(cnt[:], ge[:], AX.X, ALU.add).then_inc(cnt_s, 1)
                dve.wait_ge(sum_s, i + 1)
                dve.tensor_scalar(keep[:], psC[:], float(cap), None, ALU.is_ge).then_inc(bit_s, 1)
                dve.wait_ge(bit_s, i * 5 + 4)
                dve.sem_inc(passed, 1)
                dve.copy_predicated(thr[:], keep[:], cand[:]).then_inc(bit_s, 1)
                dve.wait_ge(bit_s, i * 5 + 5)
            th = over_t(thr[:].bitcast(F32))
            did(dve.tensor_tensor(gt[:], gate[:], th, ALU.is_gt))
            dve.tensor_reduce(cnt[:], gt[:], AX.X, ALU.add).then_inc(cnt_s, 1)
            did(dve.tensor_tensor(tie[:], gate[:], th, ALU.is_equal))
            did(dve.tensor_scalar(ge[:], gate[:], 0.0, None, ALU.is_gt))
            did(dve.tensor_tensor(tie[:], tie[:], ge[:], ALU.mult))
            dve.sem_inc(pre_s, 1)
            dve.wait_ge(sum_s, BITS + 1)
            did(dve.tensor_scalar(need[:], psC[:], -1.0, float(cap), ALU.mult, ALU.add))

            def place(j):
                dve.wait_ge(mm_s, j + 1)
                did(dve.tensor_copy(cum[:], psB[:]))
                did(dve.tensor_tensor_scan(pos[:].rearrange("p e t -> p (e t)"), one_w[:], cum[:].rearrange("p e t -> p (e t)"),
                                           0.0, ALU.mult, ALU.add))
                did(dve.tensor_tensor(cum[:], pos[:], cum[:], ALU.subtract))
                did(dve.tensor_copy(base[:], cum[:, :, 0]))
                did(dve.tensor_tensor(cum[:], cum[:], over_t(base[:]), ALU.subtract))
                did(dve.tensor_tensor(pos[:], cum[:], psA[:], ALU.add))

            place(0)
            did(dve.tensor_tensor(ge[:], pos[:], over_t(need[:]), ALU.is_lt))
            did(dve.tensor_tensor(tie[:], tie[:], ge[:], ALU.mult))
            did(dve.tensor_tensor(sel[:], gt[:], tie[:], ALU.add))
            dve.sem_inc(pre_s, 1)
            place(1)
            did(dve.tensor_scalar(base[:], iof[:], float(cap), -BIG, ALU.mult, ALU.add))
            did(dve.tensor_tensor(pos[:], pos[:], over_t(base[:]), ALU.add))
            did(dve.tensor_tensor(slot[:], pos[:], sel[:], ALU.mult))
            slot_te = slot[:].rearrange("p e t -> p t e")
            for kk, (sl_, g) in enumerate(((sel1, g1), (sel2, g2))):
                did(dve.tensor_tensor(tmp[:], sl_[:], slot_te, ALU.mult))
                did(dve.tensor_reduce(sl[:, kk, :], tmp[:], AX.X, ALU.add))
                did(dve.tensor_scalar(idx[:, :, kk], sl[:, kk, :], BIG, None, ALU.add))
                did(dve.tensor_copy(pay[:, :, kk, 0].bitcast(I32), tok[:]))
                did(dve.tensor_copy(pay[:, :, kk, 1], g[:]))
            dve.sem_inc(pay_s, 1)


def ffn_phase(nc, xn3_d, y, list_d, W1, b1, W2, b2, out, n_tok):
    NE, _, H = W1.shape
    cap = -(-int(CAPACITY * 10) * n_tok // (10 * NE))
    R = next(r for r in range(P, 0, -1) if cap % r == 0)
    NT = cap // R
    HALF = (cap + 1) // 2 + (cap + 1) // 2 % 2
    CW = 2 * HALF
    MH = H // P
    CH = 4
    MC = MH // CH
    assert cap % R == 0 and CW >= cap and HALF <= 512
    with ExitStack() as ctx:
        def sb(name, shape, dt=F32):
            return ctx.enter_context(nc.sbuf_tensor("d_" + name, shape, dt))

        def sem(name):
            return ctx.enter_context(nc.semaphore("d_" + name))

        ident = sb("ident", [P, P])
        lst = sb("lst", [R, NE * NT, 2])
        ids = [sb(f"ids{i}", [R, NT], I32) for i in range(2)]
        gts = [sb(f"gts{i}", [R, NT]) for i in range(2)]
        xg = sb("xg", [R, NT, D])
        xgT_h, xgT_l = ([sb(f"xgT_{a}{i}", [P, KD, CW], F32R) for i in range(2)] for a in "hl")
        w1, w2 = ([sb(f"w{a}_{i}", [P, MC, P * MC]) for i in range(2)] for a in (1, 2))
        w1_h, w1_l, w2_h, w2_l = ([sb(f"{a}{i}", [P, MC, P * MC], F32R) for i in range(2)] for a in ("w1_h", "w1_l", "w2_h", "w2_l"))
        hf = sb("hf", [P, 2, CW])
        h_h, h_l = sb("h_h", [P, 2, CW], F32R), sb("h_l", [P, 2, CW], F32R)
        b1c = [sb(f"b1c{i}", [P, MH]) for i in range(2)]
        b2r = [sb(f"b2r{i}", [R, D]) for i in range(2)]
        ob = sb("ob", [R, NT, D])
        psH = [ctx.enter_context(nc.psum_tensor(f"d_psH{i}", [P, 512], F32)) for i in range(2)]
        psO = [ctx.enter_context(nc.psum_tensor(f"d_psO{i}", [P, 512], F32)) for i in range(NT)]
        psT = ctx.enter_context(nc.psum_tensor("d_psT", [P, KD, P], F32))

        setup, lst_ld, ids_s = sem("setup"), sem("lst_ld"), sem("ids")
        b_ld, w1_ld, w2_ld = ([sem(f"{a}_ld{i}") for i in range(2)] for a in ("b", "w1", "w2"))
        g_ld, g_tp, g_hi, g_lo = sem("g_ld"), sem("g_tp"), sem("g_hi"), sem("g_lo")
        w1_hi, w1_lo, w2_hi, w2_lo = sem("w1_hi"), sem("w1_lo"), sem("w2_hi"), sem("w2_lo")
        h_mm, silu_s, h_hi, h_lo, o_mm = sem("h_mm"), sem("silu"), sem("h_hi"), sem("h_lo"), sem("o_mm")
        ob_s, og_s, sc, out_st = sem("ob"), sem("og"), sem("sc"), sem("out_st")
        passed_p, passed_s = sem("passed_p"), sem("passed_s")

        w1_v = W1.rearrange("e (k p) h -> e p k h", p=P)
        w2_v = W2.rearrange("e (m p) d -> e p m d", p=P)
        b1_v = b1.rearrange("e (m p) -> e p m", p=P)

        def run(body, eng):
            body(0, 0, 0)
            with eng.Fori(0, NE // 2 - 1) as i:
                body(i * 2 + 1, i, 1)
                body(i * 2 + 2, i + 1, 0)
            body(NE - 1, NE // 2 - 1, 1)

        def last(e):
            return isinstance(e, int) and e == NE - 1

        block = ctx.enter_context(nc.Block())

        @block.sync
        def _(sp):
            with nc.allow_non_contiguous_dma(reason="the lists' rows"):
                sp.dma_start(lst[:], list_d.rearrange("(g r) c -> r g c", r=R)).then_inc(lst_ld, 16)

            def body(e, k, par):
                for c in range(CH):
                    if c == 0:
                        wait(sp, silu_s, 2 * MH * (e - 1))
                        sp.sem_inc(passed_s, 1)
                        wait(sp, ob_s, NT * (e - 1))
                        sp.sem_inc(passed_s, 1)
                        with nc.allow_non_contiguous_dma(reason="small parameters"):
                            sp.dma_start(b1c[par][:], b1_v[e]).then_inc(b_ld[par], 16)
                        sp.dma_start(b2r[par][:], b2[bass.ds(e, 1), :].broadcast_to([R, D])).then_inc(b_ld[par], 16)
                    s_ = c % 2
                    cols = slice(c * MC * P, (c + 1) * MC * P)
                    wait(sp, w1_hi, CH * e + c - 1)
                    wait(sp, w1_lo, CH * e + c - 1)
                    sp.sem_inc(passed_s, 1)
                    sp.dma_start(w1[s_][:], w1_v[e, :, :, cols]).then_inc(w1_ld[s_], 16)
                    wait(sp, w2_hi, CH * e + c - 1)
                    wait(sp, w2_lo, CH * e + c - 1)
                    sp.sem_inc(passed_s, 1)
                    sp.dma_start(w2[s_][:], w2_v[e, :, c * MC:(c + 1) * MC, :]).then_inc(w2_ld[s_], 16)

            run(body, sp)
            sp.wait_ge(sc, 16 * NT * NE)
            sp.sem_inc(passed_s, 1)
            sp.dma_start(out.rearrange("b s d -> (b s) d"), y[0:n_tok, :]).then_inc(out_st, 16)
            sp.wait_ge(out_st, 16)

        @block.gpsimd
        def _(pool):
            g = nc.gpsimd
            g.memset(ident[:], 0.0).then_inc(setup, 1)
            for i in range(2):
                g.memset(f32(xgT_h[i][:, :, cap:CW]), 0.0).then_inc(setup, 1)
                g.memset(f32(xgT_l[i][:, :, cap:CW]), 0.0).then_inc(setup, 1)
            pool.wait_ge(setup, 5)
            g.affine_select(out=ident[:], in_=ident[:], compare_op=ALU.not_equal, fill=1.0, base=0,
                            pattern=[[-1, P]], channel_multiplier=1).then_inc(setup, 1)

            def gather(e, par):
                pool.wait_ge(ids_s, 2 * e + 2)
                wait(pool, g_tp, NT * e)
                g.sem_inc(passed_p, 1)
                for t in range(NT):
                    g.indirect_dma_start(out=xg[:, t, :], out_offset=None, in_=xn3_d,
                                         in_offset=bass.IndirectOffsetOnAxis(ap=ids[par][:, t:t + 1], axis=0),
                                         bounds_check=n_tok + P - 1, oob_is_err=True).then_inc(g_ld, 16)

            gather(0, 0)

            def body(e, k, par):
                if not last(e):
                    gather(e + 1, 1 - par)
                wait(pool, sc, 16 * NT * e)
                g.sem_inc(passed_p, 1)
                for t in range(NT):
                    pool.wait_ge(og_s, NT * e + t + 1)
                    g.sem_inc(passed_p, 1)
                    g.indirect_dma_start(out=y, out_offset=bass.IndirectOffsetOnAxis(ap=ids[par][:, t:t + 1], axis=0),
                                         in_=ob[:, t, :], in_offset=None, bounds_check=n_tok + P - 1, oob_is_err=True,
                                         compute_op=ALU.add).then_inc(sc, 16)

            run(body, pool)

        @block.tensor
        def _(pe):
            def split_mm(out, hi_w, lo_w, hi_x, lo_x, first, last_):
                pe.matmul(out, lo_w, hi_x, start=first, stop=False)
                pe.matmul(out, hi_w, lo_x, start=False, stop=False)
                return pe.matmul(out, hi_w, hi_x, start=False, stop=last_)

            def turn(e, t):
                if t == 0:
                    pe.wait_ge(g_ld, 16 * NT * (e + 1))
                wait(pe, g_lo, NT * e + t)
                for kk in range(KD):
                    mm = pe.transpose(psT[:, kk, 0:R], xg[:, t, kk * P:(kk + 1) * P], ident[0:R, 0:R])
                mm.then_inc(g_tp, 1)

            pe.wait_ge(setup, 6)
            for t in range(NT):
                turn(0, t)

            def body(e, k, par):
                pe.wait_ge(g_lo, NT * (e + 1))

                def outer(m):
                    c, s_ = m // MC, (m // MC) % 2
                    pe.wait_ge(h_lo, MH * e + m + 1)
                    pe.wait_ge(w2_lo, CH * e + c + 1)
                    for t in range(NT):
                        if m == 0:
                            wait(pe, ob_s, NT * (e - 1) + t + 1)
                        cc = slice(t * R, (t + 1) * R)
                        mm = split_mm(psO[t][0:R, :], h_h[:, m % 2, cc], h_l[:, m % 2, cc], w2_h[s_][:, m % MC, :],
                                      w2_l[s_][:, m % MC, :], m == 0, m == MH - 1)
                        if m == MH - 1:
                            mm.then_inc(o_mm, 1)
                    if m < MH - 1 :
                        mm.then_inc(o_mm, 1)

                for m in range(MH):
                    c, s_ = m // MC, (m // MC) % 2
                    pe.wait_ge(w1_lo, CH * e + c + 1)
                    for n in range(2):
                        wait(pe, silu_s, 2 * (MH * e + m - 1) + n + 1)
                        for kk in range(KD):
                            cc = slice((m % MC) * P, (m % MC + 1) * P)
                            mm = split_mm(psH[n][:, 0:HALF], w1_h[s_][:, kk, cc], w1_l[s_][:, kk, cc],
                                          xgT_h[par][:, kk, n * HALF:(n + 1) * HALF], xgT_l[par][:, kk, n * HALF:(n + 1) * HALF],
                                          kk == 0, kk == KD - 1)
                        mm.then_inc(h_mm, 1)
                    if m:
                        outer(m - 1)
                    if m >= 5 and (m - 5) % 2 == 0 and (m - 5) // 2 < NT and not last(e):
                        turn(e + 1, (m - 5) // 2)
                outer(MH - 1)

            run(body, pe)

        OM = MH - 1 + NT

        @block.scalar
        def _(act):
            def copy(out, in_, done):
                act.activation(out, in_, ACT.Copy).then_inc(done, 1)

            def rows_hi(e, par, t):
                act.wait_ge(g_tp, NT * e + t + 1)
                copy(xgT_h[par][:, :, t * R:(t + 1) * R], psT[:, :, 0:R], g_hi)

            def w_parts(e, k, c):
                s_ = c % 2
                act.wait_ge(w1_ld[s_], 32 * e + 16 * (c // 2) + 16)
                wait(act, h_mm, 2 * (MH * e + MC * (c - 1)))
                copy(w1_h[s_][:], w1[s_][:], w1_hi)
                act.wait_ge(w2_ld[s_], 32 * e + 16 * (c // 2) + 16)
                if c >= 2:
                    act.wait_ge(o_mm, OM * e + MC * (c - 1))
                elif c == 1:
                    wait(act, o_mm, OM * e)
                else:
                    wait(act, o_mm, OM * (e - 1) + MC * (CH - 1))
                copy(w2_h[s_][:], w2[s_][:], w2_hi)

            for t in range(NT):
                rows_hi(0, 0, t)
            w_parts(0, 0, 0)

            def body(e, k, par):
                act.wait_ge(b_ld[par], 32 * k + 32)
                for m in range(MH):
                    for n in range(2):
                        act.wait_ge(h_mm, 2 * (MH * e + m) + n + 1)
                        wait(act, h_lo, MH * e + m - 1)
                        act.activation(hf[:, m % 2, n * HALF:(n + 1) * HALF], psH[n][:, 0:HALF], ACT.Silu,
                                       bias=b1c[par][:, m:m + 1]).then_inc(silu_s, 1)
                    act.wait_ge(silu_s, 2 * (MH * e + m + 1))
                    if m >= 2:
                        act.wait_ge(o_mm, OM * e + m - 1)
                    else:
                        wait(act, o_mm, OM * e)
                    copy(h_h[:, m % 2, :], hf[:, m % 2, :], h_hi)
                    if m >= 5 and (m - 5) % 2 == 0 and (m - 5) // 2 < NT and not last(e):
                        rows_hi(e + 1, 1 - par, (m - 5) // 2)
                    if m % MC == 1 and m // MC + 1 < CH:
                        w_parts(e, k, m // MC + 1)
                    if m == MH - 2 and not last(e):
                        w_parts(e + 1, k, 0)
                for t in range(NT):
                    act.wait_ge(ob_s, NT * e + t + 1)
                    act.activation(ob[:, t, :], ob[:, t, :], ACT.Copy, scale=gts[par][:, t:t + 1]).then_inc(og_s, 1)

            run(body, act)

        @block.vector
        def _(dve):
            def minus(out, a, b_, done):
                dve.tensor_tensor(out, a, b_, ALU.subtract).then_inc(done, 1)

            def rows_lo(e, par, t):
                dve.wait_ge(g_hi, NT * e + t + 1)
                c = slice(t * R, (t + 1) * R)
                minus(xgT_l[par][:, :, c], psT[:, :, 0:R], f32(xgT_h[par][:, :, c]), g_lo)

            def w_parts(e, c):
                s_ = c % 2
                dve.wait_ge(w1_hi, CH * e + c + 1)
                minus(w1_l[s_][:], w1[s_][:], f32(w1_h[s_][:]), w1_lo)
                dve.wait_ge(w2_hi, CH * e + c + 1)
                minus(w2_l[s_][:], w2[s_][:], f32(w2_h[s_][:]), w2_lo)

            def lists(e, par):
                wait(dve, sc, 16 * NT * (e - 1))
                wait(dve, og_s, NT * (e - 1))
                at = bass.ds(e * NT, NT)
                dve.tensor_copy(ids[par][:], lst[:, at, 0].bitcast(I32)).then_inc(ids_s, 1)
                dve.tensor_copy(gts[par][:], lst[:, at, 1]).then_inc(ids_s, 1)

            dve.wait_ge(lst_ld, 16)
            lists(0, 0)
            for t in range(NT):
                rows_lo(0, 0, t)
            w_parts(0, 0)

            def body(e, k, par):
                for m in range(MH):
                    if m == 3 and not last(e):
                        lists(e + 1, 1 - par)
                    dve.wait_ge(h_hi, MH * e + m + 1)
                    minus(h_l[:, m % 2, :], hf[:, m % 2, :], f32(h_h[:, m % 2, :]), h_lo)
                    if m >= 5 and (m - 5) % 2 == 0 and (m - 5) // 2 < NT and not last(e):
                        rows_lo(e + 1, 1 - par, (m - 5) // 2)
                    if m % MC == 1 and m // MC + 1 < CH:
                        w_parts(e, m // MC + 1)
                    if m == MH - 2 and not last(e):
                        w_parts(e + 1, 0)
                for t in range(NT):
                    dve.wait_ge(o_mm, OM * e + MH - 1 + t + 1)
                    wait(dve, sc, 16 * NT * e)
                    dve.tensor_tensor(ob[:, t, :], psO[t][0:R, :], b2r[par][:], ALU.add).then_inc(ob_s, 1)

            run(body, dve)


def block_kernel(nc, x, ctxT, W_inT, conv_w, conv_b, W_xprojT, A_log, D_param, W_outT,
                 WqT, bq, WkT, bk, WvT, bv, WoT, bo, Wr, br, W1, b1, W2, b2, out):
    B, S, _ = x.shape
    n_tok = B * S
    NE = Wr.shape[1]
    cap = -(-int(CAPACITY * 10) * n_tok // (10 * NE))

    def scratch(name, shape, dt=F32):
        return nc.dram_tensor(name, shape, dt, kind="Internal").ap()

    x1 = scratch("x1_d", (B, S, D))
    rows = scratch("rows_d", (3, B, S))
    qs, ks = scratch("qs_d", (2, D, S), F32R), scratch("ks_d", (2, D, S), F32R)
    y, xn3 = scratch("y_d", (n_tok + P, D)), scratch("xn3_d", (n_tok + P, D))
    lists = scratch("lists_d", (NE * cap, 2))
    mamba_phase(nc, x, W_inT, conv_w, conv_b, W_xprojT, A_log, D_param, W_outT, x1, rows)
    with nc.sbuf_tensor("lg", [P, n_tok // P * NE], F32) as lg:
        attention_phase(nc, x1, ctxT, WqT, bq, WkT, bk, WvT, bv, WoT, bo, Wr, br, y, xn3, lg, qs, ks)
        routing_phase(nc, lg, lists, y, xn3, n_tok, NE)
    ffn_phase(nc, xn3, y, lists, W1, b1, W2, b2, out, n_tok)


def kernel(x, ctx_1024, L0_attn_W_in, L0_attn_conv_w, L0_attn_conv_b, L0_attn_W_xproj, L0_attn_A_log, L0_attn_D_param,
           L0_attn_W_out, L0_xattn_Wq, L0_xattn_bq, L0_xattn_Wk, L0_xattn_bk, L0_xattn_Wv, L0_xattn_bv, L0_xattn_Wo,
           L0_xattn_bo, L0_ffn_Wr, L0_ffn_br, L0_ffn_W1, L0_ffn_b1, L0_ffn_W2, L0_ffn_b2):
    import numpy as _np
    import concourse.bacc as _bacc
    from concourse import mybir as _mybir
    from concourse.bass_utils import run_bass_kernel_spmd as _run

    ins = dict(x=x, ctxT=ctx_1024.transpose(0, 2, 1), W_inT=L0_attn_W_in.T, conv_w=L0_attn_conv_w, conv_b=L0_attn_conv_b,
               W_xprojT=L0_attn_W_xproj.T, A_log=L0_attn_A_log, D_param=L0_attn_D_param, W_outT=L0_attn_W_out.T,
               WqT=L0_xattn_Wq.T, bq=L0_xattn_bq, WkT=L0_xattn_Wk.T, bk=L0_xattn_bk, WvT=L0_xattn_Wv.T, bv=L0_xattn_bv,
               WoT=L0_xattn_Wo.T, bo=L0_xattn_bo, Wr=L0_ffn_Wr, br=L0_ffn_br, W1=L0_ffn_W1, b1=L0_ffn_b1, W2=L0_ffn_W2,
               b2=L0_ffn_b2)
    nc = _bacc.Bacc("TRN2", target_bir_lowering=False, num_devices=1)
    arrays, args = {}, []
    for name, a in ins.items():
        a = _np.ascontiguousarray(a)
        arrays[f"in_{name}_dram"] = a
        args.append(nc.dram_tensor(f"in_{name}_dram", a.shape, _mybir.dt.from_np(a.dtype), kind="ExternalInput").ap())
    args.append(nc.dram_tensor("out_0_dram", x.shape, _mybir.dt.float32, kind="ExternalOutput").ap())
    block_kernel(nc, *args)
    r = _run(nc, [arrays], core_ids=[0])
    return r.results[0]["out_0_dram"]
```

```python
from contextlib import ExitStack

import concourse.bass as bass
from concourse import mybir

F32 = mybir.dt.float32
F32R = mybir.dt.float32r
I32 = mybir.dt.int32
ALU = mybir.AluOpType
ACT = mybir.ActivationFunctionType
AX = mybir.AxisListType
RMAX = bass.bass_isa.ReduceOp.max

P = 128
D = 512
KD = D // P
EPS = 1e-5


def wait(eng, sem, value):
    if isinstance(value, int) and value <= 0:
        return
    eng.wait_ge(sem, value)


class Chain:

    def __init__(self, eng, sem, per, b):
        self.eng, self.sem, self.per, self.b, self.n = eng, sem, per, b, 0

    def did(self, instruction):
        instruction.then_inc(self.sem, 1)
        self.n += 1

    def wait(self):
        self.eng.wait_ge(self.sem, self.b * self.per + self.n)


def f32(ap):
    return ap.bitcast(F32)


def mamba_phase(nc, x, W_inT, conv_w, conv_b, W_xprojT, A_log, D_param, W_outT, x1, rows_dram):
    B, S, _ = x.shape
    E = conv_w.shape[0]
    KE = E // P
    N = 16
    TT = S // P
    BL = 32
    NB = S // BL
    HB = P // BL
    NI = NB + NB - HB
    CL = 8
    with ExitStack() as ctx:
        def sb(name, shape, dt=F32):
            return ctx.enter_context(nc.sbuf_tensor("a_" + name, shape, dt))

        def sem(name):
            return ctx.enter_context(nc.semaphore("a_" + name))

        win_h, win_l = sb("win_h", [P, KD, 2 * E], F32R), sb("win_l", [P, KD, 2 * E], F32R)
        wout_h, wout_l = sb("wout_h", [P, KE, D], F32R), sb("wout_l", [P, KE, D], F32R)
        wx_h, wx_l = sb("wx_h", [P, KE, P], F32R), sb("wx_l", [P, KE, P], F32R)
        wx_raw = sb("wx_raw", [P, KE, 33])
        cw, cb, dp = sb("cw", [P, KE, 4]), sb("cb", [P, KE]), sb("dp", [P, KE])
        a_neg, a_log = sb("a_neg", [N, 1]), sb("a_log", [N, 1])
        ident, mask, half = sb("ident", [P, P]), sb("mask", [P, S + P]), sb("half", [P, TT])
        ones_row = sb("ones_row", [N, S])
        xl = sb("xl", [P, TT, D])
        xres = sb("xres", [P, TT, D])
        xn = sb("xn", [P, TT, D])
        st, mv, ve, rs = sb("st", [P, TT, 6]), sb("mv", [P, TT, 2]), sb("ve", [P, TT]), sb("rs", [P, TT])
        xnT_h, xnT_l = sb("xnT_h", [P, KD, S], F32R), sb("xnT_l", [P, KD, S], F32R)
        v = sb("v", [P, 2, S])
        xc = [sb(f"xc{i}", [P, KE, S]) for i in range(2)]
        xcr_h, xcr_l = sb("xcr_h", [P, 3, S], F32R), sb("xcr_l", [P, 3, S], F32R)
        zs = sb("zs", [P, KE, S])
        XT_h, XT_l = sb("XT_h", [P, TT, E], F32R), sb("XT_l", [P, TT, E], F32R)
        MTf, MT_h, MT_l = sb("MTf", [P, S + P]), sb("MT_h", [P, S + P], F32R), sb("MT_l", [P, S + P], F32R)
        t1, y2 = sb("t1", [P, 2, S]), sb("y2", [P, 2, S])
        y2_h, y2_l = sb("y2_h", [P, 2, S], F32R), sb("y2_l", [P, 2, S], F32R)
        dt_r, l_r, Bb, Cr, ab, gb = (sb(n, [N, S]) for n in ("dt_r", "l_r", "Bb", "Cr", "ab", "gb"))
        abar = sb("abar", [N, S])
        lam = sb("lam", [N, S + 1])
        EB, EC = sb("EB", [N, NI, P]), sb("EC", [N, S])
        rng, scl = sb("rng", [N, NB]), sb("scl", [N, 2])
        fl, flr, fls = sb("fl", [P, 3]), sb("flr", [P, 3]), sb("fls", [P, 2])
        flg = [sb(f"flg{i}", [P, 1], I32) for i in range(2)]
        hst, hcb, abc, xch = sb("hst", [P, N]), sb("hcb", [P, CL, N]), sb("abc", [P, 3, N, CL]), sb("xch", [P, CL])
        bxs = sb("bxs", [P, N])

        psT = [ctx.enter_context(nc.psum_tensor(f"a_psT{i}", [P, 512], F32)) for i in range(2)]
        psP = [ctx.enter_context(nc.psum_tensor(f"a_psP{i}", [P, 512], F32)) for i in range(3)]
        psX = ctx.enter_context(nc.psum_tensor("a_psX", [P, 512], F32))
        psO = [ctx.enter_context(nc.psum_tensor(f"a_psO{i}", [P, 512], F32)) for i in range(2)]

        w_ld = sem("w_ld")
        stg = [sem(f"stg{i}") for i in range(2)]
        stg_h, stg_l = sem("stg_h"), sem("stg_l")
        setup_pool, setup_dve, setup_act = sem("setup_pool"), sem("setup_dve"), sem("setup_act")
        x_ld = sem("x_ld")
        xres_ld, x1_st = sem("xres_ld"), sem("x1_st")
        ln, rstd = sem("ln"), sem("rstd")
        xn_tp, xnT_hi, xnT_lo = sem("xn_tp"), sem("xnT_hi"), sem("xnT_lo")
        x_mm, z_mm, y_mm, o_mm, xd_mm = sem("x_mm"), sem("z_mm"), sem("y_mm"), sem("o_mm"), sem("xd_mm")
        v_rdy, conv, xc_rdy, xc_hi, xc_lo = sem("v_rdy"), sem("conv"), sem("xc_rdy"), sem("xc_hi"), sem("xc_lo")
        z_rdy = sem("z_rdy")
        xt_tp, xt_hi, xt_lo = sem("xt_tp"), sem("xt_hi"), sem("xt_lo")
        m_mm, mt_f, mt_hi, mt_lo = sem("m_mm"), sem("mt_f"), sem("mt_hi"), sem("mt_lo")
        t1_rdy, t1_ok, y2_rdy, y2_hi, y2_lo, res = (sem(n) for n in ("t1_rdy", "t1_ok", "y2_rdy", "y2_hi", "y2_lo", "res"))
        rows_a, rows_b, rows_c, rows_d = sem("rows_a"), sem("rows_b"), sem("rows_c"), sem("rows_d")
        exps_a, exps_b = sem("exps_a"), sem("exps_b")
        bnd = sem("bnd")
        flag, flag_c, fb_dma = sem("flag"), sem("flag_c"), sem("fb_dma")

        passed_v = sem("passed_v")
        fb_range = range(fb_dma.num, fb_dma.num + 1)

        x_v = x.rearrange("b (t p) d -> b p t d", p=P)
        x1_v = x1.rearrange("b (t p) d -> b p t d", p=P)
        win_v = W_inT.rearrange("(k p) n -> k p n", p=P)
        wout_v = W_outT.rearrange("(c k p) n -> c p k n", p=P, k=4)
        stage = [xc[i][:].rearrange("p a b -> p (a b)") for i in range(2)]
        chunks = [(win_h[:, k, :], win_l[:, k, :], win_v[k]) for k in range(KD)]
        chunks += [(wout_h[:, 4 * c:4 * c + 4, :].rearrange("p k n -> p (k n)"),
                    wout_l[:, 4 * c:4 * c + 4, :].rearrange("p k n -> p (k n)"), wout_v[c]) for c in range(KE // 4)]
        NCH = len(chunks)

        def run(body, eng, tail):
            body(0, 0, False, True)
            body(1, 1, True, True)
            with eng.Fori(0, B // 2 - 2) as i:
                body(i * 2 + 2, 0, True, True)
                body(i * 2 + 3, 1, True, True)
            body(B - 2, 0, True, True)
            body(B - 1, 1, True, True)
            body(B, 0, True, False)
            tail()

        block = ctx.enter_context(nc.Block())

        @block.sync
        def _(sp):
            sp.dma_start(xl[:], x_v[0]).then_inc(x_ld, 16)
            for c, (_, _, src) in enumerate(chunks):
                if c >= 2:
                    sp.wait_ge(stg_h, c - 1)
                    sp.wait_ge(stg_l, c - 1)
                dst = stage[c % 2] if c < KD else stage[c % 2].rearrange("p (k n) -> p k n", k=4)
                sp.dma_start(dst, src).then_inc(stg[c % 2], 16)
                if c == 0:
                    with nc.allow_non_contiguous_dma(reason="small parameters"):
                        sp.dma_start(wx_raw[:], W_xprojT.rearrange("(k p) n -> p k n", p=P)).then_inc(w_ld, 16)
                        sp.dma_start(cw[:], conv_w.rearrange("(k p) n -> p k n", p=P)).then_inc(w_ld, 16)
                        sp.dma_start(cb[:], conv_b.rearrange("(k p) -> p k", p=P)).then_inc(w_ld, 16)
                        sp.dma_start(dp[:], D_param.rearrange("(k p) -> p k", p=P)).then_inc(w_ld, 16)
                        sp.dma_start(a_log[:], A_log.rearrange("(k p) -> k p", p=1)).then_inc(w_ld, 16)

            def body(b, par, prev, cur):
                if cur and not (isinstance(b, int) and b == B - 1):
                    sp.wait_ge(ln, 7 * b + 7)
                    sp.dma_start(xl[:], x_v[b + 1]).then_inc(x_ld, 16)
                if prev:
                    wait(sp, x1_st, 16 * (b - 1))
                    sp.dma_start(xres[:], x_v[b - 1]).then_inc(xres_ld, 16)
                    sp.wait_ge(res, 2 * b)
                    sp.dma_start(x1_v[b - 1], xres[:]).then_inc(x1_st, 16)

            run(body, sp, lambda: sp.wait_ge(x1_st, 16 * B))

        @block.gpsimd
        def _(pool):
            g = nc.gpsimd
            g.memset(ident[:], 0.0).then_inc(setup_pool, 1)
            g.memset(mask[:], 1.0).then_inc(setup_pool, 1)
            g.memset(half[:], -0.5).then_inc(setup_pool, 1)
            g.memset(f32(wx_h[:]), 0.0).then_inc(setup_pool, 1)
            g.memset(f32(wx_l[:]), 0.0).then_inc(setup_pool, 1)
            pool.wait_ge(setup_pool, 5)
            g.affine_select(out=ident[:], in_=ident[:], compare_op=ALU.not_equal, fill=1.0, base=0,
                            pattern=[[-1, P]], channel_multiplier=1).then_inc(setup_pool, 1)
            g.affine_select(out=mask[:, 0:S], in_=mask[:, 0:S], compare_op=ALU.is_ge, fill=0.0, base=0,
                            pattern=[[1, S]], channel_multiplier=-1).then_inc(setup_pool, 1)
            g.affine_select(out=mask[:, S:S + P], in_=mask[:, S:S + P], compare_op=ALU.is_ge, fill=0.0, base=0,
                            pattern=[[1, P]], channel_multiplier=-1).then_inc(setup_pool, 1)

            def rsqrt(b):
                pool.wait_ge(ln, 7 * b + 5)
                g.tensor_tensor(rs[:], ve[:], half[:], ALU.pow).then_inc(rstd, 1)

            def recurrence(b, par, d):
                o = 1 - par
                g.memset(hst[:], 0.0)
                with pool.Fori(0, S // CL) as c:
                    pool.drain()
                    with nc.allow_non_contiguous_dma(reason="rows to all partitions"):
                        for r in range(3):
                            src = rows_dram[r].rearrange("(o n) t -> o n t", o=1)[:, :, bass.ds(c * CL, CL)].broadcast_to([P, N, CL])
                            pool.dma_start(abc[:, r], src).then_inc(fb_dma, 16)
                    pool.wait_ge(fb_dma, 48)
                    pool.dma_reset(fb_range)
                    pool.sem_clear(fb_dma)
                    g.tensor_copy(xch[:], xc[o][:, d, bass.ds(c * CL, CL)])
                    for t in range(CL):
                        pool.drain()
                        g.tensor_tensor(hst[:], hst[:], abc[:, 0, :, t], ALU.mult)
                        g.tensor_tensor(bxs[:], abc[:, 1, :, t], xch[:, t:t + 1].broadcast_to([P, N]), ALU.mult)
                        pool.drain()
                        g.tensor_tensor(hst[:], hst[:], bxs[:], ALU.add)
                        pool.drain()
                        g.tensor_scalar(hst[:], hst[:], 100.0, -100.0, ALU.min, ALU.max)
                        pool.drain()
                        g.tensor_tensor(hcb[:, t], hst[:], abc[:, 2, :, t], ALU.mult)
                    w = N
                    while w > 1:
                        w //= 2
                        pool.drain()
                        g.tensor_tensor(hcb[:, :, 0:w], hcb[:, :, 0:w], hcb[:, :, w:2 * w], ALU.add)
                    pool.drain()
                    g.tensor_tensor(t1[:, d % 2, bass.ds(c * CL, CL)], hcb[:, :, 0],
                                    zs[:, d, bass.ds(c * CL, CL)], ALU.mult)
                pool.drain()

            rsqrt(0)

            def body(b, par, prev, cur):
                if prev:
                    beyond = pool.value_load(flg[1 - par][0:1, 0:1])
                for d in range(KE):
                    if prev:
                        pool.wait_ge(t1_rdy, 8 * (b - 1) + d + 1)
                        pool.sem_inc(flag_c, 1)
                        with pool.If(beyond > 999):
                            recurrence(b, par, d)
                        pool.sem_inc(t1_ok, 1)
                    if d == 5 and cur and not (isinstance(b, int) and b == B - 1):
                        rsqrt(b + 1)
                if cur:
                    pool.wait_ge(flag, b + 1)
                    pool.sem_inc(flag_c, 1)
                    g.partition_all_reduce(flr[:], fl[:], P, RMAX)
                    pool.drain()
                    g.tensor_tensor(fls[:, 0:1], flr[:, 0:1], flr[:, 1:2], ALU.mult)
                    pool.drain()
                    g.tensor_scalar(fls[:, 1:2], fls[:, 0:1], flr[:, 2:3], 1000.0, ALU.max, ALU.mult)
                    pool.drain()
                    g.tensor_scalar(flg[par][:], fls[:, 1:2], 1.0e6, None, ALU.min)
                    pool.drain()
                    again = pool.value_load(flg[par][0:1, 0:1])
                    with pool.If(again > 999):
                        for r, row in enumerate((abar, Bb, Cr)):
                            pool.dma_start(rows_dram[r], row[:]).then_inc(fb_dma, 16)
                        pool.wait_ge(fb_dma, 48)
                        pool.dma_reset(fb_range)
                        pool.sem_clear(fb_dma)
                    pool.sem_inc(rows_d, 1)

            run(body, pool, lambda: None)

        @block.tensor
        def _(pe):
            def split_mm(out, hi_w, lo_w, hi_x, lo_x, first, last):
                pe.matmul(out, lo_w, hi_x, start=first, stop=False)
                pe.matmul(out, hi_w, lo_x, start=False, stop=False)
                return pe.matmul(out, hi_w, hi_x, start=False, stop=last)

            pe.wait_ge(setup_pool, 8)
            pe.wait_ge(setup_dve, 1)

            def body(b, par, prev, cur):
                def bank(n):
                    d = (n - 8) // 2
                    if n < 3:
                        wait(pe, z_rdy, 8 * (b - 1) + min(n + 7, 8))
                    elif n < 8:
                        pe.wait_ge(conv, 24 * b + 3 * (n - 3) + 3)
                    elif n % 2 == 0:
                        if not cur:
                            pe.wait_ge(z_rdy if d < 3 else t1_rdy, 8 * b if d < 3 else 8 * (b - 1) + d - 2)
                        elif d < 2:
                            pe.wait_ge(conv, 24 * b + 3 * (n - 3) + 3)
                        else:
                            pe.wait_ge(z_rdy, 8 * b + d - 1)
                    elif not prev:
                        pe.wait_ge(conv if d < 3 else z_rdy, 24 * b + 24 if d < 3 else 8 * b + d - 2)
                    elif d < 1:
                        pe.wait_ge(conv, 24 * b + 3 * (n - 3) + 3)
                    else:
                        pe.wait_ge(t1_rdy, 8 * (b - 1) + d)
                    return psP[n % 3]

                def in_proj(n, m, done):
                    ps = bank(n)
                    for kk in range(KD):
                        if isinstance(b, int) and b == 0 and m == 0:
                            pe.wait_ge(stg_h, kk + 1)
                            pe.wait_ge(stg_l, kk + 1)
                        c = slice(m * P, m * P + P)
                        mm = split_mm(ps[:, 0:S], win_h[:, kk, c], win_l[:, kk, c], xnT_h[:, kk, :], xnT_l[:, kk, :],
                                      kk == 0, kk == KD - 1)
                    mm.then_inc(done, 1)

                def x_dbl(i):
                    pe.wait_ge(xc_lo, 8 * b + i + 1)
                    if i == 0:
                        wait(pe, mt_f, b)
                        if isinstance(b, int) and b == 0:
                            pe.wait_ge(setup_dve, 3)
                    split_mm(psX[:, 0:S], wx_h[:, i, :], wx_l[:, i, :], xcr_h[:, i % 3, :], xcr_l[:, i % 3, :],
                             i == 0, i == KE - 1).then_inc(xd_mm, 1)

                if cur:
                    pe.wait_ge(ln, 7 * b + 7)
                    for h in range(2):
                        wait(pe, xt_lo, 4 * (b - 1) + 3 + h)
                        for kk in range(2):
                            for t in range(TT):
                                mm = pe.transpose(psT[h][:, kk * S + t * P:kk * S + (t + 1) * P],
                                                  xn[:, t, (2 * h + kk) * P:(2 * h + kk + 1) * P], ident[:])
                        mm.then_inc(xn_tp, 1)
                if prev:
                    pe.wait_ge(rows_c, 2 * b)
                    for n in range(NI):
                        i = n if n < NB else n - NB + HB
                        c = i * BL if n < NB else S + (n - NB) * BL
                        mm = pe.matmul(psX[:, c:c + BL], EB[:, n, :], EC[:, i * BL:(i + 1) * BL], start=True, stop=True)
                    mm.then_inc(m_mm, 1)
                if cur:
                    pe.wait_ge(xnT_lo, 2 * b + 2)
                    for i in range(KE):
                        in_proj(i, i, x_mm)
                        if i >= 3:
                            x_dbl(i - 3)
                    x_dbl(KE - 3)
                if prev:
                    pe.wait_ge(mt_lo, b)
                    pe.wait_ge(xt_lo, 4 * b)

                def out_proj(d):
                    pe.wait_ge(y2_lo, 8 * (b - 1) + d + 1)
                    if d == 0:
                        wait(pe, res, 2 * (b - 1))
                    for t in range(TT):
                        c = slice(t * P, t * P + P)
                        mm = split_mm(psO[t][:], y2_h[:, d % 2, c], y2_l[:, d % 2, c], wout_h[:, d, :], wout_l[:, d, :],
                                      d == 0, d == KE - 1)
                    mm.then_inc(o_mm, 1)

                def turn_x(j):
                    pe.wait_ge(xc_rdy, 8 * b + 2 * j + 2)
                    if j < 2:
                        pe.wait_ge(xnT_lo, 2 * b + j + 1)
                    else:
                        pe.wait_ge(xt_lo, 4 * b + j - 1)
                    for t in range(TT):
                        for i in range(2):
                            mm = pe.transpose(psT[j % 2][:, (2 * t + i) * P:(2 * t + i + 1) * P],
                                              xc[par][:, 2 * j + i, t * P:(t + 1) * P], ident[:])
                    mm.then_inc(xt_tp, 1)

                for d in range(KE):
                    if cur and d == 1:
                        x_dbl(KE - 1)
                    if prev:
                        ps = bank(8 + 2 * d)
                        c = slice(d * P, d * P + P)
                        split_mm(ps[:, 0:S], XT_h[:, 0, c], XT_l[:, 0, c], MT_h[:, 0:S], MT_l[:, 0:S], True, False)
                        split_mm(ps[:, P:S], XT_h[:, 1, c], XT_l[:, 1, c], MT_h[:, S:], MT_l[:, S:], False, True).then_inc(y_mm, 1)
                    if cur and d == 0:
                        x_dbl(KE - 2)
                    if cur:
                        in_proj(9 + 2 * d, KE + d, z_mm)
                    if prev and d >= 2:
                        out_proj(d - 2)
                    if cur and d % 2:
                        turn_x(d // 2)
                if prev:
                    out_proj(KE - 2)
                    out_proj(KE - 1)

            run(body, pe, lambda: None)

        @block.scalar
        def _(act):
            def copy(out, in_, done):
                act.activation(out, in_, ACT.Copy).then_inc(done, 1)

            for c, (hi, _, _) in enumerate(chunks):
                act.wait_ge(stg[c % 2], 16 * (c // 2 + 1))
                copy(hi, stage[c % 2], stg_h)
            act.wait_ge(w_ld, 80)
            act.activation(a_neg[:], a_log[:], ACT.Exp).then_inc(setup_act, 1)
            act.wait_ge(stg_l, NCH)

            def body(b, par, prev, cur):
                def mt_hi_():
                    act.wait_ge(mt_f, b)
                    wait(act, y_mm, 8 * (b - 1))
                    copy(MT_h[:], MTf[:], mt_hi)

                if cur:
                    wait(act, z_mm, 8 * b)
                    for h in range(2):
                        act.wait_ge(xn_tp, 2 * b + h + 1)
                        copy(xnT_h[:, 2 * h:2 * h + 2, :], psT[h][:].rearrange("p (k s) -> p k s", k=2), xnT_hi)

                    def silu(i):
                        act.wait_ge(conv, 24 * b + 3 * i + 3)
                        if i == 0:
                            wait(act, y2_rdy, 8 * (b - 1))
                        act.activation(xc[par][:, i, :], v[:, i % 2, :], ACT.Silu).then_inc(xc_rdy, 1)
                        act.wait_ge(xc_rdy, 8 * b + i + 1)
                        wait(act, xd_mm, 8 * b + i - 2)
                        copy(xcr_h[:, i % 3, :], xc[par][:, i, :], xc_hi)

                    if prev:
                        mt_hi_()
                    for i in range(KE):
                        act.wait_ge(x_mm, 8 * b + i + 1)
                        wait(act, xc_rdy, 8 * b + i - 1)
                        act.activation(v[:, i % 2, :], psP[i % 3][:, 0:S], ACT.Identity,
                                       scale=cw[:, i, 3:4], bias=cb[:, i:i + 1]).then_inc(v_rdy, 1)
                        if i >= 1:
                            silu(i - 1)
                    silu(KE - 1)

                def y_hi(d):
                    act.wait_ge(y2_rdy, 8 * (b - 1) + d + 1)
                    wait(act, o_mm, 8 * (b - 1) + max(d - 1, 0))
                    copy(y2_h[:, d % 2, :], y2[:, d % 2, :], y2_hi)

                def xt_hi_(j):
                    act.wait_ge(xt_tp, 4 * b + j + 1)
                    copy(XT_h[:, :, 2 * j * P:(2 * j + 2) * P], psT[j % 2][:].rearrange("p (t s) -> p t s", t=TT), xt_hi)

                if prev and not cur:
                    mt_hi_()
                for d in range(KE):
                    if cur and d == 1:
                        act.wait_ge(rows_a, 3 * b + 3)
                        ch = Chain(act, exps_a, 2, b)
                        ch.did(act.activation(dt_r[:], dt_r[:], ACT.Exp))
                        ch.wait()
                        ch.did(act.activation(dt_r[:], dt_r[:], ACT.Ln, bias=1.0))
                    if cur and d == 5:
                        act.wait_ge(rows_b, 11 * b + 11)
                        act.activation(abar[:], l_r[:], ACT.Exp).then_inc(exps_b, 1)
                        act.activation(EB[:], EB[:], ACT.Exp, scale=-1.0).then_inc(exps_b, 1)
                        act.activation(EC[:], EC[:], ACT.Exp).then_inc(exps_b, 1)
                    if cur and d >= 2 and d % 2 == 0:
                        xt_hi_(d // 2 - 1)
                    if prev:
                        y_hi(d)
                    if cur:
                        act.wait_ge(z_mm, 8 * b + d + 1)
                        wait(act, t1_ok, 8 * (b - 1) + d + 1)
                        act.activation(zs[:, d, :], psP[(9 + 2 * d) % 3][:, 0:S], ACT.Silu).then_inc(z_rdy, 1)
                if cur:
                    xt_hi_(3)

            run(body, act, lambda: None)

        @block.vector
        def _(dve):
            def minus(out, a, b_, done):
                dve.tensor_tensor(out, a, b_, ALU.subtract).then_inc(done, 1)

            def moments(b):
                ch = Chain(dve, ln, 7, b)
                dve.wait_ge(x_ld, 16 * b + 16)
                for t in range(TT):
                    ch.did(dve.bn_stats(st[:, t, :], xl[:, t, :]))
                ch.wait()
                dve.sem_inc(passed_v, 1)
                for t in range(TT):
                    ch.did(dve.bn_aggr(mv[:, t, :], st[:, t, :]))
                ch.wait()
                ch.did(dve.tensor_scalar(ve[:], mv[:, :, 1], EPS, None, ALU.add))

            def normalize(b):
                wait(dve, xn_tp, 2 * b)
                dve.wait_ge(rstd, b + 1)
                for t in range(TT):
                    dve.tensor_scalar(xn[:, t, :], xl[:, t, :], mv[:, t, 0:1], rs[:, t:t + 1],
                                      ALU.subtract, ALU.mult).then_inc(ln, 1)

            dve.memset(ones_row[:], 1.0).then_inc(setup_dve, 1)
            dve.memset(lam[:, 0:1], 0.0).then_inc(setup_act, 1)
            dve.memset(fl[:], 0.0).then_inc(setup_act, 1)
            dve.memset(scl[:, 0:1], 0.01).then_inc(setup_act, 1)
            dve.memset(scl[:, 1:2], 1.0 / 60).then_inc(setup_act, 1)
            dve.wait_ge(setup_pool, 3)
            moments(0)
            normalize(0)
            for c, (hi, lo, _) in enumerate(chunks):
                dve.wait_ge(stg_h, c + 1)
                minus(lo, stage[c % 2], f32(hi), stg_l)
                if c == 0:
                    dve.wait_ge(w_ld, 80)
                    dve.wait_ge(setup_pool, 5)
                    cols = [(wx_raw[:, :, 0:N], slice(0, N)), (wx_raw[:, :, N:2 * N], slice(32, 32 + N)),
                            (wx_raw[:, :, 2 * N:2 * N + 1].broadcast_to([P, KE, N]), slice(64, 64 + N))]
                    for src, at in cols:
                        ins = dve.tensor_copy(wx_h[:, :, at], src)
                    ins.then_inc(setup_dve, 1)
                    dve.wait_ge(setup_dve, 2)
                    for src, at in cols:
                        ins = dve.tensor_tensor(wx_l[:, :, at], src, f32(wx_h[:, :, at]), ALU.subtract)
                    ins.then_inc(setup_dve, 1)
            dve.wait_ge(setup_act, 5)
            dve.tensor_scalar(a_neg[:], a_neg[:], -1.0, None, ALU.mult).then_inc(setup_dve, 1)

            def body(b, par, prev, cur):
                first = isinstance(b, int) and b == 0
                if cur:
                    for h in range(2):
                        dve.wait_ge(xnT_hi, 2 * b + h + 1)
                        minus(xnT_l[:, 2 * h:2 * h + 2, :], psT[h][:].rearrange("p (k s) -> p k s", k=2),
                              f32(xnT_h[:, 2 * h:2 * h + 2, :]), xnT_lo)
                if prev:
                    dve.wait_ge(m_mm, b)
                    wait(dve, mt_lo, b - 1)
                    dve.tensor_tensor(MTf[:], psX[:, 0:S + P], mask[:], ALU.mult).then_inc(mt_f, 1)
                    dve.wait_ge(mt_hi, b)
                    minus(MT_l[:], MTf[:], f32(MT_h[:]), mt_lo)
                    if not (isinstance(b, int) and b == 1):
                        add_res(b - 2)
                if cur:
                    def x_lo(i):
                        dve.wait_ge(xc_hi, 8 * b + i + 1)
                        minus(xcr_l[:, i % 3, :], xc[par][:, i, :], f32(xcr_h[:, i % 3, :]), xc_lo)

                    for i in range(KE):
                        dve.wait_ge(v_rdy, 8 * b + i + 1)
                        for j in range(1, 4):
                            dve.scalar_tensor_tensor(out=v[:, i % 2, j:S], in0=psP[i % 3][:, 0:S - j],
                                                     scalar=cw[:, i, 3 - j:4 - j], in1=v[:, i % 2, j:S],
                                                     op0=ALU.mult, op1=ALU.add).then_inc(conv, 1)
                            if j < 3:
                                dve.wait_ge(conv, 24 * b + 3 * i + j)
                        if i >= 1:
                            x_lo(i - 1)
                    x_lo(KE - 1)

                def rows_1():
                    dve.wait_ge(xd_mm, 8 * b + 8)
                    wait(dve, rows_d, b)
                    wait(dve, m_mm, b)
                    dve.tensor_scalar(dt_r[:], psX[64:64 + N, 0:S], 5.0, None, ALU.min).then_inc(rows_a, 1)
                    dve.tensor_copy(Bb[:], psX[0:N, 0:S]).then_inc(rows_a, 1)
                    dve.tensor_copy(Cr[:], psX[32:32 + N, 0:S]).then_inc(rows_a, 1)

                def rows_2(part):
                    ch = Chain(dve, rows_b, 11, b)
                    ref = lam[:, 0:S].rearrange("n (i t) -> n i t", t=BL)
                    ends = lam[:, 1:S + 1].rearrange("n (i t) -> n i t", t=BL)
                    if part == 0:
                        if first:
                            dve.wait_ge(setup_dve, 4)
                        dve.wait_ge(exps_a, 2 * b + 2)
                        dve.wait_ge(rows_a, 3 * b + 3)
                        ch.did(dve.tensor_scalar(dt_r[:], dt_r[:], 0.001, 0.1, ALU.max, ALU.min))
                        ch.wait()
                        ch.did(dve.tensor_scalar(l_r[:], dt_r[:], a_neg[:, 0:1], -20.0, ALU.mult, ALU.max))
                        ch.did(dve.tensor_tensor(Bb[:], Bb[:], dt_r[:], ALU.mult))
                        ch.wait()
                        ch.did(dve.tensor_tensor_scan(lam[:, 1:S + 1], ones_row[:], l_r[:], 0.0, ALU.mult, ALU.add))
                        ch.did(dve.tensor_scalar(Bb[:], Bb[:], -10.0, 10.0, ALU.max, ALU.min))
                    elif part == 1:
                        ch.n = 5
                        ch.wait()
                        ch.did(dve.tensor_tensor(EB[:, 0:NB, :], lam[:, 1:P + 1].rearrange("n (o t) -> n o t", o=1).broadcast_to([N, NB, P]),
                                                 ref[:, :, 0:1].broadcast_to([N, NB, P]), ALU.subtract))
                        ch.did(dve.tensor_tensor(EB[:, NB:, :], lam[:, P + 1:].rearrange("n (o t) -> n o t", o=1).broadcast_to([N, NI - NB, P]),
                                                 ref[:, HB:, 0:1].broadcast_to([N, NI - NB, P]), ALU.subtract))
                    else:
                        ch.n = 7
                        ch.did(dve.tensor_tensor(EC[:].rearrange("n (i t) -> n i t", t=BL), ends,
                                                 ref[:, :, 0:1].broadcast_to([N, NB, BL]), ALU.subtract))
                        ch.did(dve.tensor_tensor(rng[:], ref[:, :, 0], ends[:, :, BL - 1], ALU.subtract))
                        ch.did(dve.scalar_tensor_tensor(out=ab[:], in0=Bb[:], scalar=-1.0, in1=Bb[:], op0=ALU.mult, op1=ALU.max))
                        ch.wait()
                        ch.did(dve.tensor_scalar(EB[:], EB[:], -60.0, None, ALU.max))

                def rows_3():
                    dve.wait_ge(exps_b, 3 * b + 3)
                    bb = Bb[:].rearrange("n (o t) -> n o t", t=P)
                    dve.tensor_tensor(EB[:, 0:NB, :], EB[:, 0:NB, :], bb[:, 0:1, :].broadcast_to([N, NB, P]), ALU.mult)
                    dve.tensor_tensor(EB[:, NB:, :], EB[:, NB:, :], bb[:, 1:2, :].broadcast_to([N, NI - NB, P]),
                                      ALU.mult).then_inc(rows_c, 1)
                    dve.tensor_tensor(EC[:], EC[:], Cr[:], ALU.mult).then_inc(rows_c, 1)

                def bounds():
                    wait(dve, rows_d, b)
                    ch = Chain(dve, bnd, 4, b)
                    ch.did(dve.tensor_tensor_scan(gb[:], abar[:], ab[:], 0.0, ALU.mult, ALU.add))
                    ch.did(dve.tensor_reduce(fl[:, 0:1], xc[par][:].rearrange("p a b -> p (a b)"), AX.X, ALU.max,
                                             apply_absolute_value=True))
                    ch.did(dve.tensor_reduce(fl[0:N, 2:3], rng[:], AX.X, ALU.max))
                    ch.wait()
                    ch.did(dve.tensor_reduce(fl[0:N, 1:2], gb[:], AX.X, ALU.max))
                    ch.wait()
                    dve.tensor_tensor(fl[0:N, 1:3], fl[0:N, 1:3], scl[:], ALU.mult).then_inc(flag, 1)

                def t1_(d):
                    dve.wait_ge(y_mm, 8 * (b - 1) + d + 1)
                    if d == 0:
                        dve.wait_ge(z_rdy, 8 * b)
                    wait(dve, y2_rdy, 8 * (b - 1) + max(d - 1, 0))
                    dve.tensor_tensor(t1[:, d % 2, :], psP[(8 + 2 * d) % 3][:, 0:S], zs[:, d, :], ALU.mult).then_inc(t1_rdy, 1)

                def y2_(d):
                    dve.wait_ge(t1_ok, 8 * (b - 1) + d + 1)
                    wait(dve, y2_hi, 8 * (b - 1) + max(d - 1, 0))
                    wait(dve, y2_lo, 8 * (b - 1) + max(d - 1, 0))
                    dve.scalar_tensor_tensor(out=y2[:, d % 2, :], in0=xc[1 - par][:, d, :], scalar=dp[:, d:d + 1],
                                             in1=t1[:, d % 2, :], op0=ALU.mult, op1=ALU.add).then_inc(y2_rdy, 1)

                def y_lo(d):
                    dve.wait_ge(y2_hi, 8 * (b - 1) + d + 1)
                    minus(y2_l[:, d % 2, :], y2[:, d % 2, :], f32(y2_h[:, d % 2, :]), y2_lo)

                def xt_lo_(j):
                    dve.wait_ge(xt_hi, 4 * b + j + 1)
                    c = slice(2 * j * P, (2 * j + 2) * P)
                    minus(XT_l[:, :, c], psT[j % 2][:].rearrange("p (t s) -> p t s", t=TT), f32(XT_h[:, :, c]), xt_lo)

                more = cur and not (isinstance(b, int) and b == B - 1)
                for d in range(KE):
                    if prev:
                        t1_(d)
                        if d >= 1:
                            y_lo(d - 1)
                        y2_(d)
                    if cur:
                        if d == 0:
                            rows_1()
                        if d in (2, 3, 4):
                            rows_2(d - 2)
                        if d >= 2 and d % 2 == 0:
                            xt_lo_(d // 2 - 1)
                        if d == 5 and more:
                            moments(b + 1)
                        if d == 6:
                            rows_3()
                        if d == 7:
                            if more:
                                normalize(b + 1)
                if prev:
                    y_lo(KE - 1)
                if cur:
                    xt_lo_(3)
                if cur:
                    bounds()

            def add_res(b):
                dve.wait_ge(xres_ld, 16 * b + 16)
                dve.wait_ge(o_mm, 8 * b + 8)
                for t in range(TT):
                    dve.tensor_tensor(xres[:, t, :], psO[t][:], xres[:, t, :], ALU.add).then_inc(res, 1)

            run(body, dve, lambda: add_res(B - 1))
    return


def attention_phase(nc, x1, ctxT, WqT, bq, WkT, bk, WvT, bv, WoT, bo, Wr, br, y, xn3_d, lg, qs_d, ks_d):
    B, S, _ = x1.shape
    H, DK = 16, 32
    TT = S // P
    G = P // DK
    U = 2 * KD
    NE = Wr.shape[1]
    SCALE = float(DK) ** -0.5
    with ExitStack() as ctx:
        def sb(name, shape, dt=F32):
            return ctx.enter_context(nc.sbuf_tensor("b_" + name, shape, dt))

        def sem(name):
            return ctx.enter_context(nc.semaphore("b_" + name))

        w_h = [sb(f"w_h{i}", [P, KD, D], F32R) for i in range(4)]
        w_l = [sb(f"w_l{i}", [P, KD, D], F32R) for i in range(4)]
        wr, brb = sb("wr", [P, KD, NE]), sb("brb", [P, NE])
        bqc, bkc, bvc, bob = sb("bqc", [P, KD]), sb("bkc", [P, KD]), sb("bvc", [P, KD]), sb("bob", [P, D])
        ident, half = sb("ident", [P, P]), sb("half", [P, TT])
        xa, xres, xn = sb("xa", [P, TT, D]), sb("xres", [P, TT, D]), sb("xn", [P, TT, D])
        xn3 = sb("xn3", [P, TT, D])
        st, mv, ve, rs = sb("st", [P, TT, 6]), sb("mv", [P, TT, 2]), sb("ve", [P, TT]), sb("rs", [P, TT])
        st3, mv3, ve3, rs3 = sb("st3", [P, TT, 6]), sb("mv3", [P, TT, 2]), sb("ve3", [P, TT]), sb("rs3", [P, TT])
        xnT_h, xnT_l = sb("xnT_h", [P, KD, S], F32R), sb("xnT_l", [P, KD, S], F32R)
        cx, cx_h, cx_l = sb("cx", [P, KD, S]), sb("cx_h", [P, KD, S], F32R), sb("cx_l", [P, KD, S], F32R)
        t_h, t_l = sb("t_h", [P, 2, S], F32R), sb("t_l", [P, 2, S], F32R)
        qst = [sb(f"qst{i}", [3 * DK, H, S], F32R) for i in range(2)]
        kst = [sb(f"kst{i}", [3 * DK, H, S], F32R) for i in range(2)]
        V = [sb(f"V{i}", [P, TT, D]) for i in range(2)]
        pr = sb("pr", [P, 2, G, S])
        PT = sb("PT", [P, G, TT, S])
        mx, nm, rsum, rinv = sb("mx", [P, 2, G]), sb("nm", [P, 2, G]), sb("rsum", [P, 2, G]), sb("rinv", [P, 2, G])
        co_h, co_l = sb("co_h", [P, KD, S], F32R), sb("co_l", [P, KD, S], F32R)
        xn3T = xn[:].rearrange("p t d -> p (t d)").rearrange("p (k s) -> p k s", k=KD)

        psS = [ctx.enter_context(nc.psum_tensor(f"b_psS{i}", [P, G, S], F32)) for i in range(2)]
        psT = ctx.enter_context(nc.psum_tensor("b_psT", [P, 2 * G, P], F32))
        psV = ctx.enter_context(nc.psum_tensor("b_psV", [P, 512], F32))
        psQ = ctx.enter_context(nc.psum_tensor("b_psQ", [P, 512], F32))

        w_ld, p_ld, w_hi, w_lo = [sem(f"w_ld{i}") for i in range(2)], sem("p_ld"), sem("w_hi"), sem("w_lo")
        setup = sem("setup")
        xa_ld, xres_ld, cx_ld, x2_st, xn3_st = sem("xa_ld"), sem("xres_ld"), sem("cx_ld"), sem("x2_st"), sem("xn3_st")
        ln, rstd, ln3, rstd3 = sem("ln"), sem("rstd"), sem("ln3"), sem("rstd3")
        xn_tp, xnT_hi, xnT_lo = sem("xn_tp"), sem("xnT_hi"), sem("xnT_lo")
        cx_hi, cx_lo = sem("cx_hi"), sem("cx_lo")
        qk_mm, qk_hi, qk_lo = sem("qk_mm"), sem("qk_hi"), sem("qk_lo")
        tq_st, tk_st = [sem(f"tq_st{i}") for i in range(2)], [sem(f"tk_st{i}") for i in range(2)]
        q_ld, k_ld = sem("q_ld"), sem("k_ld")
        v_mm, v_cp = sem("v_mm"), sem("v_cp")
        s_mm, mx_s, nm_s, exp_s, ri_s, norm_s = (sem(n) for n in ("s_mm", "mx_s", "nm_s", "exp_s", "ri_s", "norm_s"))
        p_tp, pt_cp, pv_mm, co_hi, co_lo = (sem(n) for n in ("p_tp", "pt_cp", "pv_mm", "co_hi", "co_lo"))
        o_mm, x2_s, xb_s = sem("o_mm"), sem("x2_s"), sem("xb_s")
        r_tp, r_cp, r_mm, lg_s = sem("r_tp"), sem("r_cp"), sem("r_mm"), sem("lg_s")

        passed_v, passed_s, passed_p = sem("passed_v"), sem("passed_s"), sem("passed_p")

        x1_v = x1.rearrange("b (t p) d -> b p t d", p=P)
        y_v = y[0:B * S, :].rearrange("(b t p) d -> b p t d", p=P, t=TT)
        xn3_v = xn3_d[0:B * S, :].rearrange("(b t p) d -> b p t d", p=P, t=TT)
        ctx_v = ctxT.rearrange("b (k p) s -> b p k s", p=P)
        stage = [V[i] for i in range(2)]
        weights = (WqT, WkT, WvT, WoT)

        def run(body, eng):
            body(0, 0, True, False, False)
            body(1, 1, True, True, False)
            with eng.Fori(0, B // 2 - 2) as i:
                body(i * 2 + 2, 0, True, True, True)
                body(i * 2 + 3, 1, True, True, True)
            body(B - 2, 0, True, True, True)
            body(B - 1, 1, True, True, True)
            body(B, 0, False, True, True)
            body(B + 1, 1, False, False, True)

        def last(b):
            return isinstance(b, int) and b >= B - 1

        block = ctx.enter_context(nc.Block())

        @block.sync
        def _(sp):
            sp.dma_start(xa[:], x1_v[0]).then_inc(xa_ld, 16)
            sp.dma_start(cx[:], ctx_v[0]).then_inc(cx_ld, 16)
            with nc.allow_non_contiguous_dma(reason="small parameters"):
                for col, src in ((bqc, bq), (bkc, bk), (bvc, bv)):
                    sp.dma_start(col[:], src.rearrange("(k p) -> p k", p=P)).then_inc(p_ld, 16)
                sp.dma_start(wr[:], Wr.rearrange("(k p) n -> p k n", p=P)).then_inc(p_ld, 16)
                sp.dma_start(bob[:], bo.rearrange("(o n) -> o n", o=1).broadcast_to([P, D])).then_inc(p_ld, 16)
                sp.dma_start(brb[:], br.rearrange("(o n) -> o n", o=1).broadcast_to([P, NE])).then_inc(p_ld, 16)
            for c in range(8):
                if c >= 2:
                    sp.wait_ge(w_hi, c - 1)
                    sp.wait_ge(w_lo, c - 1)
                src = weights[c // 2].rearrange("(k p) n -> p k n", p=P)[:, 2 * (c % 2):2 * (c % 2) + 2, :]
                sp.dma_start(stage[c % 2][:], src).then_inc(w_ld[c % 2], 16)

            def body(b, par, cur, prev, prev2):
                def store(scratch, st_, first):
                    for i in range(KD):
                        sp.wait_ge(qk_lo, U * b + first + i + 1)
                        for part, t in enumerate((t_h, t_l)):
                            sp.dma_start(f32(scratch[part, i * P:(i + 1) * P, :]), f32(t[:, (first + i) % 2, :])).then_inc(st_[i % 2], 16)

                def load(scratch, st_, ld, stack, parts):
                    for p_ in range(2):
                        sp.wait_ge(st_[p_], 64 * b + 64)
                        sp.sem_inc(passed_s, 1)
                    wait(sp, s_mm, U * (b - 1))
                    for r, part in enumerate(parts):
                        sp.dma_start(f32(stack[r * DK:(r + 1) * DK, :, :]),
                                     f32(scratch[part].rearrange("(h d) s -> d h s", d=DK))).then_inc(ld, 16)

                if cur and not last(b):
                    sp.wait_ge(ln, 7 * b + 7)
                    sp.dma_start(xa[:], x1_v[b + 1]).then_inc(xa_ld, 16)
                if cur:
                    wait(sp, q_ld, 48 * b)
                    sp.sem_inc(passed_s, 1)
                    store(qs_d, tq_st, 0)
                if prev2:
                    sp.wait_ge(ln3, 7 * (b - 1))
                    sp.dma_start(xn3_v[b - 2], xn3[:]).then_inc(xn3_st, 16)
                if prev:
                    wait(sp, x2_st, 16 * (b - 1))
                    sp.dma_start(xres[:], x1_v[b - 1]).then_inc(xres_ld, 16)
                if cur:
                    load(qs_d, tq_st, q_ld, qst[par], (0, 1, 0))
                    if not last(b):
                        sp.wait_ge(cx_lo, b + 1)
                        sp.dma_start(cx[:], ctx_v[b + 1]).then_inc(cx_ld, 16)
                    wait(sp, k_ld, 48 * b)
                    sp.sem_inc(passed_s, 1)
                    store(ks_d, tk_st, KD)
                    load(ks_d, tk_st, k_ld, kst[par], (0, 0, 1))
                if prev:
                    sp.wait_ge(x2_s, 2 * b)
                    sp.dma_start(y_v[b - 1], xres[:]).then_inc(x2_st, 16)

            run(body, sp)
            sp.wait_ge(x2_st, 16 * B)
            sp.wait_ge(xn3_st, 16 * B)

        @block.gpsimd
        def _(pool):
            g = nc.gpsimd
            g.memset(ident[:], 0.0).then_inc(setup, 1)
            g.memset(half[:], -0.5).then_inc(setup, 1)
            pool.wait_ge(setup, 2)
            g.affine_select(out=ident[:], in_=ident[:], compare_op=ALU.not_equal, fill=1.0, base=0,
                            pattern=[[-1, P]], channel_multiplier=1).then_inc(setup, 1)

            def rsqrt(b, ln_, ve_, rs_, done):
                pool.wait_ge(ln_, 7 * b + 5)
                g.tensor_tensor(rs_[:], ve_[:], half[:], ALU.pow).then_inc(done, 1)

            rsqrt(0, ln, ve, rs, rstd)

            def body(b, par, cur, prev, prev2):
                if prev2:
                    rsqrt(b - 2, ln3, ve3, rs3, rstd3)
                if cur:
                    wait(pool, v_mm, 2 * b)
                    pool.wait_ge(cx_ld, 16 * b + 16)
                    g.sem_inc(passed_p, 1)
                    g.tensor_copy(cx_h[:], cx[:]).then_inc(cx_hi, 1)
                    pool.wait_ge(cx_hi, b + 1)
                    g.tensor_tensor(cx_l[:], cx[:], f32(cx_h[:]), ALU.subtract).then_inc(cx_lo, 1)
                if prev:
                    pool.wait_ge(xres_ld, 16 * b)
                    if isinstance(b, int) and b == 1:
                        pool.wait_ge(p_ld, 96)
                    for t in range(TT):
                        g.tensor_tensor(xres[:, t, :], xres[:, t, :], bob[:], ALU.add).then_inc(xb_s, 1)
                if cur and not last(b):
                    rsqrt(b + 1, ln, ve, rs, rstd)

            run(body, pool)

        @block.tensor
        def _(pe):
            def split_mm(out, hi_w, lo_w, hi_x, lo_x, first, last_):
                pe.matmul(out, lo_w, hi_x, start=first, stop=False)
                pe.matmul(out, hi_w, lo_x, start=False, stop=False)
                return pe.matmul(out, hi_w, hi_x, start=False, stop=last_)

            def turn_xn(b):
                pe.wait_ge(ln, 7 * b + 7)
                wait(pe, pt_cp, U * (b - 1))
                for kk in range(KD):
                    for t in range(TT):
                        mm = pe.transpose(psT[:, 2 * kk + t, :], xn[:, t, kk * P:(kk + 1) * P], ident[:])
                mm.then_inc(xn_tp, 1)

            pe.wait_ge(setup, 3)
            turn_xn(0)
            pe.wait_ge(w_lo, 8)

            def body(b, par, cur, prev, prev2):
                o = 1 - par

                def qk_tile(i):
                    m = i % KD
                    if i:
                        pe.wait_ge(qk_lo, U * b + i)
                        if i == 5 and prev2:
                            pe.wait_ge(lg_s, b - 1)
                    else:
                        wait(pe, x2_s, 2 * (b - 1) - 1)
                        wait(pe, v_cp, 2 * b)
                        pe.wait_ge(xnT_lo, b + 1)
                    if i == KD:
                        pe.wait_ge(cx_lo, b + 1)
                    n = i // KD
                    xh, xl = (xnT_h, xnT_l) if n == 0 else (cx_h, cx_l)
                    for kk in range(KD):
                        c = slice(m * P, m * P + P)
                        mm = split_mm(psQ[:, 0:S], w_h[n][:, kk, c], w_l[n][:, kk, c], xh[:, kk, :], xl[:, kk, :],
                                      kk == 0, kk == KD - 1)
                    mm.then_inc(qk_mm, 1)

                def v_tile(t):
                    if t:
                        pe.wait_ge(v_cp, 2 * b + 1)
                    else:
                        pe.wait_ge(qk_lo, U * b + U)
                    c = slice(t * P, t * P + P)
                    for kk in range(KD):
                        mm = split_mm(psQ[:], cx_h[:, kk, c], cx_l[:, kk, c], w_h[2][:, kk, :], w_l[2][:, kk, :],
                                      kk == 0, kk == KD - 1)
                    mm.then_inc(v_mm, 1)

                def scores(hb, u):
                    j, qt = u // TT, u % TT
                    stack = o if hb is not b else par
                    wait(pe, exp_s, 4 * (U * hb + u - 1))
                    if u == 0:
                        pe.wait_ge(q_ld, 48 * hb + 48)
                        pe.wait_ge(k_ld, 48 * hb + 48)
                    for h in range(G):
                        mm = pe.matmul(psS[u % 2][:, h, :], qst[stack][:, G * j + h, qt * P:(qt + 1) * P],
                                       kst[stack][:, G * j + h, :], start=True, stop=True)
                    mm.then_inc(s_mm, 1)

                def turn_p(u):
                    pe.wait_ge(norm_s, U * (b - 1) + u + 1)
                    if u:
                        pe.wait_ge(pt_cp, U * (b - 1) + u)
                        if u == 3 and prev2:
                            pe.wait_ge(r_cp, b - 1)
                    else:
                        pe.wait_ge(xnT_lo, b + 1 if cur else b)
                    for h in range(G):
                        for kt in range(TT):
                            mm = pe.transpose(psT[:, 2 * h + kt, :], pr[:, u % 2, h, kt * P:(kt + 1) * P], ident[:])
                    mm.then_inc(p_tp, 1)

                def pv(j):
                    pe.wait_ge(pt_cp, U * (b - 1) + 2 * j + 2)
                    wait(pe, co_lo, 4 * (b - 1) + j)
                    if j == 0:
                        pe.wait_ge(v_cp, 2 * b)
                        wait(pe, x2_s, 2 * (b - 1))
                    for kt in range(TT):
                        for h in range(G):
                            c = slice((G * j + h) * DK, (G * j + h + 1) * DK)
                            mm = pe.matmul(psV[h * DK:(h + 1) * DK, 0:S], V[o][:, kt, c], PT[:, h, kt, :],
                                           start=kt == 0, stop=kt == TT - 1)
                    mm.then_inc(pv_mm, 1)

                def turn_rows():
                    pe.wait_ge(ln3, 7 * (b - 1))
                    wait(pe, pt_cp, U * (b - 1) + 3 if prev else U * (b - 1))
                    for kk in range(KD):
                        for t in range(TT):
                            mm = pe.transpose(psT[:, 2 * kk + t, :], xn3[:, t, kk * P:(kk + 1) * P], ident[:])
                    mm.then_inc(r_tp, 1)

                def logits():
                    pe.wait_ge(r_cp, b - 1)
                    pe.wait_ge(x2_s, 2 * (b - 1))
                    if cur:
                        pe.wait_ge(qk_lo, U * b + 5)
                    for t in range(TT):
                        for kk in range(KD):
                            mm = pe.matmul(psQ[:, t * NE:(t + 1) * NE], xn3T[:, kk, t * P:(t + 1) * P], wr[:, kk, :],
                                           start=kk == 0, stop=kk == KD - 1)
                    mm.then_inc(r_mm, 1)

                for u in range(U):
                    if prev and 1 <= u < U - 1:
                        scores(b - 1, u + 1)
                    if cur:
                        qk_tile(u)
                    if prev and u:
                        turn_p(u - 1)
                    if prev and u >= 3 and u % 2:
                        pv((u - 3) // 2)
                    if prev2 and u == 3:
                        turn_rows()
                    if prev2 and u == 4:
                        logits()
                if cur:
                    v_tile(0)
                if prev:
                    turn_p(U - 1)
                if cur:
                    v_tile(1)
                if prev:
                    pv(KD - 1)
                if cur and not last(b):
                    turn_xn(b + 1)
                if cur:
                    scores(b, 0)
                    scores(b, 1)
                if prev:
                    for t, ps in enumerate((psQ, psV)):
                        pe.wait_ge(co_lo, 4 * b)
                        if t == 0 and cur:
                            pe.wait_ge(v_cp, 2 * b + 2)
                        elif t == 0:
                            pe.wait_ge(lg_s, b - 1)
                        c = slice(t * P, t * P + P)
                        for kk in range(KD):
                            mm = split_mm(ps[:], co_h[:, kk, c], co_l[:, kk, c], w_h[3][:, kk, :], w_l[3][:, kk, :],
                                          kk == 0, kk == KD - 1)
                        mm.then_inc(o_mm, 1)

            run(body, pe)

        @block.scalar
        def _(act):
            def copy(out, in_, done):
                act.activation(out, in_, ACT.Copy).then_inc(done, 1)

            for c in range(8):
                act.wait_ge(w_ld[c % 2], 16 * (c // 2 + 1))
                copy(w_h[c // 2][:, 2 * (c % 2):2 * (c % 2) + 2, :], stage[c % 2][:], w_hi)

            def split_xn(b):
                act.wait_ge(xn_tp, b + 1)
                wait(act, qk_mm, U * (b - 1) + 4)
                copy(xnT_h[:], psT[:].rearrange("p (k t) s -> p k (t s)", t=TT), xnT_hi)

            split_xn(0)
            act.wait_ge(p_ld, 96)
            act.wait_ge(w_lo, 8)

            def body(b, par, cur, prev, prev2):
                o = 1 - par

                def qk_hi_(i):
                    act.wait_ge(qk_mm, U * b + i + 1)
                    n, m = i // KD, i % KD
                    if m >= 2:
                        act.wait_ge((tq_st, tk_st)[n][m % 2], 64 * b + 32)
                    elif n == 1:
                        act.wait_ge(tq_st[m % 2], 64 * b + 64)
                    else:
                        wait(act, tk_st[m % 2], 64 * b)
                    act.activation(t_h[:, i % 2, :], psQ[:, 0:S], ACT.Identity,
                                   bias=(bqc, bkc)[n][:, m:m + 1]).then_inc(qk_hi, 1)

                def exps(hb, u):
                    act.wait_ge(nm_s, U * hb + u + 1)
                    wait(act, p_tp, U * hb + u - 1)
                    wait(act, norm_s, U * hb + u - 1)
                    for h in range(G):
                        act.activation(pr[:, u % 2, h, :], psS[u % 2][:, h, :], ACT.Exp, bias=nm[:, u % 2, h:h + 1],
                                       scale=SCALE, accum_out=rsum[:, u % 2, h:h + 1]).then_inc(exp_s, 1)

                def pt_copy(u):
                    act.wait_ge(p_tp, U * (b - 1) + u + 1)
                    if u % 2 == 0:
                        wait(act, pv_mm, 4 * (b - 1) + u // 2)
                    c = slice((u % 2) * P, (u % 2) * P + P)
                    copy(PT[:, :, :, c], psT[:].rearrange("p (h k) s -> p h k s", k=TT), pt_cp)

                def ctx_hi(j):
                    act.wait_ge(pv_mm, 4 * (b - 1) + j + 1)
                    wait(act, o_mm, 2 * (b - 1))
                    act.activation(co_h[:, j, :], psV[:, 0:S], ACT.Identity, bias=bvc[:, j:j + 1]).then_inc(co_hi, 1)

                def v_copy(t):
                    act.wait_ge(v_mm, 2 * b + t + 1)
                    wait(act, pv_mm, 4 * (b - 1))
                    copy(V[par][:, t, :], psQ[:], v_cp)

                for u in range(U):
                    if prev and u:
                        exps(b - 1, u)
                    if cur:
                        qk_hi_(u)
                    if prev and u:
                        pt_copy(u - 1)
                    if prev and u >= 3 and u % 2:
                        ctx_hi((u - 3) // 2)
                    if prev2 and u == 3:
                        act.wait_ge(r_tp, b - 1)
                        copy(xn3T, psT[:].rearrange("p (k t) s -> p k (t s)", t=TT), r_cp)
                if cur:
                    v_copy(0)
                if prev:
                    pt_copy(U - 1)
                if cur:
                    v_copy(1)
                if prev:
                    ctx_hi(KD - 1)
                if cur and not last(b):
                    split_xn(b + 1)
                if cur:
                    exps(b, 0)

            run(body, act)

        @block.vector
        def _(dve):
            def minus(out, a, b_, done):
                dve.tensor_tensor(out, a, b_, ALU.subtract).then_inc(done, 1)

            def moments(b, sem_, src, st, mv, ve):
                ch = Chain(dve, sem_, 7, b)
                for t in range(TT):
                    ch.did(dve.bn_stats(st[:, t, :], src[:, t, :]))
                ch.wait()
                dve.sem_inc(passed_v, 1)
                for t in range(TT):
                    ch.did(dve.bn_aggr(mv[:, t, :], st[:, t, :]))
                ch.wait()
                ch.did(dve.tensor_scalar(ve[:], mv[:, :, 1], EPS, None, ALU.add))

            def normalize(b, sem_, src, mv, rs, rstd, out):
                dve.wait_ge(rstd, b + 1)
                for t in range(TT):
                    dve.tensor_scalar(out[:, t, :], src[:, t, :], mv[:, t, 0:1], rs[:, t:t + 1],
                                      ALU.subtract, ALU.mult).then_inc(sem_, 1)

            def split_xn(b):
                dve.wait_ge(xnT_hi, b + 1)
                minus(xnT_l[:], psT[:].rearrange("p (k t) s -> p k (t s)", t=TT), f32(xnT_h[:]), xnT_lo)

            dve.wait_ge(xa_ld, 16)
            moments(0, ln, xa, st, mv, ve)
            normalize(0, ln, xa, mv, rs, rstd, xn)
            for c in range(8):
                dve.wait_ge(w_hi, c + 1)
                minus(w_l[c // 2][:, 2 * (c % 2):2 * (c % 2) + 2, :], stage[c % 2][:],
                      f32(w_h[c // 2][:, 2 * (c % 2):2 * (c % 2) + 2, :]), w_lo)
            split_xn(0)
            dve.wait_ge(p_ld, 96)

            def body(b, par, cur, prev, prev2):
                o = 1 - par

                def qk_lo_(i):
                    n, m = i // KD, i % KD
                    dve.wait_ge(qk_hi, U * b + i + 1)
                    dve.scalar_tensor_tensor(out=t_l[:, i % 2, :], in0=psQ[:, 0:S], scalar=(bqc, bkc)[n][:, m:m + 1],
                                             in1=f32(t_h[:, i % 2, :]), op0=ALU.add, op1=ALU.subtract).then_inc(qk_lo, 1)

                def row_max(hb, u):
                    n = U * hb + u
                    dve.wait_ge(s_mm, n + 1)
                    wait(dve, exp_s, 4 * (n - 1))
                    wait(dve, nm_s, n - 1)
                    dve.tensor_reduce(mx[:, u % 2, :], psS[u % 2][:], AX.X, ALU.max).then_inc(mx_s, 1)
                    dve.wait_ge(mx_s, n + 1)
                    dve.tensor_scalar(nm[:, u % 2, :], mx[:, u % 2, :], -SCALE, None, ALU.mult).then_inc(nm_s, 1)

                def norm(u):
                    n = U * (b - 1) + u
                    dve.wait_ge(exp_s, 4 * (n + 1))
                    wait(dve, norm_s, n - 1)
                    dve.reciprocal(rinv[:, u % 2, :], rsum[:, u % 2, :]).then_inc(ri_s, 1)
                    dve.wait_ge(ri_s, n + 1)
                    for h in range(G):
                        ins = dve.tensor_scalar(pr[:, u % 2, h, :], pr[:, u % 2, h, :], rinv[:, u % 2, h:h + 1], None, ALU.mult)
                    ins.then_inc(norm_s, 1)

                def ctx_lo(j):
                    dve.wait_ge(co_hi, 4 * (b - 1) + j + 1)
                    dve.scalar_tensor_tensor(out=co_l[:, j, :], in0=psV[:, 0:S], scalar=bvc[:, j:j + 1],
                                             in1=f32(co_h[:, j, :]), op0=ALU.add, op1=ALU.subtract).then_inc(co_lo, 1)

                more = cur and not last(b)
                for u in range(U):
                    if prev and 1 <= u < U - 1:
                        row_max(b - 1, u + 1)
                    if cur:
                        qk_lo_(u)
                    if prev:
                        norm(u)
                    if prev and u >= 3 and u % 2:
                        ctx_lo((u - 3) // 2)
                    if u == 0 and prev2:
                        dve.wait_ge(x2_s, 2 * (b - 1))
                        moments(b - 2, ln3, xres, st3, mv3, ve3)
                    if u == 1 and prev2:
                        normalize(b - 2, ln3, xres, mv3, rs3, rstd3, xn3)
                    if u == 4 and prev2:
                        dve.wait_ge(r_mm, b - 1)
                        for t in range(TT):
                            ins = dve.tensor_tensor(lg[:, bass.ds((b * TT + (t - 2 * TT)) * NE, NE)],
                                                    psQ[:, t * NE:(t + 1) * NE], brb[:], ALU.add)
                        ins.then_inc(lg_s, 1)
                    if u == 5 and more:
                        dve.wait_ge(xa_ld, 16 * b + 32)
                        moments(b + 1, ln, xa, st, mv, ve)
                    if u == 6 and more:
                        dve.wait_ge(xn_tp, b + 1)
                        wait(dve, r_mm, b - 1)
                        normalize(b + 1, ln, xa, mv, rs, rstd, xn)
                if prev:
                    ctx_lo(KD - 1)
                if more:
                    split_xn(b + 1)
                if prev2:
                    dve.wait_ge(xn3_st, 16 * (b - 1))
                for t, ps in enumerate((psQ, psV)):
                    if cur:
                        row_max(b, t)
                    if prev:
                        dve.wait_ge(o_mm, 2 * (b - 1) + t + 1)
                        dve.wait_ge(xb_s, 2 * b)
                        dve.tensor_tensor(xres[:, t, :], ps[:], xres[:, t, :], ALU.add).then_inc(x2_s, 1)

            run(body, dve)


CAPACITY = 1.2


def routing_phase(nc, lg, list_d, y, xn3_d, n_tok, NE):
    T = n_tok // P
    cap = -(-int(CAPACITY * 10) * n_tok // (10 * NE))
    R = next(r for r in range(P, 0, -1) if cap % r == 0)
    NG = NE * cap // R
    W = T * NE
    BITS = 30
    BIG = 1.0e5
    with ExitStack() as ctx:
        def sb(name, shape, dt=F32):
            return ctx.enter_context(nc.sbuf_tensor("c_" + name, shape, dt))

        def sem(name):
            return ctx.enter_context(nc.semaphore("c_" + name))

        te = [P, T, NE]
        ex, pb, eq, tmp, sel1, sel2, p2 = (sb(n, te) for n in ("ex", "pb", "eq", "tmp", "sel1", "sel2", "p2"))
        m, s, r, g1, g2, i1 = (sb(n, [P, T]) for n in ("m", "s", "r", "g1", "g2", "i1"))
        gate = sb("gate", [P, NE, T])
        ge, gt, tie, sel, pos, cum, slot = (sb(n, [P, NE, T]) for n in ("ge", "gt", "tie", "sel", "pos", "cum", "slot"))
        ione, iof = sb("ione", [P, NE], I32), sb("iof", [P, NE])
        tok, pay = sb("tok", [P, T], I32), sb("pay", [P, T, 2, 2])
        idx = sb("idx", [P, T, 2], I32)
        sl = sb("sl", [P, 2, T])
        thr, cand, bit, keep = (sb(n, [P, NE], I32) for n in ("thr", "cand", "bit", "keep"))
        cnt, need, base = sb("cnt", [P, NE]), sb("need", [P, NE]), sb("base", [P, NE])
        ones, below = sb("ones", [P, P]), sb("below", [P, P])
        one_w = sb("one_w", [P, W])
        fill, fill_id = sb("fill", [P, NG, 2]), sb("fill_id", [P, NG], I32)
        zero = sb("zero", [P, D])
        psC = ctx.enter_context(nc.psum_tensor("c_psC", [P, NE], F32))
        psA = ctx.enter_context(nc.psum_tensor("c_psA", [P, NE, T], F32))
        psB = ctx.enter_context(nc.psum_tensor("c_psB", [P, NE, T], F32))

        made, made_v, zero_st, fill_st = sem("made"), sem("made_v"), sem("zero_st"), sem("fill_st")
        ch_s, exp_s, cnt_s, sum_s, bit_s = sem("ch"), sem("exp"), sem("cnt"), sem("sum"), sem("bit")
        pre_s, mm_s, pay_s, sc_s = sem("pre"), sem("mm"), sem("pay"), sem("sc")
        passed = sem("passed")

        block = ctx.enter_context(nc.Block())

        @block.gpsimd
        def _(pool):
            g = nc.gpsimd
            g.iota(ione[:], [[1, NE]], base=0, channel_multiplier=0).then_inc(made, 1)
            g.iota(tok[:], [[P, T]], base=0, channel_multiplier=1).then_inc(made, 1)
            g.iota(fill_id[:], [[0, NG]], base=n_tok, channel_multiplier=1).then_inc(made, 1)
            g.memset(ones[:], 1.0).then_inc(made, 1)
            g.memset(below[:], 1.0).then_inc(made, 1)
            g.memset(zero[:], 0.0).then_inc(made, 1)
            g.memset(fill[:], 0.0).then_inc(made, 1)
            pool.wait_ge(made, 7)
            g.affine_select(out=below[:], in_=below[:], compare_op=ALU.is_gt, fill=0.0, base=0,
                            pattern=[[1, P]], channel_multiplier=-1).then_inc(made, 1)
            pool.wait_ge(pay_s, 1)
            pool.wait_ge(fill_st, 16)
            for t in range(T):
                for kk in range(2):
                    g.indirect_dma_start(out=list_d, out_offset=bass.IndirectOffsetOnAxis(ap=idx[:, t, kk:kk + 1], axis=0),
                                         in_=pay[:, t, kk, :], in_offset=None, bounds_check=NE * cap - 1,
                                         oob_is_err=False).then_inc(sc_s, 16)
            pool.wait_ge(sc_s, 16 * 2 * T)

        @block.sync
        def _(sp):
            sp.wait_ge(made, 8)
            sp.dma_start(y[n_tok:n_tok + P, :], zero[:]).then_inc(zero_st, 16)
            sp.dma_start(xn3_d[n_tok:n_tok + P, :], zero[:]).then_inc(zero_st, 16)
            sp.wait_ge(made_v, 1)
            with nc.allow_non_contiguous_dma(reason="the lists' rows"):
                sp.dma_start(list_d.rearrange("(g r) c -> r g c", r=R), fill[0:R]).then_inc(fill_st, 16)
            sp.wait_ge(zero_st, 32)

        @block.scalar
        def _(act):
            act.wait_ge(ch_s, 2)
            act.activation(ex[:], ex[:], ACT.Exp).then_inc(exp_s, 1)

        @block.tensor
        def _(pe):
            pe.wait_ge(made, 8)
            with pe.Fori(0, BITS) as i:
                pe.wait_ge(cnt_s, i + 1)
                pe.matmul(psC[:], ones[:], cnt[:], start=True, stop=True).then_inc(sum_s, 1)
            pe.wait_ge(cnt_s, BITS + 1)
            pe.matmul(psC[:], ones[:], cnt[:], start=True, stop=True).then_inc(sum_s, 1)
            for j, src in enumerate((tie, sel)):
                pe.wait_ge(pre_s, j + 1)
                pe.matmul(psA[:].rearrange("p e t -> p (e t)"), below[:], src[:].rearrange("p e t -> p (e t)"), start=True, stop=True)
                pe.matmul(psB[:].rearrange("p e t -> p (e t)"), ones[:], src[:].rearrange("p e t -> p (e t)"),
                          start=True, stop=True).then_inc(mm_s, 1)

        @block.vector
        def _(dve):
            n = [0]

            def did(ins):
                ins.then_inc(ch_s, 1)
                n[0] += 1
                dve.wait_ge(ch_s, n[0])

            def over_e(ap):
                return ap.rearrange("p (t o) -> p t o", o=1).broadcast_to(te)

            def over_t(ap):
                return ap.rearrange("p (e o) -> p e o", o=1).broadcast_to([P, NE, T])

            lgv = lg[:].rearrange("p (t e) -> p t e", e=NE)
            dve.memset(one_w[:], 1.0)
            dve.memset(thr[:], 0)
            dve.memset(bit[:], 1 << (BITS - 1))
            dve.wait_ge(made, 8)
            dve.tensor_copy(fill[:, :, 0].bitcast(I32), fill_id[:]).then_inc(made_v, 1)
            did(dve.tensor_reduce(m[:], lgv, AX.X, ALU.max))
            did(dve.tensor_tensor(ex[:], lgv, over_e(m[:]), ALU.subtract))
            did(dve.tensor_copy(iof[:], ione[:]))
            dve.wait_ge(exp_s, 1)
            did(dve.tensor_reduce(s[:], ex[:], AX.X, ALU.add))
            did(dve.reciprocal(r[:], s[:]))
            did(dve.tensor_tensor(pb[:], ex[:], over_e(r[:]), ALU.mult))

            def top(p, g, sl_):
                did(dve.tensor_reduce(g[:], p[:], AX.X, ALU.max))
                did(dve.tensor_tensor(eq[:], p[:], over_e(g[:]), ALU.is_equal))
                io = iof[:].rearrange("p (o e) -> p o e", o=1).broadcast_to(te)
                did(dve.scalar_tensor_tensor(out=tmp[:], in0=eq[:], scalar=-float(NE), in1=io, op0=ALU.mult, op1=ALU.add))
                did(dve.tensor_reduce(i1[:], tmp[:], AX.X, ALU.min))
                did(dve.tensor_tensor(sl_[:], tmp[:], over_e(i1[:]), ALU.is_equal))

            top(pb, g1, sel1)
            did(dve.scalar_tensor_tensor(out=p2[:], in0=sel1[:], scalar=-2.0, in1=pb[:], op0=ALU.mult, op1=ALU.add))
            top(p2, g2, sel2)
            did(dve.tensor_tensor(tmp[:], sel1[:], sel2[:], ALU.add))
            did(dve.tensor_tensor(gate[:].rearrange("p e t -> p t e"), pb[:], tmp[:], ALU.mult))
            with dve.Fori(0, BITS) as i:
                dve.tensor_tensor(cand[:], thr[:], bit[:], ALU.bitwise_or).then_inc(bit_s, 1)
                dve.wait_ge(bit_s, i * 5 + 1)
                dve.tensor_tensor(ge[:], gate[:], over_t(cand[:].bitcast(F32)), ALU.is_ge).then_inc(bit_s, 1)
                dve.tensor_scalar(bit[:], bit[:], 1, None, ALU.logical_shift_right).then_inc(bit_s, 1)
                dve.wait_ge(bit_s, i * 5 + 3)
                dve.tensor_reduce(cnt[:], ge[:], AX.X, ALU.add).then_inc(cnt_s, 1)
                dve.wait_ge(sum_s, i + 1)
                dve.tensor_scalar(keep[:], psC[:], float(cap), None, ALU.is_ge).then_inc(bit_s, 1)
                dve.wait_ge(bit_s, i * 5 + 4)
                dve.sem_inc(passed, 1)
                dve.copy_predicated(thr[:], keep[:], cand[:]).then_inc(bit_s, 1)
                dve.wait_ge(bit_s, i * 5 + 5)
            th = over_t(thr[:].bitcast(F32))
            did(dve.tensor_tensor(gt[:], gate[:], th, ALU.is_gt))
            dve.tensor_reduce(cnt[:], gt[:], AX.X, ALU.add).then_inc(cnt_s, 1)
            did(dve.tensor_tensor(tie[:], gate[:], th, ALU.is_equal))
            did(dve.tensor_scalar(ge[:], gate[:], 0.0, None, ALU.is_gt))
            did(dve.tensor_tensor(tie[:], tie[:], ge[:], ALU.mult))
            dve.sem_inc(pre_s, 1)
            dve.wait_ge(sum_s, BITS + 1)
            did(dve.tensor_scalar(need[:], psC[:], -1.0, float(cap), ALU.mult, ALU.add))

            def place(j):
                dve.wait_ge(mm_s, j + 1)
                did(dve.tensor_copy(cum[:], psB[:]))
                did(dve.tensor_tensor_scan(pos[:].rearrange("p e t -> p (e t)"), one_w[:], cum[:].rearrange("p e t -> p (e t)"),
                                           0.0, ALU.mult, ALU.add))
                did(dve.tensor_tensor(cum[:], pos[:], cum[:], ALU.subtract))
                did(dve.tensor_copy(base[:], cum[:, :, 0]))
                did(dve.tensor_tensor(cum[:], cum[:], over_t(base[:]), ALU.subtract))
                did(dve.tensor_tensor(pos[:], cum[:], psA[:], ALU.add))

            place(0)
            did(dve.tensor_tensor(ge[:], pos[:], over_t(need[:]), ALU.is_lt))
            did(dve.tensor_tensor(tie[:], tie[:], ge[:], ALU.mult))
            did(dve.tensor_tensor(sel[:], gt[:], tie[:], ALU.add))
            dve.sem_inc(pre_s, 1)
            place(1)
            did(dve.tensor_scalar(base[:], iof[:], float(cap), -BIG, ALU.mult, ALU.add))
            did(dve.tensor_tensor(pos[:], pos[:], over_t(base[:]), ALU.add))
            did(dve.tensor_tensor(slot[:], pos[:], sel[:], ALU.mult))
            slot_te = slot[:].rearrange("p e t -> p t e")
            for kk, (sl_, g) in enumerate(((sel1, g1), (sel2, g2))):
                did(dve.tensor_tensor(tmp[:], sl_[:], slot_te, ALU.mult))
                did(dve.tensor_reduce(sl[:, kk, :], tmp[:], AX.X, ALU.add))
                did(dve.tensor_scalar(idx[:, :, kk], sl[:, kk, :], BIG, None, ALU.add))
                did(dve.tensor_copy(pay[:, :, kk, 0].bitcast(I32), tok[:]))
                did(dve.tensor_copy(pay[:, :, kk, 1], g[:]))
            dve.sem_inc(pay_s, 1)


def ffn_phase(nc, xn3_d, y, list_d, W1, b1, W2, b2, out, n_tok):
    NE, _, H = W1.shape
    cap = -(-int(CAPACITY * 10) * n_tok // (10 * NE))
    R = next(r for r in range(P, 0, -1) if cap % r == 0)
    NT = cap // R
    HALF = (cap + 1) // 2 + (cap + 1) // 2 % 2
    CW = 2 * HALF
    MH = H // P
    CH = 4
    MC = MH // CH
    assert cap % R == 0 and CW >= cap and HALF <= 512
    with ExitStack() as ctx:
        def sb(name, shape, dt=F32):
            return ctx.enter_context(nc.sbuf_tensor("d_" + name, shape, dt))

        def sem(name):
            return ctx.enter_context(nc.semaphore("d_" + name))

        ident = sb("ident", [P, P])
        lst = sb("lst", [R, NE * NT, 2])
        ids = [sb(f"ids{i}", [R, NT], I32) for i in range(2)]
        gts = [sb(f"gts{i}", [R, NT]) for i in range(2)]
        xg = sb("xg", [R, NT, D])
        xgT_h, xgT_l = ([sb(f"xgT_{a}{i}", [P, KD, CW], F32R) for i in range(2)] for a in "hl")
        w1, w2 = ([sb(f"w{a}_{i}", [P, MC, P * MC]) for i in range(2)] for a in (1, 2))
        w1_h, w1_l, w2_h, w2_l = ([sb(f"{a}{i}", [P, MC, P * MC], F32R) for i in range(2)] for a in ("w1_h", "w1_l", "w2_h", "w2_l"))
        hf = sb("hf", [P, 2, CW])
        h_h, h_l = sb("h_h", [P, 2, CW], F32R), sb("h_l", [P, 2, CW], F32R)
        b1c = [sb(f"b1c{i}", [P, MH]) for i in range(2)]
        b2r = [sb(f"b2r{i}", [R, D]) for i in range(2)]
        ob = sb("ob", [R, NT, D])
        psH = [ctx.enter_context(nc.psum_tensor(f"d_psH{i}", [P, 512], F32)) for i in range(2)]
        psO = [ctx.enter_context(nc.psum_tensor(f"d_psO{i}", [P, 512], F32)) for i in range(NT)]
        psT = ctx.enter_context(nc.psum_tensor("d_psT", [P, KD, P], F32))

        setup, lst_ld, ids_s = sem("setup"), sem("lst_ld"), sem("ids")
        b_ld, w1_ld, w2_ld = ([sem(f"{a}_ld{i}") for i in range(2)] for a in ("b", "w1", "w2"))
        g_ld, g_tp, g_hi, g_lo = sem("g_ld"), sem("g_tp"), sem("g_hi"), sem("g_lo")
        w1_hi, w1_lo, w2_hi, w2_lo = sem("w1_hi"), sem("w1_lo"), sem("w2_hi"), sem("w2_lo")
        h_mm, silu_s, h_hi, h_lo, o_mm = sem("h_mm"), sem("silu"), sem("h_hi"), sem("h_lo"), sem("o_mm")
        ob_s, og_s, sc, out_st = sem("ob"), sem("og"), sem("sc"), sem("out_st")
        passed_p, passed_s = sem("passed_p"), sem("passed_s")

        w1_v = W1.rearrange("e (k p) h -> e p k h", p=P)
        w2_v = W2.rearrange("e (m p) d -> e p m d", p=P)
        b1_v = b1.rearrange("e (m p) -> e p m", p=P)

        def run(body, eng):
            body(0, 0, 0)
            with eng.Fori(0, NE // 2 - 1) as i:
                body(i * 2 + 1, i, 1)
                body(i * 2 + 2, i + 1, 0)
            body(NE - 1, NE // 2 - 1, 1)

        def last(e):
            return isinstance(e, int) and e == NE - 1

        block = ctx.enter_context(nc.Block())

        @block.sync
        def _(sp):
            with nc.allow_non_contiguous_dma(reason="the lists' rows"):
                sp.dma_start(lst[:], list_d.rearrange("(g r) c -> r g c", r=R)).then_inc(lst_ld, 16)

            def biases(e, par):
                with nc.allow_non_contiguous_dma(reason="small parameters"):
                    sp.dma_start(b1c[par][:], b1_v[e]).then_inc(b_ld[par], 16)
                sp.dma_start(b2r[par][:], b2[bass.ds(e, 1), :].broadcast_to([R, D])).then_inc(b_ld[par], 16)

            biases(0, 0)

            def body(e, k, par):
                for c in range(CH):
                    if c == CH - 1 and not last(e):
                        wait(sp, silu_s, 2 * MH * e)
                        sp.sem_inc(passed_s, 1)
                        wait(sp, ob_s, NT * e)
                        sp.sem_inc(passed_s, 1)
                        biases(e + 1, 1 - par)
                    s_ = c % 2
                    cols = slice(c * MC * P, (c + 1) * MC * P)
                    wait(sp, w1_hi, CH * e + c - 1)
                    wait(sp, w1_lo, CH * e + c - 1)
                    sp.sem_inc(passed_s, 1)
                    sp.dma_start(w1[s_][:], w1_v[e, :, :, cols]).then_inc(w1_ld[s_], 16)
                    wait(sp, w2_hi, CH * e + c - 1)
                    wait(sp, w2_lo, CH * e + c - 1)
                    sp.sem_inc(passed_s, 1)
                    sp.dma_start(w2[s_][:], w2_v[e, :, c * MC:(c + 1) * MC, :]).then_inc(w2_ld[s_], 16)

            run(body, sp)
            sp.wait_ge(sc, 16 * NT * NE)
            sp.sem_inc(passed_s, 1)
            sp.dma_start(out.rearrange("b s d -> (b s) d"), y[0:n_tok, :]).then_inc(out_st, 16)
            sp.wait_ge(out_st, 16)

        @block.gpsimd
        def _(pool):
            g = nc.gpsimd
            g.memset(ident[:], 0.0).then_inc(setup, 1)
            for i in range(2):
                g.memset(f32(xgT_h[i][:, :, cap:CW]), 0.0).then_inc(setup, 1)
                g.memset(f32(xgT_l[i][:, :, cap:CW]), 0.0).then_inc(setup, 1)
            pool.wait_ge(setup, 5)
            g.affine_select(out=ident[:], in_=ident[:], compare_op=ALU.not_equal, fill=1.0, base=0,
                            pattern=[[-1, P]], channel_multiplier=1).then_inc(setup, 1)

            def gather(e, par):
                pool.wait_ge(ids_s, 2 * e + 2)
                wait(pool, g_tp, NT * e)
                g.sem_inc(passed_p, 1)
                for t in range(NT):
                    g.indirect_dma_start(out=xg[:, t, :], out_offset=None, in_=xn3_d,
                                         in_offset=bass.IndirectOffsetOnAxis(ap=ids[par][:, t:t + 1], axis=0),
                                         bounds_check=n_tok + P - 1, oob_is_err=True).then_inc(g_ld, 16)

            gather(0, 0)

            def body(e, k, par):
                if not last(e):
                    gather(e + 1, 1 - par)
                wait(pool, sc, 16 * NT * e)
                g.sem_inc(passed_p, 1)
                for t in range(NT):
                    pool.wait_ge(og_s, NT * e + t + 1)
                    g.sem_inc(passed_p, 1)
                    g.indirect_dma_start(out=y, out_offset=bass.IndirectOffsetOnAxis(ap=ids[par][:, t:t + 1], axis=0),
                                         in_=ob[:, t, :], in_offset=None, bounds_check=n_tok + P - 1, oob_is_err=True,
                                         compute_op=ALU.add).then_inc(sc, 16)

            run(body, pool)

        @block.tensor
        def _(pe):
            def split_mm(out, hi_w, lo_w, hi_x, lo_x, first, last_):
                pe.matmul(out, lo_w, hi_x, start=first, stop=False)
                pe.matmul(out, hi_w, lo_x, start=False, stop=False)
                return pe.matmul(out, hi_w, hi_x, start=False, stop=last_)

            def turn(e, t):
                if t == 0:
                    pe.wait_ge(g_ld, 16 * NT * (e + 1))
                wait(pe, g_lo, NT * e + t)
                for kk in range(KD):
                    mm = pe.transpose(psT[:, kk, 0:R], xg[:, t, kk * P:(kk + 1) * P], ident[0:R, 0:R])
                mm.then_inc(g_tp, 1)

            pe.wait_ge(setup, 6)
            for t in range(NT):
                turn(0, t)

            def body(e, k, par):
                pe.wait_ge(g_lo, NT * (e + 1))

                def outer(m):
                    c, s_ = m // MC, (m // MC) % 2
                    pe.wait_ge(h_lo, MH * e + m + 1)
                    pe.wait_ge(w2_lo, CH * e + c + 1)
                    for t in range(NT):
                        if m == 0:
                            wait(pe, ob_s, NT * (e - 1) + t + 1)
                        cc = slice(t * R, (t + 1) * R)
                        mm = split_mm(psO[t][0:R, :], h_h[:, m % 2, cc], h_l[:, m % 2, cc], w2_h[s_][:, m % MC, :],
                                      w2_l[s_][:, m % MC, :], m == 0, m == MH - 1)
                        if m == MH - 1:
                            mm.then_inc(o_mm, 1)
                    if m < MH - 1 :
                        mm.then_inc(o_mm, 1)

                for m in range(MH):
                    c, s_ = m // MC, (m // MC) % 2
                    pe.wait_ge(w1_lo, CH * e + c + 1)
                    for n in range(2):
                        wait(pe, silu_s, 2 * (MH * e + m - 1) + n + 1)
                        for kk in range(KD):
                            cc = slice((m % MC) * P, (m % MC + 1) * P)
                            mm = split_mm(psH[n][:, 0:HALF], w1_h[s_][:, kk, cc], w1_l[s_][:, kk, cc],
                                          xgT_h[par][:, kk, n * HALF:(n + 1) * HALF], xgT_l[par][:, kk, n * HALF:(n + 1) * HALF],
                                          kk == 0, kk == KD - 1)
                        mm.then_inc(h_mm, 1)
                    if m:
                        outer(m - 1)
                    if m >= 5 and (m - 5) % 2 == 0 and (m - 5) // 2 < NT and not last(e):
                        turn(e + 1, (m - 5) // 2)
                outer(MH - 1)

            run(body, pe)

        OM = MH - 1 + NT

        @block.scalar
        def _(act):
            def copy(out, in_, done):
                act.activation(out, in_, ACT.Copy).then_inc(done, 1)

            def rows_hi(e, par, t):
                act.wait_ge(g_tp, NT * e + t + 1)
                copy(xgT_h[par][:, :, t * R:(t + 1) * R], psT[:, :, 0:R], g_hi)

            def w_parts(e, k, c):
                s_ = c % 2
                act.wait_ge(w1_ld[s_], 32 * e + 16 * (c // 2) + 16)
                wait(act, h_mm, 2 * (MH * e + MC * (c - 1)))
                copy(w1_h[s_][:], w1[s_][:], w1_hi)
                act.wait_ge(w2_ld[s_], 32 * e + 16 * (c // 2) + 16)
                if c >= 2:
                    act.wait_ge(o_mm, OM * e + MC * (c - 1))
                elif c == 1:
                    wait(act, o_mm, OM * e)
                else:
                    wait(act, o_mm, OM * (e - 1) + MC * (CH - 1))
                copy(w2_h[s_][:], w2[s_][:], w2_hi)

            for t in range(NT):
                rows_hi(0, 0, t)
            w_parts(0, 0, 0)

            def body(e, k, par):
                act.wait_ge(b_ld[par], 32 * k + 32)
                for m in range(MH):
                    for n in range(2):
                        act.wait_ge(h_mm, 2 * (MH * e + m) + n + 1)
                        wait(act, h_lo, MH * e + m - 1)
                        act.activation(hf[:, m % 2, n * HALF:(n + 1) * HALF], psH[n][:, 0:HALF], ACT.Silu,
                                       bias=b1c[par][:, m:m + 1]).then_inc(silu_s, 1)
                    act.wait_ge(silu_s, 2 * (MH * e + m + 1))
                    if m >= 2:
                        act.wait_ge(o_mm, OM * e + m - 1)
                    else:
                        wait(act, o_mm, OM * e)
                    copy(h_h[:, m % 2, :], hf[:, m % 2, :], h_hi)
                    if m >= 5 and (m - 5) % 2 == 0 and (m - 5) // 2 < NT and not last(e):
                        rows_hi(e + 1, 1 - par, (m - 5) // 2)
                    if m % MC == 1 and m // MC + 1 < CH:
                        w_parts(e, k, m // MC + 1)
                    if m == MH - 2 and not last(e):
                        w_parts(e + 1, k, 0)
                for t in range(NT):
                    act.wait_ge(ob_s, NT * e + t + 1)
                    act.activation(ob[:, t, :], ob[:, t, :], ACT.Copy, scale=gts[par][:, t:t + 1]).then_inc(og_s, 1)

            run(body, act)

        @block.vector
        def _(dve):
            def minus(out, a, b_, done):
                dve.tensor_tensor(out, a, b_, ALU.subtract).then_inc(done, 1)

            def rows_lo(e, par, t):
                dve.wait_ge(g_hi, NT * e + t + 1)
                c = slice(t * R, (t + 1) * R)
                minus(xgT_l[par][:, :, c], psT[:, :, 0:R], f32(xgT_h[par][:, :, c]), g_lo)

            def w_parts(e, c):
                s_ = c % 2
                dve.wait_ge(w1_hi, CH * e + c + 1)
                minus(w1_l[s_][:], w1[s_][:], f32(w1_h[s_][:]), w1_lo)
                dve.wait_ge(w2_hi, CH * e + c + 1)
                minus(w2_l[s_][:], w2[s_][:], f32(w2_h[s_][:]), w2_lo)

            def lists(e, par):
                wait(dve, sc, 16 * NT * (e - 1))
                wait(dve, og_s, NT * (e - 1))
                at = bass.ds(e * NT, NT)
                dve.tensor_copy(ids[par][:], lst[:, at, 0].bitcast(I32)).then_inc(ids_s, 1)
                dve.tensor_copy(gts[par][:], lst[:, at, 1]).then_inc(ids_s, 1)

            dve.wait_ge(lst_ld, 16)
            lists(0, 0)
            for t in range(NT):
                rows_lo(0, 0, t)
            w_parts(0, 0)

            def body(e, k, par):
                for m in range(MH):
                    if m == 3 and not last(e):
                        lists(e + 1, 1 - par)
                    dve.wait_ge(h_hi, MH * e + m + 1)
                    minus(h_l[:, m % 2, :], hf[:, m % 2, :], f32(h_h[:, m % 2, :]), h_lo)
                    if m >= 5 and (m - 5) % 2 == 0 and (m - 5) // 2 < NT and not last(e):
                        rows_lo(e + 1, 1 - par, (m - 5) // 2)
                    if m % MC == 1 and m // MC + 1 < CH:
                        w_parts(e, m // MC + 1)
                    if m == MH - 2 and not last(e):
                        w_parts(e + 1, 0)
                for t in range(NT):
                    dve.wait_ge(o_mm, OM * e + MH - 1 + t + 1)
                    wait(dve, sc, 16 * NT * e)
                    dve.tensor_tensor(ob[:, t, :], psO[t][0:R, :], b2r[par][:], ALU.add).then_inc(ob_s, 1)

            run(body, dve)


def block_kernel(nc, x, ctxT, W_inT, conv_w, conv_b, W_xprojT, A_log, D_param, W_outT,
                 WqT, bq, WkT, bk, WvT, bv, WoT, bo, Wr, br, W1, b1, W2, b2, out):
    B, S, _ = x.shape
    n_tok = B * S
    NE = Wr.shape[1]
    cap = -(-int(CAPACITY * 10) * n_tok // (10 * NE))

    def scratch(name, shape, dt=F32):
        return nc.dram_tensor(name, shape, dt, kind="Internal").ap()

    x1 = scratch("x1_d", (B, S, D))
    rows = scratch("rows_d", (3, B, S))
    qs, ks = scratch("qs_d", (2, D, S), F32R), scratch("ks_d", (2, D, S), F32R)
    y, xn3 = scratch("y_d", (n_tok + P, D)), scratch("xn3_d", (n_tok + P, D))
    lists = scratch("lists_d", (NE * cap, 2))
    mamba_phase(nc, x, W_inT, conv_w, conv_b, W_xprojT, A_log, D_param, W_outT, x1, rows)
    with nc.sbuf_tensor("lg", [P, n_tok // P * NE], F32) as lg:
        attention_phase(nc, x1, ctxT, WqT, bq, WkT, bk, WvT, bv, WoT, bo, Wr, br, y, xn3, lg, qs, ks)
        routing_phase(nc, lg, lists, y, xn3, n_tok, NE)
    ffn_phase(nc, xn3, y, lists, W1, b1, W2, b2, out, n_tok)


def kernel(x, ctx_1024, L0_attn_W_in, L0_attn_conv_w, L0_attn_conv_b, L0_attn_W_xproj, L0_attn_A_log, L0_attn_D_param,
           L0_attn_W_out, L0_xattn_Wq, L0_xattn_bq, L0_xattn_Wk, L0_xattn_bk, L0_xattn_Wv, L0_xattn_bv, L0_xattn_Wo,
           L0_xattn_bo, L0_ffn_Wr, L0_ffn_br, L0_ffn_W1, L0_ffn_b1, L0_ffn_W2, L0_ffn_b2):
    import numpy as _np
    import concourse.bacc as _bacc
    from concourse import mybir as _mybir
    from concourse.bass_utils import run_bass_kernel_spmd as _run

    ins = dict(x=x, ctxT=ctx_1024.transpose(0, 2, 1), W_inT=L0_attn_W_in.T, conv_w=L0_attn_conv_w, conv_b=L0_attn_conv_b,
               W_xprojT=L0_attn_W_xproj.T, A_log=L0_attn_A_log, D_param=L0_attn_D_param, W_outT=L0_attn_W_out.T,
               WqT=L0_xattn_Wq.T, bq=L0_xattn_bq, WkT=L0_xattn_Wk.T, bk=L0_xattn_bk, WvT=L0_xattn_Wv.T, bv=L0_xattn_bv,
               WoT=L0_xattn_Wo.T, bo=L0_xattn_bo, Wr=L0_ffn_Wr, br=L0_ffn_br, W1=L0_ffn_W1, b1=L0_ffn_b1, W2=L0_ffn_W2,
               b2=L0_ffn_b2)
    nc = _bacc.Bacc("TRN2", target_bir_lowering=False, num_devices=1)
    arrays, args = {}, []
    for name, a in ins.items():
        a = _np.ascontiguousarray(a)
        arrays[f"in_{name}_dram"] = a
        args.append(nc.dram_tensor(f"in_{name}_dram", a.shape, _mybir.dt.from_np(a.dtype), kind="ExternalInput").ap())
    args.append(nc.dram_tensor("out_0_dram", x.shape, _mybir.dt.float32, kind="ExternalOutput").ap())
    block_kernel(nc, *args)
    r = _run(nc, [arrays], core_ids=[0])
    return r.results[0]["out_0_dram"]
```

```python
from contextlib import ExitStack

import concourse.bass as bass
from concourse import mybir

F32 = mybir.dt.float32
F32R = mybir.dt.float32r
I32 = mybir.dt.int32
ALU = mybir.AluOpType
ACT = mybir.ActivationFunctionType
AX = mybir.AxisListType
RMAX = bass.bass_isa.ReduceOp.max

P = 128
D = 512
KD = D // P
EPS = 1e-5


def wait(eng, sem, value):
    if isinstance(value, int) and value <= 0:
        return
    eng.wait_ge(sem, value)


class Chain:

    def __init__(self, eng, sem, per, b):
        self.eng, self.sem, self.per, self.b, self.n = eng, sem, per, b, 0

    def did(self, instruction):
        instruction.then_inc(self.sem, 1)
        self.n += 1

    def wait(self):
        self.eng.wait_ge(self.sem, self.b * self.per + self.n)


def f32(ap):
    return ap.bitcast(F32)


def mamba_phase(nc, x, W_inT, conv_w, conv_b, W_xprojT, A_log, D_param, W_outT, x1, rows_dram):
    B, S, _ = x.shape
    E = conv_w.shape[0]
    KE = E // P
    N = 16
    TT = S // P
    BL = 32
    NB = S // BL
    HB = P // BL
    NI = NB + NB - HB
    CL = 8
    with ExitStack() as ctx:
        def sb(name, shape, dt=F32):
            return ctx.enter_context(nc.sbuf_tensor("a_" + name, shape, dt))

        def sem(name):
            return ctx.enter_context(nc.semaphore("a_" + name))

        win_h, win_l = sb("win_h", [P, KD, 2 * E], F32R), sb("win_l", [P, KD, 2 * E], F32R)
        wout_h, wout_l = sb("wout_h", [P, KE, D], F32R), sb("wout_l", [P, KE, D], F32R)
        wx_h, wx_l = sb("wx_h", [P, KE, P], F32R), sb("wx_l", [P, KE, P], F32R)
        wx_raw = sb("wx_raw", [P, KE, 33])
        cw, cb, dp = sb("cw", [P, KE, 4]), sb("cb", [P, KE]), sb("dp", [P, KE])
        a_neg, a_log = sb("a_neg", [N, 1]), sb("a_log", [N, 1])
        ident, mask, half = sb("ident", [P, P]), sb("mask", [P, S + P]), sb("half", [P, TT])
        ones_row = sb("ones_row", [N, S])
        xl = sb("xl", [P, TT, D])
        xres = sb("xres", [P, TT, D])
        xn = sb("xn", [P, TT, D])
        st, mv, ve, rs = sb("st", [P, TT, 6]), sb("mv", [P, TT, 2]), sb("ve", [P, TT]), sb("rs", [P, TT])
        xnT_h, xnT_l = sb("xnT_h", [P, KD, S], F32R), sb("xnT_l", [P, KD, S], F32R)
        v = sb("v", [P, 2, S])
        xc = [sb(f"xc{i}", [P, KE, S]) for i in range(2)]
        xcr_h, xcr_l = sb("xcr_h", [P, 3, S], F32R), sb("xcr_l", [P, 3, S], F32R)
        zs = sb("zs", [P, KE, S])
        XT_h, XT_l = sb("XT_h", [P, TT, E], F32R), sb("XT_l", [P, TT, E], F32R)
        MTf, MT_h, MT_l = sb("MTf", [P, S + P]), sb("MT_h", [P, S + P], F32R), sb("MT_l", [P, S + P], F32R)
        t1, y2 = sb("t1", [P, 2, S]), sb("y2", [P, 2, S])
        y2_h, y2_l = sb("y2_h", [P, 2, S], F32R), sb("y2_l", [P, 2, S], F32R)
        dt_r, l_r, Bb, Cr, ab, gb = (sb(n, [N, S]) for n in ("dt_r", "l_r", "Bb", "Cr", "ab", "gb"))
        abar = sb("abar", [N, S])
        lam = sb("lam", [N, S + 1])
        EB, EC = sb("EB", [N, NI, P]), sb("EC", [N, S])
        rng, scl = sb("rng", [N, NB]), sb("scl", [N, 2])
        fl, flr, fls = sb("fl", [P, 3]), sb("flr", [P, 3]), sb("fls", [P, 2])
        flg = [sb(f"flg{i}", [P, 1], I32) for i in range(2)]
        hst, hcb, abc, xch = sb("hst", [P, N]), sb("hcb", [P, CL, N]), sb("abc", [P, 3, N, CL]), sb("xch", [P, CL])
        bxs = sb("bxs", [P, N])

        psT = [ctx.enter_context(nc.psum_tensor(f"a_psT{i}", [P, 512], F32)) for i in range(2)]
        psP = [ctx.enter_context(nc.psum_tensor(f"a_psP{i}", [P, 512], F32)) for i in range(3)]
        psX = ctx.enter_context(nc.psum_tensor("a_psX", [P, 512], F32))
        psO = [ctx.enter_context(nc.psum_tensor(f"a_psO{i}", [P, 512], F32)) for i in range(2)]

        w_ld = sem("w_ld")
        stg = [sem(f"stg{i}") for i in range(3)]
        stg_h, stg_l = sem("stg_h"), sem("stg_l")
        setup_pool, setup_dve, setup_act = sem("setup_pool"), sem("setup_dve"), sem("setup_act")
        x_ld = sem("x_ld")
        xres_ld, x1_st = sem("xres_ld"), sem("x1_st")
        ln, rstd = sem("ln"), sem("rstd")
        xn_tp, xnT_hi, xnT_lo = sem("xn_tp"), sem("xnT_hi"), sem("xnT_lo")
        x_mm, z_mm, y_mm, o_mm, xd_mm = sem("x_mm"), sem("z_mm"), sem("y_mm"), sem("o_mm"), sem("xd_mm")
        v_rdy, conv, xc_rdy, xc_hi, xc_lo = sem("v_rdy"), sem("conv"), sem("xc_rdy"), sem("xc_hi"), sem("xc_lo")
        z_rdy = sem("z_rdy")
        xt_tp, xt_hi, xt_lo = sem("xt_tp"), sem("xt_hi"), sem("xt_lo")
        m_mm, mt_f, mt_hi, mt_lo = sem("m_mm"), sem("mt_f"), sem("mt_hi"), sem("mt_lo")
        t1_rdy, t1_ok, y2_rdy, y2_hi, y2_lo, res = (sem(n) for n in ("t1_rdy", "t1_ok", "y2_rdy", "y2_hi", "y2_lo", "res"))
        rows_a, rows_b, rows_c, rows_d = sem("rows_a"), sem("rows_b"), sem("rows_c"), sem("rows_d")
        exps_a, exps_b = sem("exps_a"), sem("exps_b")
        bnd = sem("bnd")
        flag, flag_c, fb_dma = sem("flag"), sem("flag_c"), sem("fb_dma")

        passed_v = sem("passed_v")
        fb_range = range(fb_dma.num, fb_dma.num + 1)

        x_v = x.rearrange("b (t p) d -> b p t d", p=P)
        x1_v = x1.rearrange("b (t p) d -> b p t d", p=P)
        win_v = W_inT.rearrange("(k p) n -> k p n", p=P)
        wout_v = W_outT.rearrange("(c k p) n -> c p k n", p=P, k=4)
        place = [0, 1, 2, 0, 2, 2]
        early = [t[:].rearrange("p a b -> p (a b)") for t in (xc[0], xc[1], zs)]
        stage = [early[i] for i in place]
        chunks = [(win_h[:, k, :], win_l[:, k, :], win_v[k]) for k in range(KD)]
        chunks += [(wout_h[:, 4 * c:4 * c + 4, :].rearrange("p k n -> p (k n)"),
                    wout_l[:, 4 * c:4 * c + 4, :].rearrange("p k n -> p (k n)"), wout_v[c]) for c in range(KE // 4)]
        NCH = len(chunks)

        def run(body, eng, tail):
            body(0, 0, False, True)
            body(1, 1, True, True)
            with eng.Fori(0, B // 2 - 2) as i:
                body(i * 2 + 2, 0, True, True)
                body(i * 2 + 3, 1, True, True)
            body(B - 2, 0, True, True)
            body(B - 1, 1, True, True)
            body(B, 0, True, False)
            tail()

        block = ctx.enter_context(nc.Block())

        @block.sync
        def _(sp):
            sp.dma_start(xl[:], x_v[0]).then_inc(x_ld, 16)
            for c, (_, _, src) in enumerate(chunks):
                if place[c] in place[:c]:
                    before = max(i for i in range(c) if place[i] == place[c])
                    sp.wait_ge(stg_h, before + 1)
                    sp.wait_ge(stg_l, before + 1)
                dst = stage[c] if c < KD else stage[c].rearrange("p (k n) -> p k n", k=4)
                sp.dma_start(dst, src).then_inc(stg[place[c]], 16)
                if c == 0:
                    with nc.allow_non_contiguous_dma(reason="small parameters"):
                        sp.dma_start(wx_raw[:], W_xprojT.rearrange("(k p) n -> p k n", p=P)).then_inc(w_ld, 16)
                        sp.dma_start(cw[:], conv_w.rearrange("(k p) n -> p k n", p=P)).then_inc(w_ld, 16)
                        sp.dma_start(cb[:], conv_b.rearrange("(k p) -> p k", p=P)).then_inc(w_ld, 16)
                        sp.dma_start(dp[:], D_param.rearrange("(k p) -> p k", p=P)).then_inc(w_ld, 16)
                        sp.dma_start(a_log[:], A_log.rearrange("(k p) -> k p", p=1)).then_inc(w_ld, 16)

            def body(b, par, prev, cur):
                if cur and not (isinstance(b, int) and b == B - 1):
                    sp.wait_ge(ln, 7 * b + 7)
                    sp.dma_start(xl[:], x_v[b + 1]).then_inc(x_ld, 16)
                if prev:
                    wait(sp, x1_st, 16 * (b - 1))
                    sp.dma_start(xres[:], x_v[b - 1]).then_inc(xres_ld, 16)
                    sp.wait_ge(res, 2 * b)
                    sp.dma_start(x1_v[b - 1], xres[:]).then_inc(x1_st, 16)

            run(body, sp, lambda: sp.wait_ge(x1_st, 16 * B))

        @block.gpsimd
        def _(pool):
            g = nc.gpsimd
            g.memset(ident[:], 0.0).then_inc(setup_pool, 1)
            g.memset(mask[:], 1.0).then_inc(setup_pool, 1)
            g.memset(half[:], -0.5).then_inc(setup_pool, 1)
            g.memset(f32(wx_h[:]), 0.0).then_inc(setup_pool, 1)
            g.memset(f32(wx_l[:]), 0.0).then_inc(setup_pool, 1)
            pool.wait_ge(setup_pool, 5)
            g.affine_select(out=ident[:], in_=ident[:], compare_op=ALU.not_equal, fill=1.0, base=0,
                            pattern=[[-1, P]], channel_multiplier=1).then_inc(setup_pool, 1)
            g.affine_select(out=mask[:, 0:S], in_=mask[:, 0:S], compare_op=ALU.is_ge, fill=0.0, base=0,
                            pattern=[[1, S]], channel_multiplier=-1).then_inc(setup_pool, 1)
            g.affine_select(out=mask[:, S:S + P], in_=mask[:, S:S + P], compare_op=ALU.is_ge, fill=0.0, base=0,
                            pattern=[[1, P]], channel_multiplier=-1).then_inc(setup_pool, 1)

            def rsqrt(b):
                pool.wait_ge(ln, 7 * b + 5)
                g.tensor_tensor(rs[:], ve[:], half[:], ALU.pow).then_inc(rstd, 1)

            def recurrence(b, par, d):
                o = 1 - par
                g.memset(hst[:], 0.0)
                with pool.Fori(0, S // CL) as c:
                    pool.drain()
                    with nc.allow_non_contiguous_dma(reason="rows to all partitions"):
                        for r in range(3):
                            src = rows_dram[r].rearrange("(o n) t -> o n t", o=1)[:, :, bass.ds(c * CL, CL)].broadcast_to([P, N, CL])
                            pool.dma_start(abc[:, r], src).then_inc(fb_dma, 16)
                    pool.wait_ge(fb_dma, 48)
                    pool.dma_reset(fb_range)
                    pool.sem_clear(fb_dma)
                    g.tensor_copy(xch[:], xc[o][:, d, bass.ds(c * CL, CL)])
                    for t in range(CL):
                        pool.drain()
                        g.tensor_tensor(hst[:], hst[:], abc[:, 0, :, t], ALU.mult)
                        g.tensor_tensor(bxs[:], abc[:, 1, :, t], xch[:, t:t + 1].broadcast_to([P, N]), ALU.mult)
                        pool.drain()
                        g.tensor_tensor(hst[:], hst[:], bxs[:], ALU.add)
                        pool.drain()
                        g.tensor_scalar(hst[:], hst[:], 100.0, -100.0, ALU.min, ALU.max)
                        pool.drain()
                        g.tensor_tensor(hcb[:, t], hst[:], abc[:, 2, :, t], ALU.mult)
                    w = N
                    while w > 1:
                        w //= 2
                        pool.drain()
                        g.tensor_tensor(hcb[:, :, 0:w], hcb[:, :, 0:w], hcb[:, :, w:2 * w], ALU.add)
                    pool.drain()
                    g.tensor_tensor(t1[:, d % 2, bass.ds(c * CL, CL)], hcb[:, :, 0],
                                    zs[:, d, bass.ds(c * CL, CL)], ALU.mult)
                pool.drain()

            rsqrt(0)

            def body(b, par, prev, cur):
                if cur:
                    for i in range(KE):
                        pool.wait_ge(xc_hi, 8 * b + i + 1)
                        g.tensor_tensor(xcr_l[:, i % 3, :], xc[par][:, i, :], f32(xcr_h[:, i % 3, :]),
                                        ALU.subtract).then_inc(xc_lo, 1)
                if prev:
                    beyond = pool.value_load(flg[1 - par][0:1, 0:1])
                for d in range(KE):
                    if prev:
                        pool.wait_ge(t1_rdy, 8 * (b - 1) + d + 1)
                        pool.sem_inc(flag_c, 1)
                        with pool.If(beyond > 999):
                            recurrence(b, par, d)
                        pool.sem_inc(t1_ok, 1)
                    if d == 5 and cur and not (isinstance(b, int) and b == B - 1):
                        rsqrt(b + 1)
                if cur:
                    pool.wait_ge(flag, b + 1)
                    pool.sem_inc(flag_c, 1)
                    g.partition_all_reduce(flr[:], fl[:], P, RMAX)
                    pool.drain()
                    g.tensor_tensor(fls[:, 0:1], flr[:, 0:1], flr[:, 1:2], ALU.mult)
                    pool.drain()
                    g.tensor_scalar(fls[:, 1:2], fls[:, 0:1], flr[:, 2:3], 1000.0, ALU.max, ALU.mult)
                    pool.drain()
                    g.tensor_scalar(flg[par][:], fls[:, 1:2], 1.0e6, None, ALU.min)
                    pool.drain()
                    again = pool.value_load(flg[par][0:1, 0:1])
                    with pool.If(again > 999):
                        for r, row in enumerate((abar, Bb, Cr)):
                            pool.dma_start(rows_dram[r], row[:]).then_inc(fb_dma, 16)
                        pool.wait_ge(fb_dma, 48)
                        pool.dma_reset(fb_range)
                        pool.sem_clear(fb_dma)
                    pool.sem_inc(rows_d, 1)

            run(body, pool, lambda: None)

        @block.tensor
        def _(pe):
            def split_mm(out, hi_w, lo_w, hi_x, lo_x, first, last):
                pe.matmul(out, lo_w, hi_x, start=first, stop=False)
                pe.matmul(out, hi_w, lo_x, start=False, stop=False)
                return pe.matmul(out, hi_w, hi_x, start=False, stop=last)

            def turn_rows(b, h):
                pe.wait_ge(ln, 7 * b + 7)
                wait(pe, xt_lo, 4 * (b - 1) + 3 + h)
                for kk in range(2):
                    for t in range(TT):
                        mm = pe.transpose(psT[h][:, kk * S + t * P:kk * S + (t + 1) * P],
                                          xn[:, t, (2 * h + kk) * P:(2 * h + kk + 1) * P], ident[:])
                mm.then_inc(xn_tp, 1)

            pe.wait_ge(setup_pool, 8)
            pe.wait_ge(setup_dve, 1)
            for h in range(2):
                turn_rows(0, h)

            def body(b, par, prev, cur):
                def bank(n):
                    d = (n - 8) // 2
                    if n < 3:
                        wait(pe, z_rdy, 8 * (b - 1) + min(n + 7, 8))
                    elif n < 8:
                        pe.wait_ge(conv, 24 * b + 3 * (n - 3) + 3)
                    elif n % 2 == 0:
                        if not cur:
                            pe.wait_ge(z_rdy if d < 3 else t1_rdy, 8 * b if d < 3 else 8 * (b - 1) + d - 2)
                        elif d < 2:
                            pe.wait_ge(conv, 24 * b + 3 * (n - 3) + 3)
                        else:
                            pe.wait_ge(z_rdy, 8 * b + d - 1)
                    elif not prev:
                        pe.wait_ge(conv if d < 3 else z_rdy, 24 * b + 24 if d < 3 else 8 * b + d - 2)
                    elif d < 1:
                        pe.wait_ge(conv, 24 * b + 3 * (n - 3) + 3)
                    else:
                        pe.wait_ge(t1_rdy, 8 * (b - 1) + d)
                    return psP[n % 3]

                def in_proj(n, m, done):
                    ps = bank(n)
                    for kk in range(KD):
                        if isinstance(b, int) and b == 0 and m == 0:
                            pe.wait_ge(stg_h, kk + 1)
                            pe.wait_ge(stg_l, kk + 1)
                        c = slice(m * P, m * P + P)
                        mm = split_mm(ps[:, 0:S], win_h[:, kk, c], win_l[:, kk, c], xnT_h[:, kk, :], xnT_l[:, kk, :],
                                      kk == 0, kk == KD - 1)
                    mm.then_inc(done, 1)

                def x_dbl(i):
                    pe.wait_ge(xc_lo, 8 * b + i + 1)
                    if i == 0:
                        wait(pe, mt_f, b)
                        if isinstance(b, int) and b == 0:
                            pe.wait_ge(setup_dve, 3)
                    split_mm(psX[:, 0:S], wx_h[:, i, :], wx_l[:, i, :], xcr_h[:, i % 3, :], xcr_l[:, i % 3, :],
                             i == 0, i == KE - 1).then_inc(xd_mm, 1)

                if prev:
                    pe.wait_ge(rows_c, 2 * b)
                    for n in range(NI):
                        i = n if n < NB else n - NB + HB
                        c = i * BL if n < NB else S + (n - NB) * BL
                        mm = pe.matmul(psX[:, c:c + BL], EB[:, n, :], EC[:, i * BL:(i + 1) * BL], start=True, stop=True)
                    mm.then_inc(m_mm, 1)
                if cur:
                    pe.wait_ge(xnT_lo, 2 * b + 2)
                    for i in range(KE):
                        in_proj(i, i, x_mm)
                        if i >= 3:
                            x_dbl(i - 3)
                    x_dbl(KE - 3)
                if isinstance(b, int) and b == 1:
                    pe.wait_ge(stg_l, NCH)
                if prev:
                    pe.wait_ge(mt_lo, b)
                    pe.wait_ge(xt_lo, 4 * b)

                def out_proj(d):
                    pe.wait_ge(y2_lo, 8 * (b - 1) + d + 1)
                    if d == 0:
                        wait(pe, res, 2 * (b - 1))
                    for t in range(TT):
                        c = slice(t * P, t * P + P)
                        mm = split_mm(psO[t][:], y2_h[:, d % 2, c], y2_l[:, d % 2, c], wout_h[:, d, :], wout_l[:, d, :],
                                      d == 0, d == KE - 1)
                    mm.then_inc(o_mm, 1)

                def turn_x(j):
                    pe.wait_ge(xc_rdy, 8 * b + 2 * j + 2)
                    if j < 2:
                        pe.wait_ge(xnT_lo, 2 * b + j + 1)
                    else:
                        pe.wait_ge(xt_lo, 4 * b + j - 1)
                    for t in range(TT):
                        for i in range(2):
                            mm = pe.transpose(psT[j % 2][:, (2 * t + i) * P:(2 * t + i + 1) * P],
                                              xc[par][:, 2 * j + i, t * P:(t + 1) * P], ident[:])
                    mm.then_inc(xt_tp, 1)

                for d in range(KE):
                    if cur and d == 1:
                        x_dbl(KE - 1)
                    if prev:
                        ps = bank(8 + 2 * d)
                        c = slice(d * P, d * P + P)
                        split_mm(ps[:, 0:S], XT_h[:, 0, c], XT_l[:, 0, c], MT_h[:, 0:S], MT_l[:, 0:S], True, False)
                        split_mm(ps[:, P:S], XT_h[:, 1, c], XT_l[:, 1, c], MT_h[:, S:], MT_l[:, S:], False, True).then_inc(y_mm, 1)
                    if cur and d == 0:
                        x_dbl(KE - 2)
                    if cur:
                        in_proj(9 + 2 * d, KE + d, z_mm)
                    if prev and d >= 2:
                        out_proj(d - 2)
                    if cur and d % 2:
                        turn_x(d // 2)
                for h in range(2):
                    if prev:
                        out_proj(KE - 2 + h)
                    if cur and not (isinstance(b, int) and b == B - 1):
                        turn_rows(b + 1, h)

            run(body, pe, lambda: None)

        @block.scalar
        def _(act):
            def copy(out, in_, done):
                act.activation(out, in_, ACT.Copy).then_inc(done, 1)

            def weights_hi(c):
                act.wait_ge(stg[place[c]], 16 * place[:c + 1].count(place[c]))
                copy(chunks[c][0], stage[c], stg_h)

            for c in range(KD):
                weights_hi(c)
            act.wait_ge(w_ld, 80)
            act.activation(a_neg[:], a_log[:], ACT.Exp).then_inc(setup_act, 1)
            act.wait_ge(stg_l, KD)

            def body(b, par, prev, cur):
                def mt_hi_():
                    act.wait_ge(mt_f, b)
                    wait(act, y_mm, 8 * (b - 1))
                    copy(MT_h[:], MTf[:], mt_hi)

                if cur:
                    wait(act, z_mm, 8 * b)
                    for h in range(2):
                        act.wait_ge(xn_tp, 2 * b + h + 1)
                        copy(xnT_h[:, 2 * h:2 * h + 2, :], psT[h][:].rearrange("p (k s) -> p k s", k=2), xnT_hi)

                    def silu(i):
                        act.wait_ge(conv, 24 * b + 3 * i + 3)
                        if i == 0:
                            wait(act, y2_rdy, 8 * (b - 1))
                        act.activation(xc[par][:, i, :], v[:, i % 2, :], ACT.Silu).then_inc(xc_rdy, 1)
                        act.wait_ge(xc_rdy, 8 * b + i + 1)
                        wait(act, xd_mm, 8 * b + i - 2)
                        copy(xcr_h[:, i % 3, :], xc[par][:, i, :], xc_hi)

                    if prev:
                        mt_hi_()
                    for i in range(KE):
                        act.wait_ge(x_mm, 8 * b + i + 1)
                        wait(act, xc_rdy, 8 * b + i - 1)
                        act.activation(v[:, i % 2, :], psP[i % 3][:, 0:S], ACT.Identity,
                                       scale=cw[:, i, 3:4], bias=cb[:, i:i + 1]).then_inc(v_rdy, 1)
                        if i >= 1:
                            silu(i - 1)
                        if isinstance(b, int) and b == 0 and i in (2, 5):
                            weights_hi(KD + i // 3)
                    silu(KE - 1)
                    if isinstance(b, int) and b == 0:
                        act.wait_ge(stg_l, NCH)

                def y_hi(d):
                    act.wait_ge(y2_rdy, 8 * (b - 1) + d + 1)
                    wait(act, o_mm, 8 * (b - 1) + max(d - 1, 0))
                    copy(y2_h[:, d % 2, :], y2[:, d % 2, :], y2_hi)

                def xt_hi_(j):
                    act.wait_ge(xt_tp, 4 * b + j + 1)
                    copy(XT_h[:, :, 2 * j * P:(2 * j + 2) * P], psT[j % 2][:].rearrange("p (t s) -> p t s", t=TT), xt_hi)

                if prev and not cur:
                    mt_hi_()
                for d in range(KE):
                    if cur and d == 1:
                        act.wait_ge(rows_a, 3 * b + 3)
                        ch = Chain(act, exps_a, 2, b)
                        ch.did(act.activation(dt_r[:], dt_r[:], ACT.Exp))
                        ch.wait()
                        ch.did(act.activation(dt_r[:], dt_r[:], ACT.Ln, bias=1.0))
                    if cur and d == 5:
                        act.wait_ge(rows_b, 11 * b + 11)
                        act.activation(abar[:], l_r[:], ACT.Exp).then_inc(exps_b, 1)
                        act.activation(EB[:], EB[:], ACT.Exp, scale=-1.0).then_inc(exps_b, 1)
                        act.activation(EC[:], EC[:], ACT.Exp).then_inc(exps_b, 1)
                    if cur and d >= 2 and d % 2 == 0:
                        xt_hi_(d // 2 - 1)
                    if prev:
                        y_hi(d)
                    if cur:
                        act.wait_ge(z_mm, 8 * b + d + 1)
                        wait(act, t1_ok, 8 * (b - 1) + d + 1)
                        act.activation(zs[:, d, :], psP[(9 + 2 * d) % 3][:, 0:S], ACT.Silu).then_inc(z_rdy, 1)
                if cur:
                    xt_hi_(3)

            run(body, act, lambda: None)

        @block.vector
        def _(dve):
            def minus(out, a, b_, done):
                dve.tensor_tensor(out, a, b_, ALU.subtract).then_inc(done, 1)

            def moments(b):
                ch = Chain(dve, ln, 7, b)
                dve.wait_ge(x_ld, 16 * b + 16)
                for t in range(TT):
                    ch.did(dve.bn_stats(st[:, t, :], xl[:, t, :]))
                ch.wait()
                dve.sem_inc(passed_v, 1)
                for t in range(TT):
                    ch.did(dve.bn_aggr(mv[:, t, :], st[:, t, :]))
                ch.wait()
                ch.did(dve.tensor_scalar(ve[:], mv[:, :, 1], EPS, None, ALU.add))

            def normalize(b):
                wait(dve, xn_tp, 2 * b)
                dve.wait_ge(rstd, b + 1)
                for t in range(TT):
                    dve.tensor_scalar(xn[:, t, :], xl[:, t, :], mv[:, t, 0:1], rs[:, t:t + 1],
                                      ALU.subtract, ALU.mult).then_inc(ln, 1)

            dve.memset(ones_row[:], 1.0).then_inc(setup_dve, 1)
            dve.memset(lam[:, 0:1], 0.0).then_inc(setup_act, 1)
            dve.memset(fl[:], 0.0).then_inc(setup_act, 1)
            dve.memset(scl[:, 0:1], 0.01).then_inc(setup_act, 1)
            dve.memset(scl[:, 1:2], 1.0 / 60).then_inc(setup_act, 1)
            dve.wait_ge(setup_pool, 3)
            moments(0)
            normalize(0)
            def weights_lo(c):
                dve.wait_ge(stg_h, c + 1)
                minus(chunks[c][1], stage[c], f32(chunks[c][0]), stg_l)

            for c in range(KD):
                weights_lo(c)
                if c == 0:
                    dve.wait_ge(w_ld, 80)
                    dve.wait_ge(setup_pool, 5)
                    cols = [(wx_raw[:, :, 0:N], slice(0, N)), (wx_raw[:, :, N:2 * N], slice(32, 32 + N)),
                            (wx_raw[:, :, 2 * N:2 * N + 1].broadcast_to([P, KE, N]), slice(64, 64 + N))]
                    for src, at in cols:
                        ins = dve.tensor_copy(wx_h[:, :, at], src)
                    ins.then_inc(setup_dve, 1)
                    dve.wait_ge(setup_dve, 2)
                    for src, at in cols:
                        ins = dve.tensor_tensor(wx_l[:, :, at], src, f32(wx_h[:, :, at]), ALU.subtract)
                    ins.then_inc(setup_dve, 1)
            dve.wait_ge(setup_act, 5)
            dve.tensor_scalar(a_neg[:], a_neg[:], -1.0, None, ALU.mult).then_inc(setup_dve, 1)

            def body(b, par, prev, cur):
                first = isinstance(b, int) and b == 0
                if cur:
                    for h in range(2):
                        dve.wait_ge(xnT_hi, 2 * b + h + 1)
                        minus(xnT_l[:, 2 * h:2 * h + 2, :], psT[h][:].rearrange("p (k s) -> p k s", k=2),
                              f32(xnT_h[:, 2 * h:2 * h + 2, :]), xnT_lo)
                if prev:
                    dve.wait_ge(m_mm, b)
                    wait(dve, mt_lo, b - 1)
                    dve.tensor_tensor(MTf[:], psX[:, 0:S + P], mask[:], ALU.mult).then_inc(mt_f, 1)
                    dve.wait_ge(mt_hi, b)
                    minus(MT_l[:], MTf[:], f32(MT_h[:]), mt_lo)
                    if not (isinstance(b, int) and b == 1):
                        add_res(b - 2)
                if cur:
                    for i in range(KE):
                        dve.wait_ge(v_rdy, 8 * b + i + 1)
                        for j in range(1, 4):
                            dve.scalar_tensor_tensor(out=v[:, i % 2, j:S], in0=psP[i % 3][:, 0:S - j],
                                                     scalar=cw[:, i, 3 - j:4 - j], in1=v[:, i % 2, j:S],
                                                     op0=ALU.mult, op1=ALU.add).then_inc(conv, 1)
                            if j < 3:
                                dve.wait_ge(conv, 24 * b + 3 * i + j)
                        if first and i in (2, 5):
                            weights_lo(KD + i // 3)
                    if first:
                        dve.wait_ge(stg_l, NCH)

                def rows_1():
                    dve.wait_ge(xd_mm, 8 * b + 8)
                    wait(dve, rows_d, b)
                    wait(dve, m_mm, b)
                    dve.tensor_scalar(dt_r[:], psX[64:64 + N, 0:S], 5.0, None, ALU.min).then_inc(rows_a, 1)
                    dve.tensor_copy(Bb[:], psX[0:N, 0:S]).then_inc(rows_a, 1)
                    dve.tensor_copy(Cr[:], psX[32:32 + N, 0:S]).then_inc(rows_a, 1)

                def rows_2(part):
                    ch = Chain(dve, rows_b, 11, b)
                    ref = lam[:, 0:S].rearrange("n (i t) -> n i t", t=BL)
                    ends = lam[:, 1:S + 1].rearrange("n (i t) -> n i t", t=BL)
                    if part == 0:
                        if first:
                            dve.wait_ge(setup_dve, 4)
                        dve.wait_ge(exps_a, 2 * b + 2)
                        dve.wait_ge(rows_a, 3 * b + 3)
                        ch.did(dve.tensor_scalar(dt_r[:], dt_r[:], 0.001, 0.1, ALU.max, ALU.min))
                        ch.wait()
                        ch.did(dve.tensor_scalar(l_r[:], dt_r[:], a_neg[:, 0:1], -20.0, ALU.mult, ALU.max))
                        ch.did(dve.tensor_tensor(Bb[:], Bb[:], dt_r[:], ALU.mult))
                        ch.wait()
                        ch.did(dve.tensor_tensor_scan(lam[:, 1:S + 1], ones_row[:], l_r[:], 0.0, ALU.mult, ALU.add))
                        ch.did(dve.tensor_scalar(Bb[:], Bb[:], -10.0, 10.0, ALU.max, ALU.min))
                    elif part == 1:
                        ch.n = 5
                        ch.wait()
                        ch.did(dve.tensor_tensor(EB[:, 0:NB, :], lam[:, 1:P + 1].rearrange("n (o t) -> n o t", o=1).broadcast_to([N, NB, P]),
                                                 ref[:, :, 0:1].broadcast_to([N, NB, P]), ALU.subtract))
                        ch.did(dve.tensor_tensor(EB[:, NB:, :], lam[:, P + 1:].rearrange("n (o t) -> n o t", o=1).broadcast_to([N, NI - NB, P]),
                                                 ref[:, HB:, 0:1].broadcast_to([N, NI - NB, P]), ALU.subtract))
                    else:
                        ch.n = 7
                        ch.did(dve.tensor_tensor(EC[:].rearrange("n (i t) -> n i t", t=BL), ends,
                                                 ref[:, :, 0:1].broadcast_to([N, NB, BL]), ALU.subtract))
                        ch.did(dve.tensor_tensor(rng[:], ref[:, :, 0], ends[:, :, BL - 1], ALU.subtract))
                        ch.did(dve.scalar_tensor_tensor(out=ab[:], in0=Bb[:], scalar=-1.0, in1=Bb[:], op0=ALU.mult, op1=ALU.max))
                        ch.wait()
                        ch.did(dve.tensor_scalar(EB[:], EB[:], -60.0, None, ALU.max))

                def rows_3():
                    dve.wait_ge(exps_b, 3 * b + 3)
                    bb = Bb[:].rearrange("n (o t) -> n o t", t=P)
                    dve.tensor_tensor(EB[:, 0:NB, :], EB[:, 0:NB, :], bb[:, 0:1, :].broadcast_to([N, NB, P]), ALU.mult)
                    dve.tensor_tensor(EB[:, NB:, :], EB[:, NB:, :], bb[:, 1:2, :].broadcast_to([N, NI - NB, P]),
                                      ALU.mult).then_inc(rows_c, 1)
                    dve.tensor_tensor(EC[:], EC[:], Cr[:], ALU.mult).then_inc(rows_c, 1)

                def bounds(part):
                    ch = Chain(dve, bnd, 4, b)
                    if part == 0:
                        wait(dve, rows_d, b)
                        ch.did(dve.tensor_reduce(fl[:, 0:1], xc[par][:].rearrange("p a b -> p (a b)"), AX.X, ALU.max,
                                                 apply_absolute_value=True))
                    else:
                        ch.n = 1
                        ch.did(dve.tensor_tensor_scan(gb[:], abar[:], ab[:], 0.0, ALU.mult, ALU.add))
                        ch.did(dve.tensor_reduce(fl[0:N, 2:3], rng[:], AX.X, ALU.max))
                        ch.wait()
                        ch.did(dve.tensor_reduce(fl[0:N, 1:2], gb[:], AX.X, ALU.max))
                        ch.wait()
                        dve.tensor_tensor(fl[0:N, 1:3], fl[0:N, 1:3], scl[:], ALU.mult).then_inc(flag, 1)

                def t1_(d):
                    dve.wait_ge(y_mm, 8 * (b - 1) + d + 1)
                    if d == 0:
                        dve.wait_ge(z_rdy, 8 * b)
                    wait(dve, y2_rdy, 8 * (b - 1) + max(d - 1, 0))
                    dve.tensor_tensor(t1[:, d % 2, :], psP[(8 + 2 * d) % 3][:, 0:S], zs[:, d, :], ALU.mult).then_inc(t1_rdy, 1)

                def y2_(d):
                    dve.wait_ge(t1_ok, 8 * (b - 1) + d + 1)
                    wait(dve, y2_hi, 8 * (b - 1) + max(d - 1, 0))
                    wait(dve, y2_lo, 8 * (b - 1) + max(d - 1, 0))
                    dve.scalar_tensor_tensor(out=y2[:, d % 2, :], in0=xc[1 - par][:, d, :], scalar=dp[:, d:d + 1],
                                             in1=t1[:, d % 2, :], op0=ALU.mult, op1=ALU.add).then_inc(y2_rdy, 1)

                def y_lo(d):
                    dve.wait_ge(y2_hi, 8 * (b - 1) + d + 1)
                    minus(y2_l[:, d % 2, :], y2[:, d % 2, :], f32(y2_h[:, d % 2, :]), y2_lo)

                def xt_lo_(j):
                    dve.wait_ge(xt_hi, 4 * b + j + 1)
                    c = slice(2 * j * P, (2 * j + 2) * P)
                    minus(XT_l[:, :, c], psT[j % 2][:].rearrange("p (t s) -> p t s", t=TT), f32(XT_h[:, :, c]), xt_lo)

                more = cur and not (isinstance(b, int) and b == B - 1)
                for d in range(KE):
                    if prev:
                        t1_(d)
                        if d >= 1:
                            y_lo(d - 1)
                        y2_(d)
                    if cur:
                        if d == 0:
                            rows_1()
                        if d == 1:
                            bounds(0)
                        if d in (2, 3, 4):
                            rows_2(d - 2)
                        if d >= 2 and d % 2 == 0:
                            xt_lo_(d // 2 - 1)
                        if d == 5 and more:
                            moments(b + 1)
                        if d == 6:
                            rows_3()
                        if d == 7:
                            if more:
                                normalize(b + 1)
                if prev:
                    y_lo(KE - 1)
                if cur:
                    xt_lo_(3)
                if cur:
                    bounds(1)

            def add_res(b):
                dve.wait_ge(xres_ld, 16 * b + 16)
                dve.wait_ge(o_mm, 8 * b + 8)
                for t in range(TT):
                    dve.tensor_tensor(xres[:, t, :], psO[t][:], xres[:, t, :], ALU.add).then_inc(res, 1)

            run(body, dve, lambda: add_res(B - 1))


def attention_phase(nc, x1, ctxT, WqT, bq, WkT, bk, WvT, bv, WoT, bo, Wr, br, y, xn3_d, lg, qs_d, ks_d):
    B, S, _ = x1.shape
    H, DK = 16, 32
    TT = S // P
    G = P // DK
    U = 2 * KD
    NE = Wr.shape[1]
    SCALE = float(DK) ** -0.5
    with ExitStack() as ctx:
        def sb(name, shape, dt=F32):
            return ctx.enter_context(nc.sbuf_tensor("b_" + name, shape, dt))

        def sem(name):
            return ctx.enter_context(nc.semaphore("b_" + name))

        w_h = [sb(f"w_h{i}", [P, KD, D], F32R) for i in range(4)]
        w_l = [sb(f"w_l{i}", [P, KD, D], F32R) for i in range(4)]
        wr, brb = sb("wr", [P, KD, NE]), sb("brb", [P, NE])
        bqc, bkc, bvc, bob = sb("bqc", [P, KD]), sb("bkc", [P, KD]), sb("bvc", [P, KD]), sb("bob", [P, D])
        ident, half = sb("ident", [P, P]), sb("half", [P, TT])
        xa, xres, xn = sb("xa", [P, TT, D]), sb("xres", [P, TT, D]), sb("xn", [P, TT, D])
        xn3 = sb("xn3", [P, TT, D])
        st, mv, ve, rs = sb("st", [P, TT, 6]), sb("mv", [P, TT, 2]), sb("ve", [P, TT]), sb("rs", [P, TT])
        st3, mv3, ve3, rs3 = sb("st3", [P, TT, 6]), sb("mv3", [P, TT, 2]), sb("ve3", [P, TT]), sb("rs3", [P, TT])
        xnT_h, xnT_l = sb("xnT_h", [P, KD, S], F32R), sb("xnT_l", [P, KD, S], F32R)
        cx, cx_h, cx_l = sb("cx", [P, KD, S]), sb("cx_h", [P, KD, S], F32R), sb("cx_l", [P, KD, S], F32R)
        t_f = sb("t_f", [P, 2, S])
        t_h, t_l = sb("t_h", [P, 2, S], F32R), sb("t_l", [P, 2, S], F32R)
        qst = [sb(f"qst{i}", [3 * DK, H, S], F32R) for i in range(2)]
        kst = [sb(f"kst{i}", [3 * DK, H, S], F32R) for i in range(2)]
        V = [sb(f"V{i}", [P, TT, D]) for i in range(2)]
        pr = sb("pr", [P, 2, G, S])
        PT = sb("PT", [P, G, TT, S])
        mx, nm, rsum, rinv = sb("mx", [P, 2, G]), sb("nm", [P, 2, G]), sb("rsum", [P, 2, G]), sb("rinv", [P, 2, G])
        co_h, co_l = sb("co_h", [P, KD, S], F32R), sb("co_l", [P, KD, S], F32R)
        xn3T = xn[:].rearrange("p t d -> p (t d)").rearrange("p (k s) -> p k s", k=KD)

        psS = [ctx.enter_context(nc.psum_tensor(f"b_psS{i}", [P, G, S], F32)) for i in range(2)]
        psT = ctx.enter_context(nc.psum_tensor("b_psT", [P, 2 * G, P], F32))
        psV = ctx.enter_context(nc.psum_tensor("b_psV", [P, 512], F32))
        psQ = ctx.enter_context(nc.psum_tensor("b_psQ", [P, 512], F32))

        w_ld, p_ld, w_hi, w_lo = [sem(f"w_ld{i}") for i in range(2)], sem("p_ld"), sem("w_hi"), sem("w_lo")
        setup = sem("setup")
        xa_ld, xres_ld, cx_ld, x2_st, xn3_st = sem("xa_ld"), sem("xres_ld"), sem("cx_ld"), sem("x2_st"), sem("xn3_st")
        ln, rstd, ln3, rstd3 = sem("ln"), sem("rstd"), sem("ln3"), sem("rstd3")
        xn_tp, xnT_hi, xnT_lo = sem("xn_tp"), sem("xnT_hi"), sem("xnT_lo")
        cx_hi, cx_lo = sem("cx_hi"), sem("cx_lo")
        qk_mm, qk_f, qk_hi, qk_lo = sem("qk_mm"), sem("qk_f"), sem("qk_hi"), sem("qk_lo")
        tq_st, tk_st = [sem(f"tq_st{i}") for i in range(2)], [sem(f"tk_st{i}") for i in range(2)]
        q_ld, k_ld = sem("q_ld"), sem("k_ld")
        v_mm, v_cp = sem("v_mm"), sem("v_cp")
        s_mm, mx_s, nm_s, exp_s, ri_s, norm_s = (sem(n) for n in ("s_mm", "mx_s", "nm_s", "exp_s", "ri_s", "norm_s"))
        p_tp, pt_cp, pv_mm, co_hi, co_lo = (sem(n) for n in ("p_tp", "pt_cp", "pv_mm", "co_hi", "co_lo"))
        o_mm, x2_s, xb_s = sem("o_mm"), sem("x2_s"), sem("xb_s")
        r_tp, r_cp, r_mm, lg_s = sem("r_tp"), sem("r_cp"), sem("r_mm"), sem("lg_s")

        passed_v, passed_s, passed_p = sem("passed_v"), sem("passed_s"), sem("passed_p")

        x1_v = x1.rearrange("b (t p) d -> b p t d", p=P)
        y_v = y[0:B * S, :].rearrange("(b t p) d -> b p t d", p=P, t=TT)
        xn3_v = xn3_d[0:B * S, :].rearrange("(b t p) d -> b p t d", p=P, t=TT)
        ctx_v = ctxT.rearrange("b (k p) s -> b p k s", p=P)
        stage = [V[i] for i in range(2)]
        weights = (WqT, WkT, WvT, WoT)

        def run(body, eng):
            body(0, 0, True, False, False)
            body(1, 1, True, True, False)
            with eng.Fori(0, B // 2 - 2) as i:
                body(i * 2 + 2, 0, True, True, True)
                body(i * 2 + 3, 1, True, True, True)
            body(B - 2, 0, True, True, True)
            body(B - 1, 1, True, True, True)
            body(B, 0, False, True, True)
            body(B + 1, 1, False, False, True)

        def last(b):
            return isinstance(b, int) and b >= B - 1

        def first(b):
            return isinstance(b, int) and b == 0

        block = ctx.enter_context(nc.Block())

        @block.sync
        def _(sp):
            sp.dma_start(xa[:], x1_v[0]).then_inc(xa_ld, 16)
            sp.dma_start(cx[:], ctx_v[0]).then_inc(cx_ld, 16)
            with nc.allow_non_contiguous_dma(reason="small parameters"):
                for col, src in ((bqc, bq), (bkc, bk), (bvc, bv)):
                    sp.dma_start(col[:], src.rearrange("(k p) -> p k", p=P)).then_inc(p_ld, 16)
                sp.dma_start(wr[:], Wr.rearrange("(k p) n -> p k n", p=P)).then_inc(p_ld, 16)
                sp.dma_start(bob[:], bo.rearrange("(o n) -> o n", o=1).broadcast_to([P, D])).then_inc(p_ld, 16)
                sp.dma_start(brb[:], br.rearrange("(o n) -> o n", o=1).broadcast_to([P, NE])).then_inc(p_ld, 16)
            for c in range(8):
                if c >= 2:
                    sp.wait_ge(w_hi, c - 1)
                    sp.wait_ge(w_lo, c - 1)
                src = weights[c // 2].rearrange("(k p) n -> p k n", p=P)[:, 2 * (c % 2):2 * (c % 2) + 2, :]
                sp.dma_start(stage[c % 2][:], src).then_inc(w_ld[c % 2], 16)

            def body(b, par, cur, prev, prev2):
                def store(scratch, st_, first):
                    for i in range(KD):
                        sp.wait_ge(qk_lo, U * b + first + i + 1)
                        for part, t in enumerate((t_h, t_l)):
                            sp.dma_start(f32(scratch[part, i * P:(i + 1) * P, :]), f32(t[:, (first + i) % 2, :])).then_inc(st_[i % 2], 16)

                def load(scratch, st_, ld, stack, parts):
                    for p_ in range(2):
                        sp.wait_ge(st_[p_], 64 * b + 64)
                        sp.sem_inc(passed_s, 1)
                    wait(sp, s_mm, U * (b - 1))
                    for r, part in enumerate(parts):
                        sp.dma_start(f32(stack[r * DK:(r + 1) * DK, :, :]),
                                     f32(scratch[part].rearrange("(h d) s -> d h s", d=DK))).then_inc(ld, 16)

                if cur and not last(b):
                    sp.wait_ge(ln, 7 * b + 7)
                    sp.dma_start(xa[:], x1_v[b + 1]).then_inc(xa_ld, 16)
                if cur:
                    wait(sp, q_ld, 48 * b)
                    sp.sem_inc(passed_s, 1)
                    store(qs_d, tq_st, 0)
                if prev2:
                    sp.wait_ge(ln3, 7 * (b - 1))
                    sp.dma_start(xn3_v[b - 2], xn3[:]).then_inc(xn3_st, 16)
                if prev:
                    wait(sp, x2_st, 16 * (b - 1))
                    sp.dma_start(xres[:], x1_v[b - 1]).then_inc(xres_ld, 16)
                if cur:
                    load(qs_d, tq_st, q_ld, qst[par], (0, 1, 0))
                    if not last(b):
                        sp.wait_ge(cx_lo, KD * b + KD)
                        sp.dma_start(cx[:], ctx_v[b + 1]).then_inc(cx_ld, 16)
                    wait(sp, k_ld, 48 * b)
                    sp.sem_inc(passed_s, 1)
                    store(ks_d, tk_st, KD)
                    load(ks_d, tk_st, k_ld, kst[par], (0, 0, 1))
                if prev:
                    sp.wait_ge(x2_s, 2 * b)
                    sp.dma_start(y_v[b - 1], xres[:]).then_inc(x2_st, 16)

            run(body, sp)
            sp.wait_ge(x2_st, 16 * B)
            sp.wait_ge(xn3_st, 16 * B)

        @block.gpsimd
        def _(pool):
            g = nc.gpsimd
            g.memset(ident[:], 0.0).then_inc(setup, 1)
            g.memset(half[:], -0.5).then_inc(setup, 1)
            pool.wait_ge(setup, 2)
            g.affine_select(out=ident[:], in_=ident[:], compare_op=ALU.not_equal, fill=1.0, base=0,
                            pattern=[[-1, P]], channel_multiplier=1).then_inc(setup, 1)

            def rsqrt(b, ln_, ve_, rs_, done):
                pool.wait_ge(ln_, 7 * b + 5)
                g.tensor_tensor(rs_[:], ve_[:], half[:], ALU.pow).then_inc(done, 1)

            rsqrt(0, ln, ve, rs, rstd)

            def cx_parts(b):
                wait(pool, v_mm, 2 * b)
                pool.wait_ge(cx_ld, 16 * b + 16)
                for k in range(KD):
                    pool.sem_inc(passed_p, 1)
                    g.tensor_copy(cx_h[:, k, :], cx[:, k, :]).then_inc(cx_hi, 1)
                    pool.wait_ge(cx_hi, KD * b + k + 1)
                    g.tensor_tensor(cx_l[:, k, :], cx[:, k, :], f32(cx_h[:, k, :]), ALU.subtract).then_inc(cx_lo, 1)

            cx_parts(0)

            def body(b, par, cur, prev, prev2):
                if prev2:
                    rsqrt(b - 2, ln3, ve3, rs3, rstd3)

                def qk_parts(i):
                    n, m = i // KD, i % KD
                    pool.wait_ge(qk_f, U * b + i + 1)
                    pool.sem_inc(passed_p, 1)
                    if m >= 2:
                        pool.wait_ge((tq_st, tk_st)[n][m % 2], 64 * b + 32)
                    elif n == 1:
                        pool.wait_ge(tq_st[m % 2], 64 * b + 64)
                    else:
                        wait(pool, tk_st[m % 2], 64 * b)
                    pool.sem_inc(passed_p, 1)
                    g.tensor_copy(t_h[:, i % 2, :], t_f[:, i % 2, :]).then_inc(qk_hi, 1)
                    pool.wait_ge(qk_hi, U * b + i + 1)
                    g.tensor_tensor(t_l[:, i % 2, :], t_f[:, i % 2, :], f32(t_h[:, i % 2, :]), ALU.subtract).then_inc(qk_lo, 1)

                for u in range(U):
                    if cur:
                        qk_parts(u)
                    if prev and u == 4:
                        pool.wait_ge(xres_ld, 16 * b)
                        if isinstance(b, int) and b == 1:
                            pool.wait_ge(p_ld, 96)
                        for t in range(TT):
                            g.tensor_tensor(xres[:, t, :], xres[:, t, :], bob[:], ALU.add).then_inc(xb_s, 1)
                    if cur and u == 6 and not last(b):
                        rsqrt(b + 1, ln, ve, rs, rstd)
                if cur and not last(b):
                    cx_parts(b + 1)

            run(body, pool)

        @block.tensor
        def _(pe):
            def split_mm(out, hi_w, lo_w, hi_x, lo_x, first, last_):
                pe.matmul(out, lo_w, hi_x, start=first, stop=False)
                pe.matmul(out, hi_w, lo_x, start=False, stop=False)
                return pe.matmul(out, hi_w, hi_x, start=False, stop=last_)

            def turn_xn(b):
                pe.wait_ge(ln, 7 * b + 7)
                wait(pe, pt_cp, U * (b - 1))
                for kk in range(KD):
                    for t in range(TT):
                        mm = pe.transpose(psT[:, 2 * kk + t, :], xn[:, t, kk * P:(kk + 1) * P], ident[:])
                mm.then_inc(xn_tp, 1)

            pe.wait_ge(setup, 3)
            turn_xn(0)

            def body(b, par, cur, prev, prev2):
                o = 1 - par

                def qk_tile(i):
                    m = i % KD
                    if first(b) and m == 0:
                        pe.wait_ge(w_lo, 2 + 2 * (i // KD))
                    if i:
                        pe.wait_ge(qk_f, U * b + i)
                        if i == 6 and prev2:
                            pe.wait_ge(lg_s, b - 1)
                    else:
                        wait(pe, x2_s, 2 * (b - 1) - 1)
                        wait(pe, v_cp, 2 * b)
                        pe.wait_ge(xnT_lo, b + 1)
                    if i == KD:
                        pe.wait_ge(cx_lo, KD * b + KD)
                    n = i // KD
                    xh, xl = (xnT_h, xnT_l) if n == 0 else (cx_h, cx_l)
                    for kk in range(KD):
                        c = slice(m * P, m * P + P)
                        mm = split_mm(psQ[:, 0:S], w_h[n][:, kk, c], w_l[n][:, kk, c], xh[:, kk, :], xl[:, kk, :],
                                      kk == 0, kk == KD - 1)
                    mm.then_inc(qk_mm, 1)

                def v_tile(t):
                    if first(b) and t == 0:
                        pe.wait_ge(w_lo, 6)
                    if t:
                        pe.wait_ge(v_cp, 2 * b + 1)
                    else:
                        pe.wait_ge(qk_f, U * b + U)
                    c = slice(t * P, t * P + P)
                    for kk in range(KD):
                        mm = split_mm(psQ[:], cx_h[:, kk, c], cx_l[:, kk, c], w_h[2][:, kk, :], w_l[2][:, kk, :],
                                      kk == 0, kk == KD - 1)
                    mm.then_inc(v_mm, 1)

                def scores(hb, u):
                    j, qt = u // TT, u % TT
                    stack = o if hb is not b else par
                    wait(pe, exp_s, 4 * (U * hb + u - 1))
                    if u == 0:
                        pe.wait_ge(q_ld, 48 * hb + 48)
                        pe.wait_ge(k_ld, 48 * hb + 48)
                    for h in range(G):
                        mm = pe.matmul(psS[u % 2][:, h, :], qst[stack][:, G * j + h, qt * P:(qt + 1) * P],
                                       kst[stack][:, G * j + h, :], start=True, stop=True)
                    mm.then_inc(s_mm, 1)

                def turn_p(u):
                    pe.wait_ge(norm_s, U * (b - 1) + u + 1)
                    if u:
                        pe.wait_ge(pt_cp, U * (b - 1) + u)
                        if u == 3 and prev2:
                            pe.wait_ge(r_cp, b - 1)
                    else:
                        pe.wait_ge(xnT_lo, b + 1 if cur else b)
                    for h in range(G):
                        for kt in range(TT):
                            mm = pe.transpose(psT[:, 2 * h + kt, :], pr[:, u % 2, h, kt * P:(kt + 1) * P], ident[:])
                    mm.then_inc(p_tp, 1)

                def pv(j):
                    pe.wait_ge(pt_cp, U * (b - 1) + 2 * j + 2)
                    wait(pe, co_lo, 4 * (b - 1) + j)
                    if j == 0:
                        pe.wait_ge(v_cp, 2 * b)
                        wait(pe, x2_s, 2 * (b - 1))
                    for kt in range(TT):
                        for h in range(G):
                            c = slice((G * j + h) * DK, (G * j + h + 1) * DK)
                            mm = pe.matmul(psV[h * DK:(h + 1) * DK, 0:S], V[o][:, kt, c], PT[:, h, kt, :],
                                           start=kt == 0, stop=kt == TT - 1)
                    mm.then_inc(pv_mm, 1)

                def turn_rows():
                    pe.wait_ge(ln3, 7 * (b - 1))
                    wait(pe, pt_cp, U * (b - 1) + 3 if prev else U * (b - 1))
                    for kk in range(KD):
                        for t in range(TT):
                            mm = pe.transpose(psT[:, 2 * kk + t, :], xn3[:, t, kk * P:(kk + 1) * P], ident[:])
                    mm.then_inc(r_tp, 1)

                def logits():
                    pe.wait_ge(r_cp, b - 1)
                    pe.wait_ge(x2_s, 2 * (b - 1))
                    if cur:
                        pe.wait_ge(qk_f, U * b + 6)
                    for t in range(TT):
                        for kk in range(KD):
                            mm = pe.matmul(psQ[:, t * NE:(t + 1) * NE], xn3T[:, kk, t * P:(t + 1) * P], wr[:, kk, :],
                                           start=kk == 0, stop=kk == KD - 1)
                    mm.then_inc(r_mm, 1)

                for u in range(U):
                    if prev and 1 <= u < U - 1:
                        scores(b - 1, u + 1)
                    if cur:
                        qk_tile(u)
                    if prev2 and u == 4:
                        turn_rows()
                    if prev and u:
                        turn_p(u - 1)
                    if prev and u >= 3 and u % 2:
                        pv((u - 3) // 2)
                    if prev2 and u == 5:
                        logits()
                if cur:
                    v_tile(0)
                if prev:
                    turn_p(U - 1)
                if cur:
                    v_tile(1)
                if prev:
                    pv(KD - 1)
                if cur and not last(b):
                    turn_xn(b + 1)
                if isinstance(b, int) and b == 1:
                    pe.wait_ge(w_lo, 8)
                for t, ps in enumerate((psQ, psV)):
                    if prev:
                        pe.wait_ge(co_lo, 4 * b)
                        if t == 0 and cur:
                            pe.wait_ge(v_cp, 2 * b + 2)
                        elif t == 0:
                            pe.wait_ge(lg_s, b - 1)
                        c = slice(t * P, t * P + P)
                        for kk in range(KD):
                            mm = split_mm(ps[:], co_h[:, kk, c], co_l[:, kk, c], w_h[3][:, kk, :], w_l[3][:, kk, :],
                                          kk == 0, kk == KD - 1)
                        mm.then_inc(o_mm, 1)
                    if cur:
                        scores(b, t)

            run(body, pe)

        @block.scalar
        def _(act):
            def copy(out, in_, done):
                act.activation(out, in_, ACT.Copy).then_inc(done, 1)

            def weights_hi(c):
                act.wait_ge(w_ld[c % 2], 16 * (c // 2 + 1))
                copy(w_h[c // 2][:, 2 * (c % 2):2 * (c % 2) + 2, :], stage[c % 2][:], w_hi)

            for c in range(2):
                weights_hi(c)

            def split_xn(b):
                act.wait_ge(xn_tp, b + 1)
                wait(act, qk_mm, U * (b - 1) + 4)
                copy(xnT_h[:], psT[:].rearrange("p (k t) s -> p k (t s)", t=TT), xnT_hi)

            split_xn(0)
            act.wait_ge(p_ld, 96)

            def body(b, par, cur, prev, prev2):
                o = 1 - par

                def qk_copy(i):
                    act.wait_ge(qk_mm, U * b + i + 1)
                    wait(act, qk_lo, U * b + i - 1)
                    act.activation(t_f[:, i % 2, :], psQ[:, 0:S], ACT.Identity,
                                   bias=(bqc, bkc)[i // KD][:, i % KD:i % KD + 1]).then_inc(qk_f, 1)

                def exps(hb, u):
                    act.wait_ge(nm_s, U * hb + u + 1)
                    wait(act, p_tp, U * hb + u - 1)
                    wait(act, norm_s, U * hb + u - 1)
                    for h in range(G):
                        act.activation(pr[:, u % 2, h, :], psS[u % 2][:, h, :], ACT.Exp, bias=nm[:, u % 2, h:h + 1],
                                       scale=SCALE, accum_out=rsum[:, u % 2, h:h + 1]).then_inc(exp_s, 1)

                def pt_copy(u):
                    act.wait_ge(p_tp, U * (b - 1) + u + 1)
                    if u % 2 == 0:
                        wait(act, pv_mm, 4 * (b - 1) + u // 2)
                    c = slice((u % 2) * P, (u % 2) * P + P)
                    copy(PT[:, :, :, c], psT[:].rearrange("p (h k) s -> p h k s", k=TT), pt_cp)

                def ctx_hi(j):
                    act.wait_ge(pv_mm, 4 * (b - 1) + j + 1)
                    wait(act, o_mm, 2 * (b - 1))
                    act.activation(co_h[:, j, :], psV[:, 0:S], ACT.Identity, bias=bvc[:, j:j + 1]).then_inc(co_hi, 1)

                def v_copy(t):
                    if first(b) and t == 0:
                        act.wait_ge(w_lo, 8)
                    act.wait_ge(v_mm, 2 * b + t + 1)
                    wait(act, pv_mm, 4 * (b - 1))
                    copy(V[par][:, t, :], psQ[:], v_cp)

                for u in range(U):
                    if prev and u:
                        exps(b - 1, u)
                    if cur:
                        qk_copy(u)
                    if first(b) and u < 3:
                        weights_hi(2 * u + 2)
                        weights_hi(2 * u + 3)
                    if prev2 and u == 4:
                        act.wait_ge(r_tp, b - 1)
                        copy(xn3T, psT[:].rearrange("p (k t) s -> p k (t s)", t=TT), r_cp)
                    if prev and u:
                        pt_copy(u - 1)
                    if prev and u >= 3 and u % 2:
                        ctx_hi((u - 3) // 2)
                if cur:
                    v_copy(0)
                if prev:
                    pt_copy(U - 1)
                if cur:
                    v_copy(1)
                if prev:
                    ctx_hi(KD - 1)
                if cur and not last(b):
                    split_xn(b + 1)
                if cur:
                    exps(b, 0)

            run(body, act)

        @block.vector
        def _(dve):
            def minus(out, a, b_, done):
                dve.tensor_tensor(out, a, b_, ALU.subtract).then_inc(done, 1)

            def stats(b, sem_, src, st, t):
                dve.bn_stats(st[:, t, :], src[:, t, :]).then_inc(sem_, 1)

            def moments(b, sem_, st, mv, ve):
                ch = Chain(dve, sem_, 7, b)
                ch.n = 2
                ch.wait()
                dve.sem_inc(passed_v, 1)
                for t in range(TT):
                    ch.did(dve.bn_aggr(mv[:, t, :], st[:, t, :]))
                ch.wait()
                ch.did(dve.tensor_scalar(ve[:], mv[:, :, 1], EPS, None, ALU.add))

            def normalize(b, sem_, src, mv, rs, rstd, out):
                dve.wait_ge(rstd, b + 1)
                for t in range(TT):
                    dve.tensor_scalar(out[:, t, :], src[:, t, :], mv[:, t, 0:1], rs[:, t:t + 1],
                                      ALU.subtract, ALU.mult).then_inc(sem_, 1)

            def split_xn(b):
                dve.wait_ge(xnT_hi, b + 1)
                minus(xnT_l[:], psT[:].rearrange("p (k t) s -> p k (t s)", t=TT), f32(xnT_h[:]), xnT_lo)

            dve.wait_ge(xa_ld, 16)
            for t in range(TT):
                stats(0, ln, xa, st, t)
            moments(0, ln, st, mv, ve)
            normalize(0, ln, xa, mv, rs, rstd, xn)
            def weights_lo(c):
                dve.wait_ge(w_hi, c + 1)
                minus(w_l[c // 2][:, 2 * (c % 2):2 * (c % 2) + 2, :], stage[c % 2][:],
                      f32(w_h[c // 2][:, 2 * (c % 2):2 * (c % 2) + 2, :]), w_lo)
            for c in range(2):
                weights_lo(c)
            split_xn(0)
            dve.wait_ge(p_ld, 96)

            def body(b, par, cur, prev, prev2):
                o = 1 - par

                def row_max(hb, u):
                    n = U * hb + u
                    dve.wait_ge(s_mm, n + 1)
                    wait(dve, exp_s, 4 * (n - 1))
                    wait(dve, nm_s, n - 1)
                    dve.tensor_reduce(mx[:, u % 2, :], psS[u % 2][:], AX.X, ALU.max).then_inc(mx_s, 1)
                    dve.wait_ge(mx_s, n + 1)
                    dve.tensor_scalar(nm[:, u % 2, :], mx[:, u % 2, :], -SCALE, None, ALU.mult).then_inc(nm_s, 1)

                def norm(u):
                    n = U * (b - 1) + u
                    dve.wait_ge(exp_s, 4 * (n + 1))
                    wait(dve, norm_s, n - 1)
                    dve.reciprocal(rinv[:, u % 2, :], rsum[:, u % 2, :]).then_inc(ri_s, 1)
                    dve.wait_ge(ri_s, n + 1)
                    for h in range(G):
                        ins = dve.tensor_scalar(pr[:, u % 2, h, :], pr[:, u % 2, h, :], rinv[:, u % 2, h:h + 1], None, ALU.mult)
                    ins.then_inc(norm_s, 1)

                def ctx_lo(j):
                    dve.wait_ge(co_hi, 4 * (b - 1) + j + 1)
                    dve.scalar_tensor_tensor(out=co_l[:, j, :], in0=psV[:, 0:S], scalar=bvc[:, j:j + 1],
                                             in1=f32(co_h[:, j, :]), op0=ALU.add, op1=ALU.subtract).then_inc(co_lo, 1)

                more = cur and not last(b)
                for u in range(U):
                    if first(b) and u < 3:
                        weights_lo(2 * u + 2)
                        weights_lo(2 * u + 3)
                    if prev and 1 <= u < U - 1:
                        row_max(b - 1, u + 1)
                    if prev:
                        norm(u)
                    if prev and u >= 3 and u % 2:
                        ctx_lo((u - 3) // 2)
                    if u == 1 and prev2:
                        normalize(b - 2, ln3, xres, mv3, rs3, rstd3, xn3)
                    if u == 5 and prev2:
                        dve.wait_ge(r_mm, b - 1)
                        for t in range(TT):
                            ins = dve.tensor_tensor(lg[:, bass.ds((b * TT + (t - 2 * TT)) * NE, NE)],
                                                    psQ[:, t * NE:(t + 1) * NE], brb[:], ALU.add)
                        ins.then_inc(lg_s, 1)
                    if u == 4 and more:
                        dve.wait_ge(xa_ld, 16 * b + 32)
                        stats(b + 1, ln, xa, st, 0)
                    if u == 5 and more:
                        stats(b + 1, ln, xa, st, 1)
                    if u == 6 and more:
                        moments(b + 1, ln, st, mv, ve)
                    if u == 7 and more:
                        dve.wait_ge(xn_tp, b + 1)
                        wait(dve, r_mm, b - 1)
                        normalize(b + 1, ln, xa, mv, rs, rstd, xn)
                if prev:
                    ctx_lo(KD - 1)
                if more:
                    split_xn(b + 1)
                if prev2:
                    dve.wait_ge(xn3_st, 16 * (b - 1))
                for t, ps in enumerate((psQ, psV)):
                    if prev:
                        dve.wait_ge(o_mm, 2 * (b - 1) + t + 1)
                        dve.wait_ge(xb_s, 2 * b)
                        dve.tensor_tensor(xres[:, t, :], ps[:], xres[:, t, :], ALU.add).then_inc(x2_s, 1)
                    if cur:
                        row_max(b, t)
                if prev:
                    dve.wait_ge(x2_s, 2 * b)
                    for t in range(TT):
                        stats(b - 1, ln3, xres, st3, t)
                    moments(b - 1, ln3, st3, mv3, ve3)

            run(body, dve)


CAPACITY = 1.2


def routing_phase(nc, lg, list_d, idx, pay, y, xn3_d, n_tok, NE):
    T = n_tok // P
    cap = -(-int(CAPACITY * 10) * n_tok // (10 * NE))
    R = next(r for r in range(P, 0, -1) if cap % r == 0)
    NG = NE * cap // R
    W = T * NE
    DIG = 3
    ROUNDS = 10
    NC = 1 << DIG
    NH = P // (NE * NC)
    TH = T // NH
    GRP = NC * NH
    BIG = 1.0e5
    with ExitStack() as ctx:
        def sb(name, shape, dt=F32):
            return ctx.enter_context(nc.sbuf_tensor("c_" + name, shape, dt))

        def sem(name):
            return ctx.enter_context(nc.semaphore("c_" + name))

        te = [P, T, NE]
        ex, pb, eq, tmp, sel1, sel2, p2 = (sb(n, te) for n in ("ex", "pb", "eq", "tmp", "sel1", "sel2", "p2"))
        m, s, r, g1, g2, i1 = (sb(n, [P, T]) for n in ("m", "s", "r", "g1", "g2", "i1"))
        gate = sb("gate", [P, NE, T])
        ge, gt, tie, sel, pos, cum, slot = (sb(n, [P, NE, T]) for n in ("ge", "gt", "tie", "sel", "pos", "cum", "slot"))
        ione, iof = sb("ione", [P, NE], I32), sb("iof", [P, NE])
        tok = sb("tok", [P, T], I32)
        sl = sb("sl", [P, 2, T])
        thr, hi_i, lo_i = (sb(n, [P, NE], I32) for n in ("thr", "hi_i", "lo_i"))
        chan, cnd, th1, cand1, dig, part_i = (sb(n, [P, 1], I32) for n in ("chan", "cnd", "th1", "cand1", "dig", "part_i"))
        cnt1, keep1, part_f = (sb(n, [P, 1]) for n in ("cnt1", "keep1", "part_f"))
        copies, reach = sb("copies", [P, TH, P]), sb("reach", [P, TH * P])
        pairs, groups = sb("pairs", [P, P]), sb("groups", [P, P])
        first_of, parts = sb("first_of", [P, NE]), sb("parts", [P, 2, NE])
        cnt, need, base = sb("cnt", [P, NE]), sb("need", [P, NE]), sb("base", [P, NE])
        ones, below = sb("ones", [P, P]), sb("below", [P, P])
        one_w = sb("one_w", [P, W])
        fill, fill_id = sb("fill", [P, NG, 2]), sb("fill_id", [P, NG], I32)
        zero = sb("zero", [P, D])
        ident = sb("ident", [P, P])
        psG = ctx.enter_context(nc.psum_tensor("c_psG", [P, TH * P], F32))
        psC = ctx.enter_context(nc.psum_tensor("c_psC", [P, 2 * NE], F32))
        psD = ctx.enter_context(nc.psum_tensor("c_psD", [P, 1], F32))
        psA = ctx.enter_context(nc.psum_tensor("c_psA", [P, NE, T], F32))
        psB = ctx.enter_context(nc.psum_tensor("c_psB", [P, NE, T], F32))

        made, made_v, zero_st, fill_st = sem("made"), sem("made_v"), sem("zero_st"), sem("fill_st")
        ch_s, exp_s, cnt_s, sum_s = sem("ch"), sem("exp"), sem("cnt"), sem("sum")
        cn_s, kp_s, th_s = sem("cn"), sem("kp"), sem("th")
        pre_s, mm_s = sem("pre"), sem("mm")
        gate_s, gt_mm, pr_mm, gr_mm, th_mm = sem("gate"), sem("gt_mm"), sem("pr_mm"), sem("gr_mm"), sem("th_mm")

        MADE = 19
        block = ctx.enter_context(nc.Block())

        @block.gpsimd
        def _(pool):
            g = nc.gpsimd
            g.iota(ione[:], [[1, NE]], base=0, channel_multiplier=0).then_inc(made, 1)
            g.iota(tok[:], [[P, T]], base=0, channel_multiplier=1).then_inc(made, 1)
            g.iota(fill_id[:], [[0, NG]], base=n_tok, channel_multiplier=1).then_inc(made, 1)
            g.memset(ones[:], 1.0).then_inc(made, 1)
            g.memset(below[:], 1.0).then_inc(made, 1)
            g.memset(zero[:], 0.0).then_inc(made, 1)
            g.memset(fill[:], 0.0).then_inc(made, 1)
            g.iota(chan[:], [[1, 1]], base=0, channel_multiplier=1).then_inc(made, 1)
            g.memset(pairs[:], 1.0).then_inc(made, 1)
            g.memset(groups[:], 1.0).then_inc(made, 1)
            g.memset(ident[:], 0.0).then_inc(made, 1)
            g.memset(first_of[:], 0.0).then_inc(made, 1)
            pool.wait_ge(made, 12)
            for m, n in ((pairs, NH), (groups, GRP)):
                v = m[:].rearrange("p (a b) -> p a b", b=n)
                g.affine_select(out=v, in_=v, compare_op=ALU.is_ge, fill=0.0, base=0,
                                pattern=[[-n, P // n], [0, n]], channel_multiplier=1).then_inc(made, 1)
            pool.wait_ge(made, 14)
            for m, n in ((pairs, NH), (groups, GRP)):
                v = m[:].rearrange("p (a b) -> p a b", b=n)
                g.affine_select(out=v, in_=v, compare_op=ALU.is_ge, fill=0.0, base=n - 1,
                                pattern=[[n, P // n], [0, n]], channel_multiplier=-1).then_inc(made, 1)
            g.affine_select(out=ident[:], in_=ident[:], compare_op=ALU.not_equal, fill=1.0, base=0,
                            pattern=[[-1, P]], channel_multiplier=1).then_inc(made, 1)
            g.affine_select(out=first_of[:], in_=first_of[:], compare_op=ALU.not_equal, fill=1.0, base=0,
                            pattern=[[-GRP, NE]], channel_multiplier=1).then_inc(made, 1)
            g.affine_select(out=below[:], in_=below[:], compare_op=ALU.is_gt, fill=0.0, base=0,
                            pattern=[[1, P]], channel_multiplier=-1).then_inc(made, 1)

        @block.sync
        def _(sp):
            sp.wait_ge(made, MADE)
            sp.dma_start(y[n_tok:n_tok + P, :], zero[:]).then_inc(zero_st, 16)
            sp.dma_start(xn3_d[n_tok:n_tok + P, :], zero[:]).then_inc(zero_st, 16)
            sp.wait_ge(made_v, 1)
            with nc.allow_non_contiguous_dma(reason="the lists' rows"):
                sp.dma_start(list_d.rearrange("(g r) c -> r g c", r=R), fill[0:R]).then_inc(fill_st, 16)
            sp.wait_ge(zero_st, 32)
            sp.wait_ge(fill_st, 16)

        @block.scalar
        def _(act):
            act.wait_ge(ch_s, 2)
            act.activation(ex[:], ex[:], ACT.Exp).then_inc(exp_s, 1)

        @block.tensor
        def _(pe):
            pe.wait_ge(made, MADE)
            pe.wait_ge(gate_s, 1)
            for t in range(TH):
                mm = pe.transpose(psG[:, t * P:(t + 1) * P], copies[:, t, :], ident[:])
            mm.then_inc(gt_mm, 1)
            for rd in range(ROUNDS):
                pe.wait_ge(cn_s, rd + 1)
                pe.matmul(psD[:], pairs[:], cnt1[:], start=True, stop=True).then_inc(pr_mm, 1)
                pe.wait_ge(kp_s, rd + 1)
                pe.matmul(psC[:, 0:1], groups[:], keep1[:], start=True, stop=True).then_inc(gr_mm, 1)
            pe.wait_ge(th_s, 1)
            pe.matmul(psC[:], ones[:], parts[:].rearrange("p a e -> p (a e)"), start=True, stop=True).then_inc(th_mm, 1)
            pe.wait_ge(cnt_s, 1)
            pe.matmul(psC[:, 0:NE], ones[:], cnt[:], start=True, stop=True).then_inc(sum_s, 1)
            for j, src in enumerate((tie, sel)):
                pe.wait_ge(pre_s, j + 1)
                pe.matmul(psA[:].rearrange("p e t -> p (e t)"), below[:], src[:].rearrange("p e t -> p (e t)"), start=True, stop=True)
                pe.matmul(psB[:].rearrange("p e t -> p (e t)"), ones[:], src[:].rearrange("p e t -> p (e t)"),
                          start=True, stop=True).then_inc(mm_s, 1)

        @block.vector
        def _(dve):
            n = [0]

            def did(ins):
                ins.then_inc(ch_s, 1)
                n[0] += 1
                dve.wait_ge(ch_s, n[0])

            def over_e(ap):
                return ap.rearrange("p (t o) -> p t o", o=1).broadcast_to(te)

            def over_t(ap):
                return ap.rearrange("p (e o) -> p e o", o=1).broadcast_to([P, NE, T])

            lgv = lg[:].rearrange("p (t e) -> p t e", e=NE)
            dve.memset(one_w[:], 1.0)
            dve.wait_ge(made, 8)
            dve.tensor_copy(fill[:, :, 0].bitcast(I32), fill_id[:]).then_inc(made_v, 1)
            did(dve.tensor_reduce(m[:], lgv, AX.X, ALU.max))
            did(dve.tensor_tensor(ex[:], lgv, over_e(m[:]), ALU.subtract))
            did(dve.tensor_copy(iof[:], ione[:]))
            dve.wait_ge(exp_s, 1)
            did(dve.tensor_reduce(s[:], ex[:], AX.X, ALU.add))
            did(dve.reciprocal(r[:], s[:]))
            did(dve.tensor_tensor(pb[:], ex[:], over_e(r[:]), ALU.mult))

            def top(p, g, sl_):
                did(dve.tensor_reduce(g[:], p[:], AX.X, ALU.max))
                did(dve.tensor_tensor(eq[:], p[:], over_e(g[:]), ALU.is_equal))
                io = iof[:].rearrange("p (o e) -> p o e", o=1).broadcast_to(te)
                did(dve.scalar_tensor_tensor(out=tmp[:], in0=eq[:], scalar=-float(NE), in1=io, op0=ALU.mult, op1=ALU.add))
                did(dve.tensor_reduce(i1[:], tmp[:], AX.X, ALU.min))
                did(dve.tensor_tensor(sl_[:], tmp[:], over_e(i1[:]), ALU.is_equal))

            top(pb, g1, sel1)
            did(dve.scalar_tensor_tensor(out=p2[:], in0=sel1[:], scalar=-2.0, in1=pb[:], op0=ALU.mult, op1=ALU.add))
            top(p2, g2, sel2)
            did(dve.tensor_tensor(tmp[:], sel1[:], sel2[:], ALU.add))
            did(dve.tensor_tensor(gate[:].rearrange("p e t -> p t e"), pb[:], tmp[:], ALU.mult))
            for h in range(NH):
                src = gate[:, :, h * TH:(h + 1) * TH].rearrange("p e (t o) -> p t e o", o=1)
                ins = dve.tensor_copy(copies[:].rearrange("p t (e c h) -> p t e c h", e=NE, h=NH)[:, :, :, :, h],
                                      src.broadcast_to([P, TH, NE, NC]))
            did(ins)
            dve.sem_inc(gate_s, 1)
            did(dve.memset(th1[:], 0))
            did(dve.tensor_scalar(cnd[:], chan[:], NH.bit_length() - 1, NC - 1, ALU.logical_shift_right, ALU.bitwise_and))
            dve.wait_ge(gt_mm, 1)
            for rd in range(ROUNDS):
                low = DIG * (ROUNDS - 1 - rd)
                did(dve.tensor_scalar(cand1[:], cnd[:], low, None, ALU.logical_shift_left))
                did(dve.tensor_tensor(cand1[:], cand1[:], th1[:], ALU.bitwise_or))
                did(dve.tensor_scalar(reach[:], psG[:], cand1[:].bitcast(F32), None, ALU.is_ge, ALU.add, accum_out=cnt1[:]))
                dve.sem_inc(cn_s, 1)
                dve.wait_ge(pr_mm, rd + 1)
                did(dve.tensor_scalar(keep1[:], psD[:], float(cap), None, ALU.is_ge))
                dve.sem_inc(kp_s, 1)
                dve.wait_ge(gr_mm, rd + 1)
                did(dve.tensor_scalar(dig[:], psC[:, 0:1], 1.0 / NH, -1.0, ALU.mult, ALU.add))
                did(dve.tensor_scalar(dig[:], dig[:], low, None, ALU.logical_shift_left))
                did(dve.tensor_tensor(th1[:], th1[:], dig[:], ALU.bitwise_or))
            for i, (op, by) in enumerate(((ALU.logical_shift_right, 16), (ALU.bitwise_and, 0xffff))):
                did(dve.tensor_scalar(part_i[:], th1[:], by, None, op))
                did(dve.tensor_copy(part_f[:], part_i[:]))
                did(dve.tensor_scalar(parts[:, i, :], first_of[:], part_f[:, 0:1], None, ALU.mult))
            dve.sem_inc(th_s, 1)
            dve.wait_ge(th_mm, 1)
            did(dve.tensor_copy(hi_i[:], psC[:, 0:NE]))
            did(dve.tensor_copy(lo_i[:], psC[:, NE:]))
            did(dve.tensor_scalar(hi_i[:], hi_i[:], 16, None, ALU.logical_shift_left))
            did(dve.tensor_tensor(thr[:], hi_i[:], lo_i[:], ALU.bitwise_or))
            th = over_t(thr[:].bitcast(F32))
            did(dve.tensor_tensor(gt[:], gate[:], th, ALU.is_gt))
            dve.tensor_reduce(cnt[:], gt[:], AX.X, ALU.add).then_inc(cnt_s, 1)
            did(dve.tensor_tensor(tie[:], gate[:], th, ALU.is_equal))
            did(dve.tensor_scalar(ge[:], gate[:], 0.0, None, ALU.is_gt))
            did(dve.tensor_tensor(tie[:], tie[:], ge[:], ALU.mult))
            dve.sem_inc(pre_s, 1)
            dve.wait_ge(sum_s, 1)
            did(dve.tensor_scalar(need[:], psC[:, 0:NE], -1.0, float(cap), ALU.mult, ALU.add))

            def place(j):
                dve.wait_ge(mm_s, j + 1)
                did(dve.tensor_copy(cum[:], psB[:]))
                did(dve.tensor_tensor_scan(pos[:].rearrange("p e t -> p (e t)"), one_w[:], cum[:].rearrange("p e t -> p (e t)"),
                                           0.0, ALU.mult, ALU.add))
                did(dve.tensor_tensor(cum[:], pos[:], cum[:], ALU.subtract))
                did(dve.tensor_copy(base[:], cum[:, :, 0]))
                did(dve.tensor_tensor(cum[:], cum[:], over_t(base[:]), ALU.subtract))
                did(dve.tensor_tensor(pos[:], cum[:], psA[:], ALU.add))

            place(0)
            did(dve.tensor_tensor(ge[:], pos[:], over_t(need[:]), ALU.is_lt))
            did(dve.tensor_tensor(tie[:], tie[:], ge[:], ALU.mult))
            did(dve.tensor_tensor(sel[:], gt[:], tie[:], ALU.add))
            dve.sem_inc(pre_s, 1)
            place(1)
            did(dve.tensor_scalar(base[:], iof[:], float(cap), -BIG, ALU.mult, ALU.add))
            did(dve.tensor_tensor(pos[:], pos[:], over_t(base[:]), ALU.add))
            did(dve.tensor_tensor(slot[:], pos[:], sel[:], ALU.mult))
            slot_te = slot[:].rearrange("p e t -> p t e")
            for kk, (sl_, g) in enumerate(((sel1, g1), (sel2, g2))):
                did(dve.tensor_tensor(tmp[:], sl_[:], slot_te, ALU.mult))
                did(dve.tensor_reduce(sl[:, kk, :], tmp[:], AX.X, ALU.add))
                did(dve.tensor_scalar(idx[:, :, kk], sl[:, kk, :], BIG, None, ALU.add))
                did(dve.tensor_copy(pay[:, :, kk, 0].bitcast(I32), tok[:]))
                did(dve.tensor_copy(pay[:, :, kk, 1], g[:]))


def ffn_phase(nc, xn3_d, y, list_d, idx, pay, W1, b1, W2, b2, out, n_tok):
    NE, _, H = W1.shape
    cap = -(-int(CAPACITY * 10) * n_tok // (10 * NE))
    R = next(r for r in range(P, 0, -1) if cap % r == 0)
    NT = cap // R
    HALF = (cap + 1) // 2 + (cap + 1) // 2 % 2
    CW = 2 * HALF
    MH = H // P
    CH = 4
    MC = MH // CH
    assert cap % R == 0 and CW >= cap and HALF <= 512
    with ExitStack() as ctx:
        def sb(name, shape, dt=F32):
            return ctx.enter_context(nc.sbuf_tensor("d_" + name, shape, dt))

        def sem(name):
            return ctx.enter_context(nc.semaphore("d_" + name))

        ident = sb("ident", [P, P])
        lst = sb("lst", [R, NE * NT, 2])
        ids = [sb(f"ids{i}", [R, NT], I32) for i in range(2)]
        gts = [sb(f"gts{i}", [R, NT]) for i in range(2)]
        xg = sb("xg", [R, NT, D])
        xgT_h, xgT_l = ([sb(f"xgT_{a}{i}", [P, KD, CW], F32R) for i in range(2)] for a in "hl")
        w1, w2 = ([sb(f"w{a}_{i}", [P, MC, P * MC]) for i in range(2)] for a in (1, 2))
        w1_h, w1_l, w2_h, w2_l = ([sb(f"{a}{i}", [P, MC, P * MC], F32R) for i in range(2)] for a in ("w1_h", "w1_l", "w2_h", "w2_l"))
        hf = sb("hf", [P, 2, CW])
        h_h, h_l = sb("h_h", [P, 2, CW], F32R), sb("h_l", [P, 2, CW], F32R)
        b1c = [sb(f"b1c{i}", [P, MH]) for i in range(2)]
        b2r = [sb(f"b2r{i}", [R, D]) for i in range(2)]
        ob = sb("ob", [R, NT, D])
        psH = [ctx.enter_context(nc.psum_tensor(f"d_psH{i}", [P, 512], F32)) for i in range(2)]
        psO = [ctx.enter_context(nc.psum_tensor(f"d_psO{i}", [P, 512], F32)) for i in range(NT)]
        psT = ctx.enter_context(nc.psum_tensor("d_psT", [P, KD, P], F32))

        listed = sem("listed")
        setup, lst_ld, ids_s = sem("setup"), sem("lst_ld"), sem("ids")
        b_ld, w1_ld, w2_ld = ([sem(f"{a}_ld{i}") for i in range(2)] for a in ("b", "w1", "w2"))
        g_ld = [sem(f"g_ld{t}") for t in range(NT)]
        g_tp, g_hi, g_lo = sem("g_tp"), sem("g_hi"), sem("g_lo")
        w1_hi, w1_lo, w2_hi, w2_lo = sem("w1_hi"), sem("w1_lo"), sem("w2_hi"), sem("w2_lo")
        h_mm, silu_s, h_hi, h_lo, o_mm = sem("h_mm"), sem("silu"), sem("h_hi"), sem("h_lo"), sem("o_mm")
        ob_s, og_s, sc, out_st = sem("ob"), sem("og"), sem("sc"), sem("out_st")
        passed_p, passed_s = sem("passed_p"), sem("passed_s")

        w1_v = W1.rearrange("e (k p) h -> e p k h", p=P)
        w2_v = W2.rearrange("e (m p) d -> e p m d", p=P)
        b1_v = b1.rearrange("e (m p) -> e p m", p=P)

        def run(body, eng):
            body(0, 0, 0)
            with eng.Fori(0, NE // 2 - 1) as i:
                body(i * 2 + 1, i, 1)
                body(i * 2 + 2, i + 1, 0)
            body(NE - 1, NE // 2 - 1, 1)

        def last(e):
            return isinstance(e, int) and e == NE - 1

        def first(e):
            return isinstance(e, int) and e == 0

        def turned(e, t):
            return (psO[t][:].rearrange("p (k r) -> p k r", k=KD) if first(e) else psT[:])[:, :, 0:R]

        block = ctx.enter_context(nc.Block())

        @block.sync
        def _(sp):
            def biases(e, par):
                with nc.allow_non_contiguous_dma(reason="small parameters"):
                    sp.dma_start(b1c[par][:], b1_v[e]).then_inc(b_ld[par], 16)
                sp.dma_start(b2r[par][:], b2[bass.ds(e, 1), :].broadcast_to([R, D])).then_inc(b_ld[par], 16)

            biases(0, 0)

            def body(e, k, par):
                for c in range(CH):
                    if c == CH - 1 and not last(e):
                        wait(sp, silu_s, 2 * MH * e)
                        sp.sem_inc(passed_s, 1)
                        wait(sp, ob_s, NT * e)
                        sp.sem_inc(passed_s, 1)
                        biases(e + 1, 1 - par)
                    if first(e) and c == 2:
                        sp.wait_ge(listed, 16 * 2 * (n_tok // P))
                        with nc.allow_non_contiguous_dma(reason="the lists' rows"):
                            sp.dma_start(lst[:], list_d.rearrange("(g r) c -> r g c", r=R)).then_inc(lst_ld, 16)
                    s_ = c % 2
                    cols = slice(c * MC * P, (c + 1) * MC * P)
                    wait(sp, w1_hi, CH * e + c - 1)
                    wait(sp, w1_lo, CH * e + c - 1)
                    sp.sem_inc(passed_s, 1)
                    sp.dma_start(w1[s_][:], w1_v[e, :, :, cols]).then_inc(w1_ld[s_], 16)
                    wait(sp, w2_hi, CH * e + c - 1)
                    wait(sp, w2_lo, CH * e + c - 1)
                    sp.sem_inc(passed_s, 1)
                    sp.dma_start(w2[s_][:], w2_v[e, :, c * MC:(c + 1) * MC, :]).then_inc(w2_ld[s_], 16)

            run(body, sp)
            sp.wait_ge(sc, 16 * NT * NE)
            sp.sem_inc(passed_s, 1)
            sp.dma_start(out.rearrange("b s d -> (b s) d"), y[0:n_tok, :]).then_inc(out_st, 16)
            sp.wait_ge(out_st, 16)

        @block.gpsimd
        def _(pool):
            g = nc.gpsimd
            g.memset(ident[:], 0.0).then_inc(setup, 1)
            for i in range(2):
                g.memset(f32(xgT_h[i][:, :, cap:CW]), 0.0).then_inc(setup, 1)
                g.memset(f32(xgT_l[i][:, :, cap:CW]), 0.0).then_inc(setup, 1)
            pool.wait_ge(setup, 5)
            g.affine_select(out=ident[:], in_=ident[:], compare_op=ALU.not_equal, fill=1.0, base=0,
                            pattern=[[-1, P]], channel_multiplier=1).then_inc(setup, 1)

            def gather(e, par):
                pool.wait_ge(ids_s, 2 * e + 2)
                wait(pool, g_tp, NT * e)
                g.sem_inc(passed_p, 1)
                for t in range(NT):
                    g.indirect_dma_start(out=xg[:, t, :], out_offset=None, in_=xn3_d,
                                         in_offset=bass.IndirectOffsetOnAxis(ap=ids[par][:, t:t + 1], axis=0),
                                         bounds_check=n_tok + P - 1, oob_is_err=True).then_inc(g_ld[t], 16)

            for t in range(n_tok // P):
                for kk in range(2):
                    g.indirect_dma_start(out=list_d, out_offset=bass.IndirectOffsetOnAxis(ap=idx[:, t, kk:kk + 1], axis=0),
                                         in_=pay[:, t, kk, :], in_offset=None, bounds_check=NE * cap - 1,
                                         oob_is_err=False).then_inc(listed, 16)
            pool.wait_ge(listed, 16 * 2 * (n_tok // P))
            gather(0, 0)

            def body(e, k, par):
                if not last(e):
                    gather(e + 1, 1 - par)
                wait(pool, sc, 16 * NT * e)
                g.sem_inc(passed_p, 1)
                for t in range(NT):
                    pool.wait_ge(og_s, NT * e + t + 1)
                    g.sem_inc(passed_p, 1)
                    g.indirect_dma_start(out=y, out_offset=bass.IndirectOffsetOnAxis(ap=ids[par][:, t:t + 1], axis=0),
                                         in_=ob[:, t, :], in_offset=None, bounds_check=n_tok + P - 1, oob_is_err=True,
                                         compute_op=ALU.add).then_inc(sc, 16)

            run(body, pool)

        @block.tensor
        def _(pe):
            def split_mm(out, hi_w, lo_w, hi_x, lo_x, first, last_):
                pe.matmul(out, lo_w, hi_x, start=first, stop=False)
                pe.matmul(out, hi_w, lo_x, start=False, stop=False)
                return pe.matmul(out, hi_w, hi_x, start=False, stop=last_)

            def turn(e, t):
                pe.wait_ge(g_ld[t], 16 * (e + 1))
                if not first(e):
                    pe.wait_ge(g_lo, NT * e + t)
                for kk in range(KD):
                    mm = pe.transpose(turned(e, t)[:, kk, :], xg[:, t, kk * P:(kk + 1) * P], ident[0:R, 0:R])
                mm.then_inc(g_tp, 1)

            pe.wait_ge(setup, 6)
            for t in range(NT):
                turn(0, t)

            def body(e, k, par):
                pe.wait_ge(g_lo, NT * (e + 1))

                def outer(m):
                    c, s_ = m // MC, (m // MC) % 2
                    pe.wait_ge(h_lo, MH * e + m + 1)
                    pe.wait_ge(w2_lo, CH * e + c + 1)
                    for t in range(NT):
                        if m == 0:
                            wait(pe, ob_s, NT * (e - 1) + t + 1)
                        cc = slice(t * R, (t + 1) * R)
                        mm = split_mm(psO[t][0:R, :], h_h[:, m % 2, cc], h_l[:, m % 2, cc], w2_h[s_][:, m % MC, :],
                                      w2_l[s_][:, m % MC, :], m == 0, m == MH - 1)
                        if m == MH - 1:
                            mm.then_inc(o_mm, 1)
                    if m < MH - 1 :
                        mm.then_inc(o_mm, 1)

                for m in range(MH):
                    c, s_ = m // MC, (m // MC) % 2
                    pe.wait_ge(w1_lo, CH * e + c + 1)
                    for n in range(2):
                        wait(pe, silu_s, 2 * (MH * e + m - 1) + n + 1)
                        for kk in range(KD):
                            cc = slice((m % MC) * P, (m % MC + 1) * P)
                            mm = split_mm(psH[n][:, 0:HALF], w1_h[s_][:, kk, cc], w1_l[s_][:, kk, cc],
                                          xgT_h[par][:, kk, n * HALF:(n + 1) * HALF], xgT_l[par][:, kk, n * HALF:(n + 1) * HALF],
                                          kk == 0, kk == KD - 1)
                        mm.then_inc(h_mm, 1)
                    if m:
                        outer(m - 1)
                    if m >= 5 and (m - 5) % 2 == 0 and (m - 5) // 2 < NT and not last(e):
                        turn(e + 1, (m - 5) // 2)
                outer(MH - 1)

            run(body, pe)

        OM = MH - 1 + NT

        @block.scalar
        def _(act):
            def copy(out, in_, done):
                act.activation(out, in_, ACT.Copy).then_inc(done, 1)

            def rows_hi(e, par, t):
                act.wait_ge(g_tp, NT * e + t + 1)
                copy(xgT_h[par][:, :, t * R:(t + 1) * R], turned(e, t), g_hi)

            def w_parts(e, k, c):
                s_ = c % 2
                act.wait_ge(w1_ld[s_], 32 * e + 16 * (c // 2) + 16)
                wait(act, h_mm, 2 * (MH * e + MC * (c - 1)))
                copy(w1_h[s_][:], w1[s_][:], w1_hi)
                act.wait_ge(w2_ld[s_], 32 * e + 16 * (c // 2) + 16)
                if c >= 2:
                    act.wait_ge(o_mm, OM * e + MC * (c - 1))
                elif c == 1:
                    wait(act, o_mm, OM * e)
                else:
                    wait(act, o_mm, OM * (e - 1) + MC * (CH - 1))
                copy(w2_h[s_][:], w2[s_][:], w2_hi)

            w_parts(0, 0, 0)
            for t in range(NT):
                rows_hi(0, 0, t)

            def body(e, k, par):
                act.wait_ge(b_ld[par], 32 * k + 32)
                for m in range(MH):
                    for n in range(2):
                        act.wait_ge(h_mm, 2 * (MH * e + m) + n + 1)
                        wait(act, h_lo, MH * e + m - 1)
                        act.activation(hf[:, m % 2, n * HALF:(n + 1) * HALF], psH[n][:, 0:HALF], ACT.Silu,
                                       bias=b1c[par][:, m:m + 1]).then_inc(silu_s, 1)
                    act.wait_ge(silu_s, 2 * (MH * e + m + 1))
                    if m >= 2:
                        act.wait_ge(o_mm, OM * e + m - 1)
                    else:
                        wait(act, o_mm, OM * e)
                    copy(h_h[:, m % 2, :], hf[:, m % 2, :], h_hi)
                    if m >= 5 and (m - 5) % 2 == 0 and (m - 5) // 2 < NT and not last(e):
                        rows_hi(e + 1, 1 - par, (m - 5) // 2)
                    if m % MC == 1 and m // MC + 1 < CH:
                        w_parts(e, k, m // MC + 1)
                    if m == MH - 2 and not last(e):
                        w_parts(e + 1, k, 0)
                for t in range(NT):
                    act.wait_ge(ob_s, NT * e + t + 1)
                    act.activation(ob[:, t, :], ob[:, t, :], ACT.Copy, scale=gts[par][:, t:t + 1]).then_inc(og_s, 1)

            run(body, act)

        @block.vector
        def _(dve):
            def minus(out, a, b_, done):
                dve.tensor_tensor(out, a, b_, ALU.subtract).then_inc(done, 1)

            def rows_lo(e, par, t):
                dve.wait_ge(g_hi, NT * e + t + 1)
                c = slice(t * R, (t + 1) * R)
                minus(xgT_l[par][:, :, c], turned(e, t), f32(xgT_h[par][:, :, c]), g_lo)

            def w_parts(e, c):
                s_ = c % 2
                dve.wait_ge(w1_hi, CH * e + c + 1)
                minus(w1_l[s_][:], w1[s_][:], f32(w1_h[s_][:]), w1_lo)
                dve.wait_ge(w2_hi, CH * e + c + 1)
                minus(w2_l[s_][:], w2[s_][:], f32(w2_h[s_][:]), w2_lo)

            def lists(e, par):
                wait(dve, sc, 16 * NT * (e - 1))
                wait(dve, og_s, NT * (e - 1))
                at = bass.ds(e * NT, NT)
                dve.tensor_copy(ids[par][:], lst[:, at, 0].bitcast(I32)).then_inc(ids_s, 1)
                dve.tensor_copy(gts[par][:], lst[:, at, 1]).then_inc(ids_s, 1)

            w_parts(0, 0)
            dve.wait_ge(lst_ld, 16)
            lists(0, 0)
            for t in range(NT):
                rows_lo(0, 0, t)

            def body(e, k, par):
                for m in range(MH):
                    if m == 3 and not last(e):
                        lists(e + 1, 1 - par)
                    dve.wait_ge(h_hi, MH * e + m + 1)
                    minus(h_l[:, m % 2, :], hf[:, m % 2, :], f32(h_h[:, m % 2, :]), h_lo)
                    if m >= 5 and (m - 5) % 2 == 0 and (m - 5) // 2 < NT and not last(e):
                        rows_lo(e + 1, 1 - par, (m - 5) // 2)
                    if m % MC == 1 and m // MC + 1 < CH:
                        w_parts(e, m // MC + 1)
                    if m == MH - 2 and not last(e):
                        w_parts(e + 1, 0)
                for t in range(NT):
                    dve.wait_ge(o_mm, OM * e + MH - 1 + t + 1)
                    wait(dve, sc, 16 * NT * e)
                    dve.tensor_tensor(ob[:, t, :], psO[t][0:R, :], b2r[par][:], ALU.add).then_inc(ob_s, 1)

            run(body, dve)


def block_kernel(nc, x, ctxT, W_inT, conv_w, conv_b, W_xprojT, A_log, D_param, W_outT,
                 WqT, bq, WkT, bk, WvT, bv, WoT, bo, Wr, br, W1, b1, W2, b2, out):
    B, S, _ = x.shape
    n_tok = B * S
    NE = Wr.shape[1]
    cap = -(-int(CAPACITY * 10) * n_tok // (10 * NE))

    def scratch(name, shape, dt=F32):
        return nc.dram_tensor(name, shape, dt, kind="Internal").ap()

    x1 = scratch("x1_d", (B, S, D))
    rows = scratch("rows_d", (3, B, S))
    qs, ks = scratch("qs_d", (2, D, S), F32R), scratch("ks_d", (2, D, S), F32R)
    y, xn3 = scratch("y_d", (n_tok + P, D)), scratch("xn3_d", (n_tok + P, D))
    lists = scratch("lists_d", (NE * cap, 2))
    mamba_phase(nc, x, W_inT, conv_w, conv_b, W_xprojT, A_log, D_param, W_outT, x1, rows)
    with nc.sbuf_tensor("idx", [P, n_tok // P, 2], I32) as idx, nc.sbuf_tensor("pay", [P, n_tok // P, 2, 2], F32) as pay:
        with nc.sbuf_tensor("lg", [P, n_tok // P * NE], F32) as lg:
            attention_phase(nc, x1, ctxT, WqT, bq, WkT, bk, WvT, bv, WoT, bo, Wr, br, y, xn3, lg, qs, ks)
            routing_phase(nc, lg, lists, idx, pay, y, xn3, n_tok, NE)
        ffn_phase(nc, xn3, y, lists, idx, pay, W1, b1, W2, b2, out, n_tok)


def kernel(x, ctx_1024, L0_attn_W_in, L0_attn_conv_w, L0_attn_conv_b, L0_attn_W_xproj, L0_attn_A_log, L0_attn_D_param,
           L0_attn_W_out, L0_xattn_Wq, L0_xattn_bq, L0_xattn_Wk, L0_xattn_bk, L0_xattn_Wv, L0_xattn_bv, L0_xattn_Wo,
           L0_xattn_bo, L0_ffn_Wr, L0_ffn_br, L0_ffn_W1, L0_ffn_b1, L0_ffn_W2, L0_ffn_b2):
    import numpy as _np
    import concourse.bacc as _bacc
    from concourse import mybir as _mybir
    from concourse.bass_utils import run_bass_kernel_spmd as _run

    ins = dict(x=x, ctxT=ctx_1024.transpose(0, 2, 1), W_inT=L0_attn_W_in.T, conv_w=L0_attn_conv_w, conv_b=L0_attn_conv_b,
               W_xprojT=L0_attn_W_xproj.T, A_log=L0_attn_A_log, D_param=L0_attn_D_param, W_outT=L0_attn_W_out.T,
               WqT=L0_xattn_Wq.T, bq=L0_xattn_bq, WkT=L0_xattn_Wk.T, bk=L0_xattn_bk, WvT=L0_xattn_Wv.T, bv=L0_xattn_bv,
               WoT=L0_xattn_Wo.T, bo=L0_xattn_bo, Wr=L0_ffn_Wr, br=L0_ffn_br, W1=L0_ffn_W1, b1=L0_ffn_b1, W2=L0_ffn_W2,
               b2=L0_ffn_b2)
    nc = _bacc.Bacc("TRN2", target_bir_lowering=False, num_devices=1)
    arrays, args = {}, []
    for name, a in ins.items():
        a = _np.ascontiguousarray(a)
        arrays[f"in_{name}_dram"] = a
        args.append(nc.dram_tensor(f"in_{name}_dram", a.shape, _mybir.dt.from_np(a.dtype), kind="ExternalInput").ap())
    args.append(nc.dram_tensor("out_0_dram", x.shape, _mybir.dt.float32, kind="ExternalOutput").ap())
    block_kernel(nc, *args)
    r = _run(nc, [arrays], core_ids=[0])
    return r.results[0]["out_0_dram"]
```
